# Optimizing a Trainium2 kernel written in Bass

```python
import numpy as np
import jax
import jax.numpy as jnp

def _softmax(x, axis=-1):
    return jax.nn.softmax(x, axis=axis)

def _gelu(x):
    return jax.nn.gelu(x, approximate=True)

def _silu(x):
    return jax.nn.silu(x)

def _sigmoid(x):
    return jax.nn.sigmoid(x)

def _layernorm(x, axis=-1, eps=1e-05):
    m = jnp.mean(x, axis=axis, keepdims=True)
    v = jnp.var(x, axis=axis, keepdims=True)
    return (x - m) / jnp.sqrt(v + eps)

def _scatter_add(tgt, idx, src, axis=0):
    return tgt.at[idx].add(src)

def _segment_sum(src, seg, n):
    return jax.ops.segment_sum(src, seg, n)
kernel_name = 'mk_decoder_preln_d2_seqx_r8_7e9d53'

def setup_inputs(seed: int=0):
    np.random.seed(seed)
    _w = jnp.asarray

    def _rec_inputs():
        import jax
        import jax.numpy as jnp
        _rk = jax.random.key(seed)
        x = -0.0002928 + 1 * jax.random.normal(jax.random.fold_in(_rk, 1), (64, 64, 128), jnp.float32)
        _lenS = 64 - jax.random.randint(jax.random.fold_in(_rk, 7), (64,), 0, max(1, 64 // 4) + 1, jnp.int32)
        _lenS2 = 64 - jax.random.randint(jax.random.fold_in(_rk, 8), (64,), 0, max(1, 64 // 4) + 1, jnp.int32)
        _ctx_1024P = jax.random.normal(jax.random.fold_in(_rk, 11), (64, 16, 128), jnp.float32)
        _ctx_1024c = jax.random.dirichlet(jax.random.fold_in(_rk, 511), 0.3 * jnp.ones((16,), jnp.float32), (64, 64))
        _ctx_1024t = jnp.einsum('bsk,bkd->bsd', _ctx_1024c, _ctx_1024P)
        _ctx_1024t = _ctx_1024t * jax.lax.rsqrt(jnp.mean(jnp.square(_ctx_1024t)) + 1e-12) * 0.953939
        ctx_1024 = -1.39393e-06 + 0.999914 * (_ctx_1024t + 0.3 * jax.random.normal(jax.random.fold_in(_rk, 611), (64, 64, 128), jnp.float32))
        return (x, ctx_1024)
    x, ctx_1024 = _rec_inputs()

    def _L0_attn_setup():
        import math
        import jax, jax.numpy as jnp
        import numpy as np
        D_MODEL = 128
        D_STATE = 64
        BATCH = 8
        SEQLEN = 256

        def _reference_tuple_inner(x, log_Lam_real, Lam_imag, B_real, B_imag, C_real, C_imag, D, log_dt, W_out, b_out):
            B, L, H = x.shape
            N = log_Lam_real.shape[0]
            dt = jnp.exp(log_dt)
            Lam_r = -jnp.exp(log_Lam_real)
            mag = jnp.exp(Lam_r * dt)
            Lbar_r = mag * jnp.cos(Lam_imag * dt)
            Lbar_i = mag * jnp.sin(Lam_imag * dt)
            Bu_r = jnp.einsum('blh,nh->bln', x, dt * B_real)
            Bu_i = jnp.einsum('blh,nh->bln', x, dt * B_imag)

            def step(carry, bu):
                sr, si = carry
                bur, bui = bu
                nr = Lbar_r * sr - Lbar_i * si + bur
                ni = Lbar_r * si + Lbar_i * sr + bui
                return ((nr, ni), (nr, ni))
            sr0 = jnp.zeros((B, N), dtype=x.dtype)
            si0 = jnp.zeros((B, N), dtype=x.dtype)
            (sr, si), (SR, SI) = jax.lax.scan(step, (sr0, si0), (jnp.swapaxes(Bu_r, 0, 1), jnp.swapaxes(Bu_i, 0, 1)))
            y = jnp.einsum('lbn,hn->blh', SR, C_real) - jnp.einsum('lbn,hn->blh', SI, C_imag) + D * x
            out = y @ W_out.T + b_out
            return (out, (sr, si))
        key = jax.random.key(seed)
        ks = jax.random.split(key, 8)
        x = jax.random.normal(ks[0], (BATCH, SEQLEN, D_MODEL), dtype=jnp.float32)
        log_Lam_real = jnp.log(0.5 * jnp.ones((D_STATE,), dtype=jnp.float32))
        Lam_imag = math.pi * jnp.arange(D_STATE, dtype=jnp.float32)
        B_real = 0.02 * jax.random.normal(ks[1], (D_STATE, D_MODEL), dtype=jnp.float32)
        B_imag = 0.02 * jax.random.normal(ks[2], (D_STATE, D_MODEL), dtype=jnp.float32)
        C_real = 0.02 * jax.random.normal(ks[3], (D_MODEL, D_STATE), dtype=jnp.float32)
        C_imag = 0.02 * jax.random.normal(ks[4], (D_MODEL, D_STATE), dtype=jnp.float32)
        Dp = jnp.ones((D_MODEL,), dtype=jnp.float32)
        log_dt = jnp.zeros((1,), dtype=jnp.float32)
        W_out = 0.02 * jax.random.normal(ks[5], (D_MODEL, D_MODEL), dtype=jnp.float32)
        b_out = jnp.zeros((D_MODEL,), dtype=jnp.float32)
        return {'x': x, 'log_Lam_real': log_Lam_real, 'Lam_imag': Lam_imag, 'B_real': B_real, 'B_imag': B_imag, 'C_real': C_real, 'C_imag': C_imag, 'D': Dp, 'log_dt': log_dt, 'W_out': W_out, 'b_out': b_out}
    _L0_attn_all = _L0_attn_setup()
    _L0_attn_in = {k: v for k, v in _L0_attn_all.items() if k in ('log_Lam_real', 'Lam_imag', 'B_real', 'B_imag', 'C_real', 'C_imag', 'D', 'log_dt', 'W_out', 'b_out')}
    del _L0_attn_all

    def _L0_xattn_setup():
        import jax, jax.numpy as jnp
        import numpy as np
        NUM_HEADS = 16
        key = jax.random.key(seed)
        kq, kk, kv = jax.random.split(key, 3)
        b, s, h = (1, 512, 128)
        q = jax.random.normal(kq, (b, s, h), dtype=jnp.float32)
        k = jax.random.normal(kk, (b, s, h), dtype=jnp.float32)
        v = jax.random.normal(kv, (b, s, h), dtype=jnp.float32)
        return {'q': q, 'k': k, 'v': v}
    _L0_xattn_all = _L0_xattn_setup()
    _L0_xattn_in = {k: v for k, v in _L0_xattn_all.items() if k in ()}
    del _L0_xattn_all

    def _L0_ffn_setup():
        import jax, jax.numpy as jnp
        import numpy as np
        D = 128
        F = 4 * D
        E = 8
        NS = 2
        TOP_K = 2
        B, S = (2, 128)
        key = jax.random.key(seed)
        ks = jax.random.split(key, 7)
        w = 1.0 / np.sqrt(D)
        wf = 1.0 / np.sqrt(F)
        return {'x': jax.random.normal(ks[0], (B, S, D), jnp.float32), 'centroids': jax.random.normal(ks[1], (E, D), jnp.float32) * w, 'routing_bias': jnp.zeros((E,), jnp.float32), 'Wfc_r': jax.random.normal(ks[2], (E, F, D), jnp.float32) * w, 'Wproj_r': jax.random.normal(ks[3], (E, D, F), jnp.float32) * wf, 'Wfc_sh': jax.random.normal(ks[4], (NS, F, D), jnp.float32) * w, 'Wproj_sh': jax.random.normal(ks[5], (NS, D, F), jnp.float32) * wf}
    _L0_ffn_all = _L0_ffn_setup()
    _L0_ffn_in = {k: v for k, v in _L0_ffn_all.items() if k in ('centroids', 'routing_bias', 'Wfc_r', 'Wproj_r', 'Wfc_sh', 'Wproj_sh')}
    del _L0_ffn_all

    def _L1_attn_setup():
        import jax, jax.numpy as jnp
        import numpy as np
        B, T, HID = (4, 256, 128)
        H, D, V = (8, 64, 128)
        EPS = 1e-05

        def _rotary(x, T, D):
            inv_freq = 1.0 / 10000.0 ** (jnp.arange(0, D, 2, dtype=jnp.float32) / D)
            t = jnp.arange(T, dtype=jnp.float32)
            freqs = t[:, None] * inv_freq[None, :]
            emb = jnp.concatenate([freqs, freqs], axis=-1)
            cos = jnp.cos(emb)[None, None, :, :]
            sin = jnp.sin(emb)[None, None, :, :]
            x1, x2 = jnp.split(x, 2, axis=-1)
            rot = jnp.concatenate([-x2, x1], axis=-1)
            return x * cos + rot * sin
        key = jax.random.key(seed)
        ks = jax.random.split(key, 7)
        sc = 0.02
        return {'x': jax.random.normal(ks[0], (B, T, HID), dtype=jnp.float32), 'Wq': jax.random.normal(ks[1], (H * D, HID), dtype=jnp.float32) * sc, 'Wk': jax.random.normal(ks[2], (H * D, HID), dtype=jnp.float32) * sc, 'Wv': jax.random.normal(ks[3], (H * V, HID), dtype=jnp.float32) * sc, 'Wg': jax.random.normal(ks[4], (H * V, HID), dtype=jnp.float32) * sc, 'Wo': jax.random.normal(ks[5], (HID, H * V), dtype=jnp.float32) * sc, 'gn_weight': jnp.ones((H * V,), dtype=jnp.float32), 'gn_bias': jnp.zeros((H * V,), dtype=jnp.float32)}
    _L1_attn_all = _L1_attn_setup()
    _L1_attn_in = {k: v for k, v in _L1_attn_all.items() if k in ('Wq', 'Wk', 'Wv', 'Wg', 'Wo', 'gn_weight', 'gn_bias')}
    del _L1_attn_all

    def _L1_xattn_setup():
        import jax, jax.numpy as jnp
        import numpy as np
        D_MODEL = 128
        NUM_HEADS = 16
        D_HEAD = D_MODEL // NUM_HEADS
        key = jax.random.key(seed)
        ks = jax.random.split(key, 9)
        B, L, E = (2, 256, D_MODEL)
        bound = 1.0 / np.sqrt(E)
        inp = {'query': jax.random.normal(ks[0], (B, L, E), dtype=jnp.float32), 'key': jax.random.normal(ks[1], (B, L, E), dtype=jnp.float32), 'value': jax.random.normal(ks[2], (B, L, E), dtype=jnp.float32), 'wq': jax.random.uniform(ks[3], (E, E), jnp.float32, -bound, bound), 'bq': jax.random.uniform(ks[4], (E,), jnp.float32, -bound, bound), 'wk': jax.random.uniform(ks[5], (E, E), jnp.float32, -bound, bound), 'bk': jax.random.uniform(ks[6], (E,), jnp.float32, -bound, bound), 'wv': jax.random.uniform(ks[7], (E, E), jnp.float32, -bound, bound), 'bv': jax.random.uniform(ks[8], (E,), jnp.float32, -bound, bound)}
        return inp
    _L1_xattn_all = _L1_xattn_setup()
    _L1_xattn_in = {k: v for k, v in _L1_xattn_all.items() if k in ('wq', 'bq', 'wk', 'bk', 'wv', 'bv')}
    del _L1_xattn_all

    def _L1_ffn_setup():
        import jax, jax.numpy as jnp
        import numpy as np
        N_EMBED = 128
        FFN_HIDDEN = 512
        NUM_EXPERTS = 8
        TOP_K = 2
        key = jax.random.key(seed)
        ks = jax.random.split(key, 8)
        d, f, E = (N_EMBED, FFN_HIDDEN, NUM_EXPERTS)
        s_d = 1.0 / np.sqrt(d)
        s_f = 1.0 / np.sqrt(f)
        return {'x': jax.random.normal(ks[0], (2, 256, d), dtype=jnp.float32), 'Wg': jax.random.uniform(ks[1], (d, E), jnp.float32, -s_d, s_d), 'bg': jax.random.uniform(ks[2], (E,), jnp.float32, -s_d, s_d), 'W1': jax.random.uniform(ks[3], (E, d, f), jnp.float32, -s_d, s_d), 'b1': jax.random.uniform(ks[4], (E, f), jnp.float32, -s_d, s_d), 'W2': jax.random.uniform(ks[5], (E, f, d), jnp.float32, -s_f, s_f), 'b2': jax.random.uniform(ks[6], (E, d), jnp.float32, -s_f, s_f)}
    _L1_ffn_all = _L1_ffn_setup()
    _L1_ffn_in = {k: v for k, v in _L1_ffn_all.items() if k in ('Wg', 'bg', 'W1', 'b1', 'W2', 'b2')}
    del _L1_ffn_all
    return {'x': x, 'ctx_1024': ctx_1024, 'L0_attn_log_Lam_real': _L0_attn_in['log_Lam_real'], 'L0_attn_Lam_imag': _L0_attn_in['Lam_imag'], 'L0_attn_B_real': _L0_attn_in['B_real'], 'L0_attn_B_imag': _L0_attn_in['B_imag'], 'L0_attn_C_real': _L0_attn_in['C_real'], 'L0_attn_C_imag': _L0_attn_in['C_imag'], 'L0_attn_D': _L0_attn_in['D'], 'L0_attn_log_dt': _L0_attn_in['log_dt'], 'L0_attn_W_out': _L0_attn_in['W_out'], 'L0_attn_b_out': _L0_attn_in['b_out'], 'L0_ffn_centroids': _L0_ffn_in['centroids'], 'L0_ffn_routing_bias': _L0_ffn_in['routing_bias'], 'L0_ffn_Wfc_r': _L0_ffn_in['Wfc_r'], 'L0_ffn_Wproj_r': _L0_ffn_in['Wproj_r'], 'L0_ffn_Wfc_sh': _L0_ffn_in['Wfc_sh'], 'L0_ffn_Wproj_sh': _L0_ffn_in['Wproj_sh'], 'L1_attn_Wq': _L1_attn_in['Wq'], 'L1_attn_Wk': _L1_attn_in['Wk'], 'L1_attn_Wv': _L1_attn_in['Wv'], 'L1_attn_Wg': _L1_attn_in['Wg'], 'L1_attn_Wo': _L1_attn_in['Wo'], 'L1_attn_gn_weight': _L1_attn_in['gn_weight'], 'L1_attn_gn_bias': _L1_attn_in['gn_bias'], 'L1_xattn_wq': _L1_xattn_in['wq'], 'L1_xattn_bq': _L1_xattn_in['bq'], 'L1_xattn_wk': _L1_xattn_in['wk'], 'L1_xattn_bk': _L1_xattn_in['bk'], 'L1_xattn_wv': _L1_xattn_in['wv'], 'L1_xattn_bv': _L1_xattn_in['bv'], 'L1_ffn_Wg': _L1_ffn_in['Wg'], 'L1_ffn_bg': _L1_ffn_in['bg'], 'L1_ffn_W1': _L1_ffn_in['W1'], 'L1_ffn_b1': _L1_ffn_in['b1'], 'L1_ffn_W2': _L1_ffn_in['W2'], 'L1_ffn_b2': _L1_ffn_in['b2']}

def reference(x, ctx_1024, L0_attn_log_Lam_real, L0_attn_Lam_imag, L0_attn_B_real, L0_attn_B_imag, L0_attn_C_real, L0_attn_C_imag, L0_attn_D, L0_attn_log_dt, L0_attn_W_out, L0_attn_b_out, L0_ffn_centroids, L0_ffn_routing_bias, L0_ffn_Wfc_r, L0_ffn_Wproj_r, L0_ffn_Wfc_sh, L0_ffn_Wproj_sh, L1_attn_Wq, L1_attn_Wk, L1_attn_Wv, L1_attn_Wg, L1_attn_Wo, L1_attn_gn_weight, L1_attn_gn_bias, L1_xattn_wq, L1_xattn_bq, L1_xattn_wk, L1_xattn_bk, L1_xattn_wv, L1_xattn_bv, L1_ffn_Wg, L1_ffn_bg, L1_ffn_W1, L1_ffn_b1, L1_ffn_W2, L1_ffn_b2):
    import jax
    import jax.numpy as jnp

    def _L0_attn_ref(x, log_Lam_real, Lam_imag, B_real, B_imag, C_real, C_imag, D, log_dt, W_out, b_out):
        import math
        import jax, jax.numpy as jnp
        import numpy as np
        D_MODEL = 128
        D_STATE = 64
        BATCH = 8
        SEQLEN = 256

        def _reference_tuple_inner(x, log_Lam_real, Lam_imag, B_real, B_imag, C_real, C_imag, D, log_dt, W_out, b_out):
            B, L, H = x.shape
            N = log_Lam_real.shape[0]
            dt = jnp.exp(log_dt)
            Lam_r = -jnp.exp(log_Lam_real)
            mag = jnp.exp(Lam_r * dt)
            Lbar_r = mag * jnp.cos(Lam_imag * dt)
            Lbar_i = mag * jnp.sin(Lam_imag * dt)
            Bu_r = jnp.einsum('blh,nh->bln', x, dt * B_real)
            Bu_i = jnp.einsum('blh,nh->bln', x, dt * B_imag)

            def step(carry, bu):
                sr, si = carry
                bur, bui = bu
                nr = Lbar_r * sr - Lbar_i * si + bur
                ni = Lbar_r * si + Lbar_i * sr + bui
                return ((nr, ni), (nr, ni))
            sr0 = jnp.zeros((B, N), dtype=x.dtype)
            si0 = jnp.zeros((B, N), dtype=x.dtype)
            (sr, si), (SR, SI) = jax.lax.scan(step, (sr0, si0), (jnp.swapaxes(Bu_r, 0, 1), jnp.swapaxes(Bu_i, 0, 1)))
            y = jnp.einsum('lbn,hn->blh', SR, C_real) - jnp.einsum('lbn,hn->blh', SI, C_imag) + D * x
            out = y @ W_out.T + b_out
            return (out, (sr, si))
        return _reference_tuple_inner(x, log_Lam_real, Lam_imag, B_real, B_imag, C_real, C_imag, D, log_dt, W_out, b_out)[0]

    def _L0_xattn_ref(q, k, v):
        import jax, jax.numpy as jnp
        import numpy as np
        NUM_HEADS = 16
        b, s, hd = q.shape
        n = NUM_HEADS
        d = hd // n
        qh = q.reshape(b, s, n, d)
        kh = k.reshape(b, s, n, d)
        vh = v.reshape(b, s, n, d)
        scale = 1.0 / jnp.sqrt(jnp.float32(d))
        scores = jnp.einsum('bqnd,bknd->bnqk', qh, kh) * scale
        probs = jax.nn.softmax(scores, axis=-1)
        out = jnp.einsum('bnqk,bknd->bqnd', probs, vh)
        return out.reshape(b, s, hd)

    def _L0_ffn_ref(x, centroids, routing_bias, Wfc_r, Wproj_r, Wfc_sh, Wproj_sh):
        import jax, jax.numpy as jnp
        import numpy as np
        D = 128
        F = 4 * D
        E = 8
        NS = 2
        TOP_K = 2
        B, S = (2, 128)
        raw = jnp.einsum('bsd,ed->bse', x, centroids)
        routing_scores = jax.nn.sigmoid(raw)
        balanced = jax.nn.sigmoid(raw + routing_bias)
        _, top_idx = jax.lax.top_k(balanced, TOP_K)
        gathered = jnp.take_along_axis(routing_scores, top_idx, axis=-1)
        top_w = jax.nn.softmax(gathered, axis=-1)
        combine = jnp.sum(jax.nn.one_hot(top_idx, E, dtype=x.dtype) * top_w[..., None], axis=-2)
        h_sh = jax.nn.gelu(jnp.einsum('bsd,nfd->bsnf', x, Wfc_sh), approximate=False)
        shared_out = jnp.einsum('bsnf,ndf->bsd', h_sh, Wproj_sh)
        h_r = jax.nn.gelu(jnp.einsum('bsd,efd->bsef', x, Wfc_r), approximate=False)
        expert_out = jnp.einsum('bsef,edf->bsed', h_r, Wproj_r)
        routed_out = jnp.einsum('bsed,bse->bsd', expert_out, combine)
        return x + shared_out + routed_out

    def _L1_attn_ref(x, Wq, Wk, Wv, Wg, Wo, gn_weight, gn_bias):
        import jax, jax.numpy as jnp
        import numpy as np
        B, T, HID = (4, 256, 128)
        H, D, V = (8, 64, 128)
        EPS = 1e-05

        def _rotary(x, T, D):
            inv_freq = 1.0 / 10000.0 ** (jnp.arange(0, D, 2, dtype=jnp.float32) / D)
            t = jnp.arange(T, dtype=jnp.float32)
            freqs = t[:, None] * inv_freq[None, :]
            emb = jnp.concatenate([freqs, freqs], axis=-1)
            cos = jnp.cos(emb)[None, None, :, :]
            sin = jnp.sin(emb)[None, None, :, :]
            x1, x2 = jnp.split(x, 2, axis=-1)
            rot = jnp.concatenate([-x2, x1], axis=-1)
            return x * cos + rot * sin
        Bx, Tx, _ = x.shape
        q = jnp.einsum('bti,oi->bto', x, Wq).reshape(Bx, Tx, H, D).transpose(0, 2, 1, 3)
        k = jnp.einsum('bti,oi->bto', x, Wk).reshape(Bx, Tx, H, D).transpose(0, 2, 1, 3)
        v = jnp.einsum('bti,oi->bto', x, Wv).reshape(Bx, Tx, H, V).transpose(0, 2, 1, 3)
        g = jnp.einsum('bti,oi->bto', x, Wg)
        q = _rotary(q, Tx, D)
        k = _rotary(k, Tx, D)
        gamma = 1.0 - jnp.exp2(-5.0 - jnp.arange(H, dtype=jnp.float32))
        s = jnp.log2(gamma)
        n = jnp.arange(Tx, dtype=jnp.float32)
        rel = n[:, None] - n[None, :]
        causal = rel >= 0
        decay = jnp.where(causal[None, :, :], jnp.exp2(rel[None, :, :] * s[:, None, None]), 0.0)
        scores = jnp.einsum('bhtd,bhsd->bhts', q, k) * D ** (-0.5)
        scores = scores * decay[None]
        o = jnp.einsum('bhts,bhsv->bhtv', scores, v)
        o = o.transpose(0, 2, 1, 3)
        mean = jnp.mean(o, axis=-1, keepdims=True)
        var = jnp.var(o, axis=-1, keepdims=True)
        o = (o - mean) * jax.lax.rsqrt(var + EPS)
        o = o * gn_weight.reshape(H, V) + gn_bias.reshape(H, V)
        o = o.reshape(Bx, Tx, H * V)
        o = o * jax.nn.silu(g)
        return jnp.einsum('btc,oc->bto', o, Wo)

    def _L1_xattn_ref(query, key, value, wq, bq, wk, bk, wv, bv):
        import jax, jax.numpy as jnp
        import numpy as np
        D_MODEL = 128
        NUM_HEADS = 16
        D_HEAD = D_MODEL // NUM_HEADS
        B, L, E = query.shape
        H, Dh = (NUM_HEADS, D_HEAD)
        scale = Dh ** 0.5
        q = (query @ wq.T + bq).reshape(B, L, H, Dh).transpose(0, 2, 1, 3)
        k = (key @ wk.T + bk).reshape(B, L, H, Dh).transpose(0, 2, 1, 3)
        v = (value @ wv.T + bv).reshape(B, L, H, Dh).transpose(0, 2, 1, 3)
        scores = jnp.einsum('bhld,bhsd->bhls', q, k) / scale
        attn = jax.nn.softmax(scores, axis=-1)
        out = jnp.einsum('bhls,bhsd->bhld', attn, v)
        return out.transpose(0, 2, 1, 3).reshape(B, L, E)

    def _L1_ffn_ref(x, Wg, bg, W1, b1, W2, b2):
        import jax, jax.numpy as jnp
        import numpy as np
        N_EMBED = 128
        FFN_HIDDEN = 512
        NUM_EXPERTS = 8
        TOP_K = 2
        gate_scores = jax.nn.softmax(x @ Wg + bg, axis=-1)
        topk_scores, topk_idx = jax.lax.top_k(gate_scores, TOP_K)
        topk_scores = topk_scores / (jnp.sum(topk_scores, axis=-1, keepdims=True) + 1e-08)
        onehot = jax.nn.one_hot(topk_idx, NUM_EXPERTS, dtype=x.dtype)
        combine_w = jnp.einsum('bsk,bske->bse', topk_scores, onehot)
        output = jnp.zeros_like(x)
        for e in range(NUM_EXPERTS):
            h = jax.nn.gelu(x @ W1[e] + b1[e])
            y = h @ W2[e] + b2[e]
            output = output + y * combine_w[..., e:e + 1]
        return output
    x = x + _L0_attn_ref(_layernorm(x, axis=-1), L0_attn_log_Lam_real, L0_attn_Lam_imag, L0_attn_B_real, L0_attn_B_imag, L0_attn_C_real, L0_attn_C_imag, L0_attn_D, L0_attn_log_dt, L0_attn_W_out, L0_attn_b_out)
    x = x + _L0_xattn_ref(_layernorm(x, axis=-1), ctx_1024, ctx_1024)
    x = x + _L0_ffn_ref(_layernorm(x, axis=-1), L0_ffn_centroids, L0_ffn_routing_bias, L0_ffn_Wfc_r, L0_ffn_Wproj_r, L0_ffn_Wfc_sh, L0_ffn_Wproj_sh)
    x = x + _L1_attn_ref(_layernorm(x, axis=-1), L1_attn_Wq, L1_attn_Wk, L1_attn_Wv, L1_attn_Wg, L1_attn_Wo, L1_attn_gn_weight, L1_attn_gn_bias)
    x = x + _L1_xattn_ref(_layernorm(x, axis=-1), ctx_1024, ctx_1024, L1_xattn_wq, L1_xattn_bq, L1_xattn_wk, L1_xattn_bk, L1_xattn_wv, L1_xattn_bv)
    x = x + _L1_ffn_ref(_layernorm(x, axis=-1), L1_ffn_Wg, L1_ffn_bg, L1_ffn_W1, L1_ffn_b1, L1_ffn_W2, L1_ffn_b2)
    return x

_drawn_inputs = setup_inputs


def setup_inputs(seed=0):
    import zlib

    import numpy as np

    out = dict(_drawn_inputs(seed))
    spreads = {'L0_attn_log_Lam_real': (-0.6931471824645996, 0.6),
     'L0_attn_D': (1.0, 0.2),
     'L0_attn_b_out': (0.0, 0.1),
     'L0_ffn_routing_bias': (0.0, 0.1),
     'L1_attn_gn_weight': (1.0, 0.6),
     'L1_attn_gn_bias': (0.0, 2.0)}
    factors = {'L0_attn_Lam_imag': 64.0,
     'L0_attn_B_real': 3.192,
     'L0_attn_B_imag': 3.178,
     'L0_attn_C_real': 3.167,
     'L0_attn_C_imag': 3.178,
     'L1_xattn_wq': 3.514,
     'L1_xattn_bq': 8.0,
     'L1_xattn_wk': 3.467,
     'L1_xattn_bk': 64.0,
     'L1_xattn_bv': 2.669,
     'L1_ffn_bg': 4.103,
     'L1_ffn_b1': 8.0,
     'L1_ffn_b2': 7.977}
    for name, (base, spread) in spreads.items():
        noise = np.random.default_rng([zlib.crc32(name.encode()), seed]).standard_normal(out[name].shape)
        drawn = base * np.exp(spread * noise) if base else spread * noise
        out[name] = jnp.asarray(drawn.astype(out[name].dtype))
    for name, factor in factors.items():
        out[name] = (out[name] * factor).astype(out[name].dtype)
    return out
```

```python
from contextlib import ExitStack
import math

import numpy as np
import concourse.bass as bass
from concourse import mybir

F32 = mybir.dt.float32
I32 = mybir.dt.int32
ACT = mybir.ActivationFunctionType
ALU = mybir.AluOpType
AXIS = mybir.AxisListType

P = 128
D = 128
BATCH, SEQ = 64, 64
TOKENS = BATCH * SEQ
TILES = TOKENS // P
EPS = 1e-5


def need(eng, sem, value):
    if isinstance(value, int) and value <= 0:
        return
    eng.wait_ge(sem, value)


def skewed(eng, items, depth, step, unroll=2, peeled=1):
    for s in range(peeled * unroll):
        step(s // unroll, s % unroll)
    with eng.Fori(peeled, items // unroll) as i:
        for k in range(unroll):
            step(i, k)
    for s in range(items, items + depth):
        step(s // unroll, s % unroll)


def live(m, items):
    return not isinstance(m, int) or 0 <= m < items


class Program:

    def __init__(self, nc, ctx, dram):
        self.nc, self.ctx, self.dram = nc, ctx, dram
        self.phase_ctx, self.phase_sems = None, []
        self.X = self.sbuf("X", [P, TILES, D])
        self.stats = self.sbuf("stats", [P, TILES, 6])
        self.mean = self.sbuf("mean", [P, TILES])
        self.rstd = self.sbuf("rstd", [P, TILES])
        self.ident = self.sbuf("ident", [P, P])

    def sem(self, name):
        handle = self.phase_ctx.enter_context(self.nc.semaphore(name))
        self.phase_sems.append(handle.num)
        return handle

    def run(self, phase):
        self.phase_sems = []
        with ExitStack() as self.phase_ctx:
            phase(self)
        numbers = sorted(self.phase_sems)
        starts = [n for n in numbers if n - 1 not in numbers]
        ends = [n + 1 for n in numbers if n + 1 not in numbers]
        with self.nc.Block() as block:

            @block.sync
            def _(sp):
                for low, high in zip(starts, ends):
                    sp.sem_clear(range(low, high))

    def sbuf(self, name, shape, dt=F32, ctx=None):
        return (ctx or self.ctx).enter_context(self.nc.sbuf_tensor(name, shape, dt))

    def banks(self, name, ctx):
        return [ctx.enter_context(self.nc.psum_tensor(f"{name}_bank{b}", [P, 512], F32)) for b in range(8)]


def row_statistics(g, name):
    nc = g.nc
    with ExitStack() as ctx:
        diff = g.sbuf(f"{name}_ln_diff", [P, TILES], ctx=ctx)
        var = g.sbuf(f"{name}_ln_var", [P, TILES], ctx=ctx)
        minus_half = g.sbuf(f"{name}_ln_minus_half", [P, TILES], ctx=ctx)
        step = g.sem(f"{name}_ln_stat_step")
        var_ready = g.sem(f"{name}_ln_var_ready")
        filled = g.sem(f"{name}_ln_minus_half_filled")
        rstd_ready = g.sem(f"{name}_ln_rstd_ready")
        st = g.stats
        with nc.Block() as block:

            @block.vector
            def _(dve):
                dve.tensor_tensor(g.mean[:], st[:, :, 1], st[:, :, 4], ALU.add)
                dve.tensor_tensor(diff[:], st[:, :, 1], st[:, :, 4], ALU.subtract)
                dve.tensor_tensor(var[:], st[:, :, 2], st[:, :, 5], ALU.add).then_inc(step, 1)
                dve.wait_ge(step, 1)
                dve.tensor_scalar(g.mean[:], g.mean[:], 0.5, None, ALU.mult)
                dve.tensor_tensor(diff[:], diff[:], diff[:], ALU.mult)
                dve.tensor_scalar(var[:], var[:], 1.0 / D, EPS, ALU.mult, ALU.add).then_inc(step, 1)
                dve.wait_ge(step, 2)
                dve.scalar_tensor_tensor(out=var[:], in0=diff[:], scalar=0.25, in1=var[:],
                                         op0=ALU.mult, op1=ALU.add).then_inc(var_ready, 1)

            @block.gpsimd
            def _(pool):
                pool.memset(minus_half[:], -0.5).then_inc(filled, 1)
                pool.wait_ge(filled, 1)
                pool.wait_ge(var_ready, 1)
                pool.tensor_tensor(g.rstd[:], var[:], minus_half[:], ALU.pow).then_inc(rstd_ready, 1)


GROUP = 4
GROUPS = TILES // GROUP
GT = GROUP * P
STATES = 64
TWO_PI_HI = 201.0 / 32.0
TWO_PI_LO = 2.0 * math.pi - TWO_PI_HI
TWO_PI_MID = float(np.float32(round(TWO_PI_LO * 2**21) / 2**21))
TWO_PI_END = TWO_PI_LO - TWO_PI_MID
ROUND_1 = 1.5 * 2**23
LN2_HI = 0.693359375
LN2_LO = math.log(2.0) - LN2_HI


def ssm_tables(g, t):
    nc, dram = g.nc, g.dram
    with ExitStack() as ctx:
        def sb(name, shape, dt=F32):
            return g.sbuf(f"ssm_{name}", shape, dt, ctx)

        log_lam, lam_im, log_dt = sb("log_lam", [P, 1]), sb("lam_im", [P, 1]), sb("log_dt", [P, 1])
        b_re_im, b_im_re = sb("b_re_im", [D, P]), sb("b_im_re", [D, P])
        c_re_im, c_im_re = sb("c_re_im", [D, P]), sb("c_im_re", [D, P])
        w_out, d_col = sb("w_out", [D, D]), sb("d_col", [D, 1])
        time_row = sb("time_row", [P, SEQ])
        dt, n, r, poly = sb("dt", [P, 1]), sb("n", [P, 1]), sb("r", [P, 1]), sb("poly", [P, 1])
        n_int = sb("n_int", [P, 1], I32)
        lam, mag = sb("lam", [P, 1]), sb("mag", [P, 1])
        theta, theta_hi, theta_lo = sb("theta", [P, 1]), sb("theta_hi", [P, 1]), sb("theta_lo", [P, 1])
        turn, ang, ang_lo, ang_cos = (sb(k, [P, SEQ]) for k in ("turn", "ang", "ang_lo", "ang_cos"))
        folded = [ctx.enter_context(nc.psum_tensor(f"ssm_folded{i}", [P, 512], F32)) for i in range(2)]
        loaded = g.sem("ssm_parameters_loaded")
        step = g.sem("ssm_table_step")
        lam_ready, arg_ready, mag_ready = g.sem("ssm_lam_ready"), g.sem("ssm_arg_ready"), g.sem("ssm_mag_ready")
        ang_ready, sin_ready = g.sem("ssm_angles_ready"), g.sem("ssm_sines_ready")
        c_ready, fold_done = g.sem("ssm_c_ready"), g.sem("ssm_fold_done")
        with nc.Block() as block:

            @block.sync
            def _(sp):
                for i in range(4):
                    sp.dma_start(g.X[:, 8 * i:8 * i + 8, :],
                                 dram["x"].rearrange("(i p) d -> p i d", p=P)[:, 8 * i:8 * i + 8, :])\
                        .then_inc(t["x_loaded"][i], 16)

            @block.scalar
            def _(act):
                loads = [
                    (log_lam[0:STATES, :], dram["L0_attn_log_Lam_real"]),
                    (log_lam[STATES:P, :], dram["L0_attn_log_Lam_real"]),
                    (lam_im[0:STATES, :], dram["L0_attn_Lam_imag"]),
                    (lam_im[STATES:P, :], dram["L0_attn_Lam_imag"]),
                    (log_dt[:], dram["L0_attn_log_dt"].to_broadcast([P, 1])),
                    (b_re_im[:], dram["ssm_b_re_im"]), (b_im_re[:], dram["ssm_b_im_re"]),
                    (c_re_im[:], dram["ssm_c_re_im"]), (c_im_re[:], dram["ssm_c_im_re"]),
                    (w_out[:], dram["ssm_w_out"]), (d_col[:], dram["L0_attn_D"]),
                    (time_row[:], dram["time_row"]), (g.ident[:], dram["ident"]),
                    (t["b_out"][:], dram["L0_attn_b_out"].to_broadcast([P, D])),
                ]
                for dst, src in loads:
                    act.dma_start(dst, src).then_inc(loaded, 16)
                act.wait_ge(loaded, 16 * 14)
                nc.scalar.activation(lam[:], log_lam[:], ACT.Exp).then_inc(lam_ready, 1)
                act.wait_ge(arg_ready, 1)
                nc.scalar.activation(mag[:], lam[:], ACT.Exp, scale=-1.0).then_inc(mag_ready, 1)
                act.wait_ge(ang_ready, 1)
                nc.scalar.activation(t["sin"][:], ang[:], ACT.Sin)
                nc.scalar.activation(t["cos"][:], ang_cos[:], ACT.Sin).then_inc(sin_ready, 1)

            @block.vector
            def _(dve):
                done = [0]

                def seq(ins):
                    done[0] += 1
                    ins.then_inc(step, 1)
                    dve.wait_ge(step, done[0])

                dve.wait_ge(loaded, 16 * 14)
                seq(dve.tensor_scalar(n[:], log_dt[:], 1.0 / math.log(2.0), ROUND_1, ALU.mult, ALU.add))
                seq(dve.tensor_scalar(n[:], n[:], ROUND_1, None, ALU.subtract))
                seq(dve.tensor_scalar(n[:], n[:], -126.0, 127.0, ALU.max, ALU.min))
                seq(dve.scalar_tensor_tensor(out=r[:], in0=n[:], scalar=-LN2_HI, in1=log_dt[:],
                                             op0=ALU.mult, op1=ALU.add))
                seq(dve.scalar_tensor_tensor(out=r[:], in0=n[:], scalar=-LN2_LO, in1=r[:],
                                             op0=ALU.mult, op1=ALU.add))
                seq(dve.tensor_scalar(poly[:], r[:], 1.0 / math.factorial(8), 1.0 / math.factorial(7),
                                      ALU.mult, ALU.add))
                for k in range(6, -1, -1):
                    seq(dve.tensor_scalar(poly[:], poly[:], r[:], 1.0 / math.factorial(k), ALU.mult, ALU.add))
                seq(dve.tensor_scalar(n[:], n[:], 127.0, 2.0**23, ALU.add, ALU.mult))
                seq(dve.tensor_copy(n_int[:], n[:]))
                seq(dve.tensor_tensor(dt[:], poly[:], n_int[:].bitcast(F32), ALU.mult))
                seq(dve.tensor_tensor(theta[:], lam_im[:], dt[:], ALU.mult))
                seq(dve.tensor_scalar(n[:], theta[:], 1.0 / (2 * math.pi), ROUND_1, ALU.mult, ALU.add))
                seq(dve.tensor_scalar(n[:], n[:], ROUND_1, None, ALU.subtract))
                for part in (TWO_PI_HI, TWO_PI_MID, TWO_PI_END):
                    seq(dve.scalar_tensor_tensor(out=theta[:], in0=n[:], scalar=-part, in1=theta[:],
                                                 op0=ALU.mult, op1=ALU.add))
                seq(dve.tensor_scalar(theta_hi[:], theta[:], 1.5 * 2**13, 1.5 * 2**13, ALU.add, ALU.subtract))
                seq(dve.tensor_tensor(theta_lo[:], theta[:], theta_hi[:], ALU.subtract))
                seq(dve.tensor_scalar(turn[:], time_row[:], theta[:], 1.0 / (2 * math.pi), ALU.mult, ALU.mult))
                seq(dve.tensor_scalar(turn[:], turn[:], ROUND_1, ROUND_1, ALU.add, ALU.subtract))
                seq(dve.tensor_scalar(ang[:], time_row[:], theta_hi[:], None, ALU.mult))
                seq(dve.tensor_scalar(ang_lo[:], time_row[:], theta_lo[:], None, ALU.mult))
                seq(dve.scalar_tensor_tensor(out=ang[:], in0=turn[:], scalar=-TWO_PI_HI, in1=ang[:],
                                             op0=ALU.mult, op1=ALU.add))
                seq(dve.scalar_tensor_tensor(out=ang[:], in0=turn[:], scalar=-TWO_PI_LO, in1=ang[:],
                                             op0=ALU.mult, op1=ALU.add))
                seq(dve.tensor_tensor(ang[:], ang[:], ang_lo[:], ALU.add))
                seq(dve.tensor_scalar(ang_cos[:], ang[:], math.pi / 2, -2 * math.pi, ALU.is_gt, ALU.mult))
                seq(dve.scalar_tensor_tensor(out=ang_cos[:], in0=ang[:], scalar=math.pi / 2, in1=ang_cos[:],
                                             op0=ALU.add, op1=ALU.add))
                top = 3.1415925
                seq(dve.tensor_scalar(ang[:], ang[:], -top, top, ALU.max, ALU.min))
                seq(dve.tensor_scalar(ang_cos[:], ang_cos[:], -top, top, ALU.max, ALU.min))
                dve.tensor_copy(turn[:], turn[:]).then_inc(ang_ready, 1)
                seq(dve.tensor_scalar(t["u_cos"][:], b_re_im[:], dt[:], None, ALU.mult))
                seq(dve.tensor_scalar(t["u_sin"][:], b_im_re[:], dt[:], None, ALU.mult))
                seq(dve.tensor_scalar(c_re_im[:, STATES:P], c_re_im[:, STATES:P], -1.0, None, ALU.mult))
                dve.tensor_scalar(c_im_re[:, 0:STATES], c_im_re[:, 0:STATES], -1.0, None, ALU.mult)\
                    .then_inc(c_ready, 1)
                seq(dve.tensor_scalar(t["w_skip"][:], w_out[:], d_col[:], None, ALU.mult))
                dve.wait_ge(fold_done, 1)
                dve.tensor_copy(t["w_cos"][:], folded[0][:, 0:D])
                seq(dve.tensor_copy(t["w_sin"][:], folded[1][:, 0:D]))
                dve.wait_ge(lam_ready, 1)
                dve.tensor_tensor(lam[:], lam[:], dt[:], ALU.mult).then_inc(arg_ready, 1)
                seq(dve.memset(t["decay"][:], 0.0))
                dve.wait_ge(mag_ready, 1)
                dve.tensor_scalar(t["decay"][:, :, 1:SEQ], t["decay"][:, :, 1:SEQ], mag[:], None, ALU.add)
                dve.wait_ge(sin_ready, 1)
                seq(dve.tensor_scalar(t["sin"][STATES:P, :], t["sin"][STATES:P, :], -1.0, None, ALU.mult))
                for i in range(TILES):
                    if i % 8 == 0:
                        dve.wait_ge(t["x_loaded"][i // 8], 16)
                    dve.bn_stats(g.stats[:, i, :], g.X[:, i, :])

            @block.tensor
            def _(pe):
                pe.wait_ge(loaded, 16 * 14)
                pe.wait_ge(c_ready, 1)
                pe.matmul(folded[0][:, 0:D], c_re_im[:], w_out[:], start=True, stop=True)
                pe.matmul(folded[1][:, 0:D], c_im_re[:], w_out[:], start=True, stop=True).then_inc(fold_done, 1)


def ssm_phase(g):
    nc = g.nc
    with ExitStack() as ctx:
        def sb(name, shape):
            return g.sbuf(f"ssm_{name}", shape, ctx=ctx)

        t = {"x_loaded": [g.sem(f"x_loaded{i}") for i in range(4)]}
        for name, shape in (("cos", [P, SEQ]), ("sin", [P, SEQ]), ("decay", [P, GT // SEQ, SEQ]),
                            ("u_cos", [D, P]), ("u_sin", [D, P]), ("w_cos", [P, D]), ("w_sin", [P, D]),
                            ("w_skip", [D, D]), ("b_out", [P, D])):
            t[name] = sb(name, shape)
        ssm_tables(g, t)
        row_statistics(g, "ssm")
        xn = [sb(f"xn{k}", [P, GROUP, D]) for k in range(2)]
        xnT = [sb(f"xnT{k}", [D, GT]) for k in range(3)]
        part_cos = [sb(f"part_cos{k}", [P, GT]) for k in range(2)]
        part_sin = [sb(f"part_sin{k}", [P, GT]) for k in range(2)]
        z = [sb(f"z{k}", [P, GT]) for k in range(2)]
        z_cos = [sb(f"z_cos{k}", [P, GT]) for k in range(2)]
        z_sin = [sb(f"z_sin{k}", [P, GT]) for k in range(2)]
        banks = g.banks("ssm", ctx)
        bank_t, bank_uc, bank_us, bank_o = banks[0:2], banks[2:4], banks[4:6], banks[6:8]
        names = ("xn_ready", "xnT_in_psum", "xnT_ready", "inputs_in_psum", "parts_ready", "drive_ready",
                 "z_ready", "z_cos_ready", "z_sin_ready", "out_in_psum", "bias_added", "x_updated")
        S = {k: g.sem(f"ssm_{k}") for k in names}
        batch = lambda ap: ap.rearrange("p (b t) -> p b t", t=SEQ)
        over = lambda ap: ap.unsqueeze(1).to_broadcast([P, GT // SEQ, SEQ])
        N = GROUPS
        with nc.Block() as block:

            @block.vector
            def _(dve):
                for s in range(N + 2):
                    if s < N:
                        need(dve, S["xnT_in_psum"], s - 1)
                        for j in range(GROUP):
                            i = GROUP * s + j
                            last = dve.tensor_scalar(xn[s % 2][:, j, :], g.X[:, i, :], g.mean[:, i:i + 1],
                                                     g.rstd[:, i:i + 1], ALU.subtract, ALU.mult)
                        last.then_inc(S["xn_ready"], 1)
                    m = s - 1
                    if 0 <= m < N:
                        dve.wait_ge(S["drive_ready"], m + 1)
                        need(dve, S["z_sin_ready"], m - 1)
                        dve.tensor_tensor_scan(z[m % 2][:], t["decay"][:].rearrange("p b t -> p (b t)"),
                                               part_cos[m % 2][:], 0.0, ALU.mult, ALU.add)\
                            .then_inc(S["z_ready"], 1)
                        dve.wait_ge(S["z_ready"], m + 1)
                        need(dve, S["out_in_psum"], m - 1)
                        dve.tensor_tensor(batch(z_cos[m % 2][:]), batch(z[m % 2][:]), over(t["cos"][:]),
                                          ALU.mult).then_inc(S["z_cos_ready"], 1)
                    if s < N:
                        dve.wait_ge(S["inputs_in_psum"], s + 1)
                        need(dve, S["z_ready"], s - 1)
                        dve.tensor_tensor(batch(part_cos[s % 2][:]), batch(bank_uc[s % 2][:]), over(t["cos"][:]),
                                          ALU.mult)
                        dve.tensor_tensor(batch(part_sin[s % 2][:]), batch(bank_us[s % 2][:]), over(t["sin"][:]),
                                          ALU.mult).then_inc(S["parts_ready"], 1)
                    m = s - 2
                    if 0 <= m < N:
                        dve.wait_ge(S["out_in_psum"], m + 1)
                        dve.wait_ge(S["bias_added"], m + 1)
                        tiles = g.X[:, GROUP * m:GROUP * m + GROUP, :]
                        dve.tensor_tensor(tiles, bank_o[m % 2][:].rearrange("p (j d) -> p j d", d=D), tiles,
                                          ALU.add).then_inc(S["x_updated"], 1)
                        dve.wait_ge(S["x_updated"], m + 1)
                        for i in range(GROUP * m, GROUP * m + GROUP):
                            dve.bn_stats(g.stats[:, i, :], g.X[:, i, :])

            @block.gpsimd
            def _(pool):
                for s in range(N + 1):
                    if s < N:
                        pool.wait_ge(S["parts_ready"], s + 1)
                        pool.tensor_tensor(part_cos[s % 2][:], part_cos[s % 2][:], part_sin[s % 2][:], ALU.add)\
                            .then_inc(S["drive_ready"], 1)
                        tiles = g.X[:, GROUP * s:GROUP * s + GROUP, :]
                        pool.tensor_tensor(tiles, tiles, t["b_out"][:].unsqueeze(1).to_broadcast([P, GROUP, D]),
                                           ALU.add).then_inc(S["bias_added"], 1)
                    m = s - 1
                    if 0 <= m < N:
                        pool.wait_ge(S["z_ready"], m + 1)
                        need(pool, S["out_in_psum"], m - 1)
                        pool.tensor_tensor(batch(z_sin[m % 2][:]), batch(z[m % 2][:]), over(t["sin"][:]),
                                           ALU.mult).then_inc(S["z_sin_ready"], 1)

            @block.scalar
            def _(act):
                for s in range(N):
                    act.wait_ge(S["xnT_in_psum"], s + 1)
                    need(act, S["out_in_psum"], s - 2)
                    nc.scalar.activation(xnT[s % 3][:], bank_t[s % 2][:], ACT.Copy).then_inc(S["xnT_ready"], 1)

            @block.tensor
            def _(pe):
                for s in range(N + 2):
                    if s < N:
                        pe.wait_ge(S["xn_ready"], s + 1)
                        need(pe, S["xnT_ready"], s - 1)
                        for j in range(GROUP):
                            last = pe.transpose(bank_t[s % 2][:, j * P:(j + 1) * P], xn[s % 2][:, j, :], g.ident[:])
                        last.then_inc(S["xnT_in_psum"], 1)
                    m = s - 2
                    if 0 <= m < N:
                        pe.wait_ge(S["z_cos_ready"], m + 1)
                        pe.wait_ge(S["z_sin_ready"], m + 1)
                        need(pe, S["x_updated"], m - 1)
                        for j in range(GROUP):
                            cols = slice(j * P, (j + 1) * P)
                            out = bank_o[m % 2][:, cols]
                            pe.matmul(out, z_cos[m % 2][:, cols], t["w_cos"][:], start=True, stop=False)
                            pe.matmul(out, z_sin[m % 2][:, cols], t["w_sin"][:], start=False, stop=False)
                            last = pe.matmul(out, xnT[m % 3][:, cols], t["w_skip"][:], start=False, stop=True)
                        last.then_inc(S["out_in_psum"], 1)
                    if s < N:
                        pe.wait_ge(S["xnT_ready"], s + 1)
                        need(pe, S["parts_ready"], s - 1)
                        pe.matmul(bank_uc[s % 2][:], t["u_cos"][:], xnT[s % 3][:], start=True, stop=True)
                        pe.matmul(bank_us[s % 2][:], t["u_sin"][:], xnT[s % 3][:], start=True, stop=True)\
                            .then_inc(S["inputs_in_psum"], 1)


HEADS, HEAD = 16, 8
QUAD = 4
QUADS = BATCH // QUAD
QKEYS = QUAD * SEQ
OCT = 8
OCTS = BATCH // OCT
OKEYS = OCT * SEQ
OTILES = OKEYS // P


def project_context(g, kT, v_twice):
    nc, dram = g.nc, g.dram
    with ExitStack() as ctx:
        ctxT = [g.sbuf(f"kv_ctxT{k}", [D, OCT, 2, SEQ], ctx=ctx) for k in range(2)]
        wk, wv = g.sbuf("kv_wk", [D, D], ctx=ctx), g.sbuf("kv_wv", [D, D], ctx=ctx)
        bk = g.sbuf("kv_bk", [D, 1], ctx=ctx)
        banks = g.banks("kv", ctx)
        weights = g.sem("kv_weights_loaded")
        loaded = [g.sem(f"kv_context_loaded{k}") for k in range(2)]
        done, k_ready, v_ready = g.sem("kv_products_done"), g.sem("kv_k_ready"), g.sem("kv_v_ready")
        with nc.Block() as block:

            @block.sync
            def _(sp):
                for dst, src in ((wk, "xa_wk"), (wv, "xa_wv"), (bk, "L1_xattn_bk")):
                    sp.dma_start(dst[:], dram[src]).then_inc(weights, 16)

                def step(i, k):
                    s = 2 * i + k
                    need(sp, done, 2 * (s - 1))
                    for copy in range(2):
                        sp.dma_start(ctxT[k][:, :, copy, :], dram["ctxT"][:, bass.ds(s * OCT, OCT), :])\
                            .then_inc(loaded[k], 16)
                skewed(sp, OCTS, 0, step)

            @block.tensor
            def _(pe):
                pe.wait_ge(weights, 48)

                def step(i, k):
                    s = 4 * i + k
                    octet, row = k // 2, k % 2 * QUAD
                    pe.wait_ge(loaded[octet], 32 * (i + 1))
                    need(pe, k_ready, s - 1)
                    need(pe, v_ready, s - 1)
                    pe.matmul(banks[k % 2][:, 0:QKEYS], wk[:], ctxT[octet][:, row:row + QUAD, 0, :],
                              start=True, stop=True)
                    for b in range(QUAD):
                        last = pe.matmul(banks[2 + k % 2][:, b * D:(b + 1) * D], ctxT[octet][:, row + b, :, :], wv[:],
                                         start=True, stop=True)
                    last.then_inc(done, 1)
                skewed(pe, QUADS, 0, step, 4)

            @block.scalar
            def _(act):
                act.wait_ge(weights, 48)

                def step(i, k):
                    s = 2 * i + k
                    act.wait_ge(done, s + 1)
                    nc.scalar.activation(kT[:, bass.ds(s * QKEYS, QKEYS)], banks[k][:, 0:QKEYS], ACT.Identity,
                                         bias=bk[:]).then_inc(k_ready, 1)
                skewed(act, QUADS, 0, step)

            @block.vector
            def _(dve):
                def step(i, k):
                    s = 2 * i + k
                    dve.wait_ge(done, s + 1)
                    dve.tensor_copy(v_twice[:, bass.ds(s * QUAD, QUAD), :],
                                    banks[2 + k][:].rearrange("p (b d) -> p b d", d=D)).then_inc(v_ready, 1)
                skewed(dve, QUADS, 0, step)


def attention(g, name, projected):
    nc, dram = g.nc, g.dram
    row_statistics(g, name)
    with ExitStack() as ctx:
        def sb(n, shape):
            return g.sbuf(f"{name}_{n}", shape, ctx=ctx)

        if projected:
            kT, v_twice = sb("kT", [D, TOKENS]), sb("v_twice", [P, BATCH, D])
            project_context(g, kT, v_twice)
            wq, bq, bv = sb("wq", [D, D]), sb("bq", [D, 1]), sb("bv", [P, D])
            q = [sb(f"q{k}", [D, P]) for k in range(2)]
        else:
            v_rows = [sb(f"v_rows{k}", [P, OCT, D]) for k in range(2)]
        xn = [sb(f"xn{k}", [P, D]) for k in range(2)]
        xnT = [sb(f"xnT{k}", [D, P]) for k in range(2)]
        qT = q if projected else xnT
        k_diag = [sb(f"k_diag{k}", [D, HEADS, OCT, SEQ]) for k in range(2)]
        v_diag = [sb(f"v_diag{k}", [P, OCT, HEADS // 2, 2, HEAD + 1]) for k in range(2)]
        top = [sb(f"top{k}", [P, HEADS]) for k in range(2)]
        prob = [sb(f"prob{k}", [P, HEADS, SEQ]) for k in range(2)]
        probT = [sb(f"probT{k}", [P, HEADS // 2, P]) for k in range(2)]
        ones = sb("ones", [P, OCT, HEADS // 2, HEAD])
        recip = sb("recip", [P, HEADS])
        mixed = sb("mixed", [P, HEADS, HEAD])
        bank_s = [ctx.enter_context(nc.psum_tensor(f"{name}_scores{k}", [P, HEADS, SEQ], F32)) for k in range(2)]
        bank_t = ctx.enter_context(nc.psum_tensor(f"{name}_probT_psum", [P, HEADS // 2, P], F32))
        bank_o = ctx.enter_context(nc.psum_tensor(f"{name}_mixed_psum", [P, 512], F32))
        bank_x = ctx.enter_context(nc.psum_tensor(f"{name}_xT_psum", [P, 512], F32))
        names = ("weights_loaded", "first_cleared", "second_cleared", "v_cleared", "ones_set", "xn_ready", "xnT_in_psum", "xnT_ready", "q_in_psum",
                 "q_ready", "scores_in_psum", "top_ready", "shifted", "exp_ready", "probT_in_psum",
                 "probT_ready", "mixed_in_psum", "recip_ready", "mixed_ready", "x_updated", "v_diag_ready",
                 "bias_added")
        S = {k: g.sem(f"{name}_{k}") for k in names}
        k_loaded = [g.sem(f"{name}_k_loaded{k}") for k in range(2)]
        v_loaded = [g.sem(f"{name}_v_loaded{k}") for k in range(2)]
        q_ready = S["q_ready"] if projected else S["xnT_ready"]
        N, UNROLL = TILES, 2 * OTILES

        with nc.Block() as block:

            @block.sync
            def _(sp):
                if projected:
                    for dst, src in ((wq[:], dram["xa_wq"]), (bq[:], dram["L1_xattn_bq"]),
                                     (bv[:], dram["L1_xattn_bv"].to_broadcast([P, D]))):
                        sp.dma_start(dst, src).then_inc(S["weights_loaded"], 16)
                sp.wait_ge(S["first_cleared"], 1)

                def step(i, k):
                    j = 2 * i + k
                    if isinstance(j, int) and j == 1:
                        sp.wait_ge(S["second_cleared"], 1)
                    need(sp, S["scores_in_psum"], OTILES * (j - 1))
                    for h in range(HEADS):
                        rows = slice(h * HEAD, (h + 1) * HEAD)
                        if projected:
                            src = kT[rows, bass.ds(j * OKEYS, OKEYS)].rearrange("p (b t) -> p b t", t=SEQ)
                        else:
                            src = dram["ctxT"][rows, bass.ds(j * OCT, OCT), :]
                        sp.dma_start(k_diag[k][rows, h, :, :], src).then_inc(k_loaded[k], 16)
                    if not projected:
                        need(sp, S["v_diag_ready"], j - 1)
                        for half in range(2):
                            sp.dma_start(v_rows[k][half * SEQ:(half + 1) * SEQ, :, :],
                                         dram["ctx"].rearrange("b t d -> t b d")[:, bass.ds(j * OCT, OCT), :])\
                                .then_inc(v_loaded[k], 16)
                skewed(sp, OCTS, 0, step)

            @block.gpsimd
            def _(pool):
                pool.memset(k_diag[0][:], 0.0).then_inc(S["first_cleared"], 1)
                for k in range(2):
                    pool.memset(v_diag[k][:], 0.0).then_inc(S["v_cleared"], 1)
                pool.memset(ones[:], 1.0).then_inc(S["v_cleared"], 1)
                pool.wait_ge(S["v_cleared"], 3)
                for k in range(2):
                    for half in range(2):
                        pool.memset(v_diag[k][half * SEQ:(half + 1) * SEQ, :, :, half, HEAD:HEAD + 1], 1.0)\
                            .then_inc(S["ones_set"], 1)
                if projected:
                    pool.wait_ge(S["weights_loaded"], 48)

                def step(i, k):
                    j = 2 * i + k
                    need(pool, S["mixed_in_psum"], OTILES * (j - 1))
                    if not projected:
                        pool.wait_ge(v_loaded[k], 32 * (i + 1))
                    else:
                        need(pool, S["bias_added"], OTILES * j)
                    for half in range(2):
                        rows = slice(half * SEQ, (half + 1) * SEQ)
                        src = v_twice[rows, bass.ds(j * OCT, OCT), :] if projected else v_rows[k][rows, :, :]
                        src = src.rearrange("p b (h c d) -> p b h c d", c=2, d=HEAD)[:, :, :, half, :]
                        last = pool.tensor_tensor(v_diag[k][rows, :, :, half, 0:HEAD], src,
                                                  ones[rows, :, :, :], ALU.mult)
                    last.then_inc(S["v_diag_ready"], 1)
                    if projected:
                        pool.wait_ge(S["v_diag_ready"], j + 1)
                        for m in [OTILES * j + t for t in range(OTILES)]:
                            pool.wait_ge(S["xn_ready"], m + 1)
                            pool.tensor_tensor(g.X[:, m, :], g.X[:, m, :], bv[:], ALU.add)\
                                .then_inc(S["bias_added"], 1)
                skewed(pool, OCTS, 0, step)

            @block.vector
            def _(dve):
                dve.memset(k_diag[1][:], 0.0).then_inc(S["second_cleared"], 1)

                def step(i, k):
                    s = UNROLL * i + k
                    m = s - 5
                    if live(m, N):
                        dve.wait_ge(S["mixed_in_psum"], m + 1)
                        need(dve, S["mixed_ready"], m)
                        out = bank_o[:, 0:HEADS * (HEAD + 1)].rearrange("p (h c) -> p h c", c=HEAD + 1)
                        dve.reciprocal(recip[:], out[:, :, HEAD]).then_inc(S["recip_ready"], 1)
                        dve.wait_ge(S["recip_ready"], m + 1)
                        need(dve, S["x_updated"], m)
                        dve.tensor_tensor(mixed[:], out[:, :, 0:HEAD],
                                          recip[:].unsqueeze(2).to_broadcast([P, HEADS, HEAD]), ALU.mult)\
                            .then_inc(S["mixed_ready"], 1)
                        dve.wait_ge(S["mixed_ready"], m + 1)
                        if projected:
                            dve.wait_ge(S["bias_added"], m + 1)
                        dve.tensor_tensor(g.X[:, m, :], g.X[:, m, :], mixed[:].rearrange("p h c -> p (h c)"),
                                          ALU.add).then_inc(S["x_updated"], 1)
                    if live(s, N):
                        need(dve, S["xnT_in_psum"], s - 1)
                        dve.tensor_scalar(xn[k % 2][:], g.X[:, s, :], g.mean[:, bass.ds(s, 1)],
                                          g.rstd[:, bass.ds(s, 1)], ALU.subtract, ALU.mult)\
                            .then_inc(S["xn_ready"], 1)
                    m, b = s - 2, (k - 2) % 2
                    if live(m, N):
                        dve.wait_ge(S["scores_in_psum"], m + 1)
                        need(dve, S["shifted"], m - 1)
                        dve.tensor_reduce(top[b][:], bank_s[b][:], AXIS.X, ALU.max).then_inc(S["top_ready"], 1)
                        dve.wait_ge(S["top_ready"], m + 1)
                        need(dve, S["probT_in_psum"], m - 1)
                        dve.tensor_tensor(prob[b][:], bank_s[b][:],
                                          top[b][:].unsqueeze(2).to_broadcast([P, HEADS, SEQ]), ALU.subtract)\
                            .then_inc(S["shifted"], 1)
                    m = s - 5
                    if live(m, N):
                        dve.wait_ge(S["x_updated"], m + 1)
                        dve.bn_stats(g.stats[:, m, :], g.X[:, m, :])
                skewed(dve, N, 5, step, UNROLL)

            @block.scalar
            def _(act):
                if projected:
                    act.wait_ge(S["weights_loaded"], 48)

                def step(i, k):
                    s = UNROLL * i + k
                    if live(s, N):
                        act.wait_ge(S["xnT_in_psum"], s + 1)
                        need(act, S["q_in_psum"] if projected else S["scores_in_psum"], s - 1)
                        nc.scalar.activation(xnT[k % 2][:], bank_x[:, 0:P], ACT.Copy).then_inc(S["xnT_ready"], 1)
                    if projected and live(s, N):
                        act.wait_ge(S["q_in_psum"], s + 1)
                        need(act, S["scores_in_psum"], s - 1)
                        nc.scalar.activation(qT[k % 2][:], bank_x[:, P:2 * P], ACT.Identity, bias=bq[:])\
                            .then_inc(S["q_ready"], 1)
                    m = s - 2
                    if live(m, N):
                        act.wait_ge(S["probT_in_psum"], m + 1)
                        need(act, S["mixed_in_psum"], m - 1)
                        nc.scalar.activation(probT[k % 2][:], bank_t[:], ACT.Copy).then_inc(S["probT_ready"], 1)
                    m, b = s - 1, (k - 1) % 2
                    if live(m, N):
                        act.wait_ge(S["shifted"], m + 1)
                        nc.scalar.activation(prob[b][:], prob[b][:], ACT.Exp, scale=1.0 / math.sqrt(HEAD))\
                            .then_inc(S["exp_ready"], 1)
                skewed(act, N, 2, step, UNROLL)

            @block.tensor
            def _(pe):
                pe.wait_ge(S["ones_set"], 4)
                if projected:
                    pe.wait_ge(S["weights_loaded"], 48)

                def step(i, k):
                    s = UNROLL * i + k
                    if live(s, N):
                        pe.wait_ge(S["xn_ready"], s + 1)
                        need(pe, q_ready, s)
                        pe.transpose(bank_x[:, 0:P], xn[k % 2][:], g.ident[:]).then_inc(S["xnT_in_psum"], 1)
                    m, b = s - 1, (k - 1) % 2
                    if live(m, N):
                        octet = ((k - 1) // OTILES) % 2
                        pe.wait_ge(k_loaded[octet], 16 * HEADS * (i + (k - 1) // UNROLL + 1))
                        pe.wait_ge(q_ready, m + 1)
                        need(pe, S["shifted"], m - 1)
                        for row in range(2):
                            for half in range(2):
                                heads = slice(8 * half, 8 * half + 8)
                                last = pe.matmul(bank_s[b][64 * row:64 * row + 64, heads, :],
                                                 qT[b][:, 64 * row:64 * row + 64],
                                                 k_diag[octet][:, heads, 2 * ((k - 1) % OTILES) + row, :], start=True, stop=True)
                        last.then_inc(S["scores_in_psum"], 1)
                    if projected and live(s, N):
                        pe.wait_ge(S["xnT_ready"], s + 1)
                        pe.matmul(bank_x[:, P:2 * P], wq[:], xnT[k % 2][:], start=True, stop=True)\
                            .then_inc(S["q_in_psum"], 1)
                    m, b = s - 2, (k - 2) % 2
                    if live(m, N):
                        pe.wait_ge(S["exp_ready"], m + 1)
                        need(pe, S["probT_ready"], m)
                        for hp in range(HEADS // 2):
                            last = pe.transpose(bank_t[:, hp, :],
                                                prob[b][:, 2 * hp:2 * hp + 2, :].rearrange("p h t -> p (h t)"),
                                                g.ident[:])
                        last.then_inc(S["probT_in_psum"], 1)
                    m, b = s - 3, (k - 3) % 2
                    if live(m, N):
                        octet = ((k - 3) // OTILES) % 2
                        pe.wait_ge(S["probT_ready"], m + 1)
                        pe.wait_ge(S["v_diag_ready"], 2 * i + (k - 3) // OTILES + 1)
                        need(pe, S["mixed_ready"], m)
                        for hp in range(HEADS // 2):
                            for row in range(2):
                                last = pe.matmul(
                                    bank_o[64 * row:64 * row + 64, 18 * hp:18 * hp + 18],
                                    probT[b][:, hp, 64 * row:64 * row + 64],
                                    v_diag[octet][:, 2 * ((k - 3) % OTILES) + row, hp, :, :].rearrange("p c d -> p (c d)"),
                                    start=True, stop=True)
                        last.then_inc(S["mixed_in_psum"], 1)
                skewed(pe, N, 3, step, UNROLL)


R_HEADS, R_KEY, R_VAL = 8, 64, 128


def retention_tables():
    freq = 1.0 / 10000.0 ** (np.arange(0, R_KEY, 2, dtype=np.float32) / np.float32(R_KEY))
    angle = (np.arange(P) % SEQ).astype(np.float32)[:, None] * freq[None, :].astype(np.float32)
    cos, sin = np.cos(angle.astype(np.float64)), np.sin(angle.astype(np.float64))
    gamma = 1.0 - np.exp2(-5.0 - np.arange(R_HEADS))
    rel = np.arange(SEQ)[None, :] - np.arange(SEQ)[:, None]
    decay = np.where(rel >= 0, gamma[:, None, None] ** np.maximum(rel, 0), 0.0) * R_KEY ** -0.5
    decay = np.tile(decay.transpose(1, 0, 2), (2, 1, 1))
    return (np.concatenate([cos, cos], 1).astype(np.float32), np.concatenate([-sin, sin], 1).astype(np.float32),
            decay.astype(np.float32))


def retention_phase(g):
    nc, dram = g.nc, g.dram
    row_statistics(g, "ret")
    with ExitStack() as ctx:
        def sb(n, shape):
            return g.sbuf(f"ret_{n}", shape, ctx=ctx)

        def ring(n, shape, size=2):
            return [sb(f"{n}{k}", shape) for k in range(size)]

        H, HP, W = R_HEADS, R_HEADS // 2, R_HEADS * R_VAL
        wqk, wv, wg = sb("wqk", [D, 1024]), sb("wv", [D, H, R_VAL]), sb("wg", [D, W])
        wo = sb("wo", [R_VAL, H, D])
        cos, sin, decay = sb("cos", [P, R_KEY]), sb("sin", [P, R_KEY]), sb("decay", [P, H, SEQ])
        gn_w, gn_b = sb("gn_w", [R_VAL, H]), sb("gn_b", [R_VAL, H])
        wv_mean = sb("wv_mean", [D, H])
        xn, xnT = ring("xn", [P, D]), ring("xnT", [D, P], 4)
        qk, turned = ring("qk", [P, 2, H, R_KEY]), ring("turned", [P, 2, H, R_KEY])
        q_diag, kT = ring("q_diag", [P, HP, 2, 2, SEQ]), ring("kT", [P, HP, P])
        v = ring("v", [P, H, R_VAL])
        s_diag = ring("s_diag", [P, H, 2, SEQ])
        square, normed = sb("square", [P, H, R_VAL]), ring("normed", [P, H, R_VAL])
        var, rstd = ring("var", [P, H]), ring("rstd", [P, H])
        minus_half = sb("minus_half", [P, H])
        gate, gated = ring("gate", [R_VAL, H, P]), ring("gated", [R_VAL, H, P])
        ps_qk, ps_vg, ps_t, ps_o = (ctx.enter_context(nc.psum_tensor(f"ret_ps{k}", [P, 1024], F32))
                                    for k in range(4))
        names = ("loaded", "cleared", "wv_step", "wv_ready", "xn_ready", "xnT_in_psum", "xnT_ready", "qk_in_psum",
                 "turned_ready", "qk_ready", "qkT_in_psum", "q_diag_ready", "kT_ready", "scores_in_psum",
                 "s_ready", "v_in_psum", "v_ready", "gate_in_psum", "gate_ready", "mixed_in_psum", "square_ready",
                 "sum_ready", "var_ready", "rstd_ready", "normed_ready", "normedT_in_psum", "scaled",
                 "biased", "gated_ready", "out_in_psum", "x_updated", "half_set")
        S = {k: g.sem(f"ret_{k}") for k in names}
        N, UNROLL, DEPTH = TILES, 4, 3
        heads = lambda ap: ap.rearrange("p (h c) -> p h c", c=R_VAL)

        with nc.Block() as block:

            @block.sync
            def _(sp):
                for dst, src in ((wv, "ret_wv"), (wqk, "ret_wqk"), (cos, "ret_cos"), (sin, "ret_sin"),
                                 (decay, "ret_decay"), (wg, "ret_wg"), (wo, "ret_wo"), (gn_w, "ret_gn_w"),
                                 (gn_b, "ret_gn_b")):
                    sp.dma_start(dst[:], dram[src]).then_inc(S["loaded"], 16)

            @block.gpsimd
            def _(pool):
                for k in range(2):
                    pool.memset(q_diag[k][:], 0.0).then_inc(S["cleared"], 1)
                    pool.memset(s_diag[k][:], 0.0).then_inc(S["cleared"], 1)
                pool.memset(minus_half[:], -0.5).then_inc(S["half_set"], 1)
                pool.wait_ge(S["loaded"], 16 * 9)
                pool.wait_ge(S["half_set"], 1)

                def step(i, k):
                    s = UNROLL * i + k
                    m, b = s - 2, k % 2
                    if live(m, N):
                        pool.wait_ge(S["var_ready"], m + 1)
                        need(pool, S["normed_ready"], m - 1)
                        pool.tensor_tensor(rstd[b][:], var[b][:], minus_half[:], ALU.pow).then_inc(S["rstd_ready"], 1)
                    if live(s, N):
                        pool.wait_ge(S["turned_ready"], s + 1)
                        pool.tensor_tensor(qk[k % 2][:], qk[k % 2][:], turned[k % 2][:], ALU.add)\
                            .then_inc(S["qk_ready"], 1)
                    m, b = s - 2, k % 2
                    if live(m, N):
                        pool.wait_ge(S["scaled"], m + 1)
                        pool.tensor_tensor(gated[b][:], gated[b][:], gn_b[:].unsqueeze(2).to_broadcast([R_VAL, H, P]),
                                           ALU.add).then_inc(S["biased"], 1)
                skewed(pool, N, 2, step, UNROLL)

            @block.vector
            def _(dve):
                dve.wait_ge(S["loaded"], 16 * 9)
                dve.tensor_reduce(wv_mean[:], wv[:], AXIS.X, ALU.add).then_inc(S["wv_step"], 1)
                dve.wait_ge(S["wv_step"], 1)
                dve.tensor_scalar(wv_mean[:], wv_mean[:], 1.0 / R_VAL, None, ALU.mult).then_inc(S["wv_step"], 1)
                dve.wait_ge(S["wv_step"], 2)
                dve.tensor_tensor(wv[:], wv[:], wv_mean[:].unsqueeze(2).to_broadcast([D, H, R_VAL]),
                                  ALU.subtract).then_inc(S["wv_ready"], 1)
                dve.wait_ge(S["cleared"], 4)

                def step(i, k):
                    s = UNROLL * i + k
                    m, b = s - 4, k % 2
                    if live(m, N):
                        dve.wait_ge(S["biased"], m + 1)
                        dve.wait_ge(S["gate_ready"], m + 1)
                        dve.tensor_tensor(gated[b][:], gated[b][:], gate[b][:], ALU.mult)\
                            .then_inc(S["gated_ready"], 1)
                    m, b = s - 3, (k - 3) % 2
                    if live(m, N):
                        dve.wait_ge(S["square_ready"], m + 1)
                        need(dve, S["rstd_ready"], m - 1)
                        dve.tensor_reduce(var[b][:], square[:], AXIS.X, ALU.add).then_inc(S["sum_ready"], 1)
                        dve.wait_ge(S["sum_ready"], m + 1)
                        dve.tensor_scalar(var[b][:], var[b][:], 1.0 / R_VAL, EPS, ALU.mult, ALU.add)\
                            .then_inc(S["var_ready"], 1)
                    m = s - 4
                    if live(m, N):
                        dve.wait_ge(S["out_in_psum"], m + 1)
                        dve.tensor_tensor(g.X[:, m, :], ps_vg[:, 0:D], g.X[:, m, :], ALU.add)\
                            .then_inc(S["x_updated"], 1)
                    m, b = s - 1, (k - 1) % 2
                    if live(m, N):
                        dve.wait_ge(S["qk_in_psum"], m + 1)
                        need(dve, S["qkT_in_psum"], m - 1)
                        src = ps_qk[:].rearrange("p (a e) -> p a e", e=R_KEY)
                        fold = lambda ap: ap.rearrange("p q h e -> p (q h) e")
                        dve.tensor_tensor(fold(qk[b][:]), src,
                                          cos[:].unsqueeze(1).to_broadcast([P, 2 * H, R_KEY]), ALU.mult)
                        for part in range(2):
                            to, of = slice(32 * part, 32 * part + 32), slice(32 - 32 * part, 64 - 32 * part)
                            last = dve.tensor_tensor(fold(turned[b][:])[:, :, to], src[:, :, of],
                                                     sin[:, to].unsqueeze(1).to_broadcast([P, 2 * H, 32]), ALU.mult)
                        last.then_inc(S["turned_ready"], 1)
                    m, b = s - 3, (k - 3) % 2
                    if live(m, N):
                        dve.wait_ge(S["rstd_ready"], m + 1)
                        need(dve, S["normedT_in_psum"], m - 1)
                        dve.tensor_tensor(normed[b][:], heads(ps_o[:]),
                                          rstd[b][:].unsqueeze(2).to_broadcast([P, H, R_VAL]), ALU.mult)\
                            .then_inc(S["normed_ready"], 1)
                    m, b = s - 2, k % 2
                    if live(m, N):
                        dve.wait_ge(S["scores_in_psum"], m + 1)
                        need(dve, S["mixed_in_psum"], m - 1)
                        for row in range(2):
                            rows = slice(64 * row, 64 * row + 64)
                            last = dve.tensor_tensor(s_diag[b][rows, :, row, :],
                                                     ps_t[rows, 0:512].rearrange("p (h t) -> p h t", t=SEQ),
                                                     decay[rows, :, :], ALU.mult)
                        last.then_inc(S["s_ready"], 1)
                    if live(s, N):
                        need(dve, S["xnT_in_psum"], s - 1)
                        dve.tensor_scalar(xn[k % 2][:], g.X[:, s, :], g.mean[:, bass.ds(s, 1)],
                                          g.rstd[:, bass.ds(s, 1)], ALU.subtract, ALU.mult)\
                            .then_inc(S["xn_ready"], 1)
                    m = s - 4
                    if live(m, N):
                        dve.wait_ge(S["x_updated"], m + 1)
                        dve.bn_stats(g.stats[:, m, :], g.X[:, m, :])
                    m, b = s - 3, (k - 3) % 2
                    if live(m, N):
                        dve.wait_ge(S["normedT_in_psum"], m + 1)
                        need(dve, S["out_in_psum"], m - 1)
                        dve.tensor_tensor(gated[b][:], heads(ps_t[:]),
                                          gn_w[:].unsqueeze(2).to_broadcast([R_VAL, H, P]), ALU.mult)\
                            .then_inc(S["scaled"], 1)
                skewed(dve, N, 4, step, UNROLL)

            @block.scalar
            def _(act):
                act.wait_ge(S["cleared"], 4)

                def step(i, k):
                    s = UNROLL * i + k
                    if live(s, N):
                        act.wait_ge(S["xnT_in_psum"], s + 1)
                        need(act, S["gate_in_psum"], s - 3)
                        nc.scalar.activation(xnT[k][:], ps_qk[:, 0:P], ACT.Copy).then_inc(S["xnT_ready"], 1)
                    m, b = s - 1, (k - 1) % 2
                    if live(m, N):
                        act.wait_ge(S["qkT_in_psum"], m + 1)
                        need(act, S["scores_in_psum"], m - 1)
                        for half in range(2):
                            rows = slice(64 * half, 64 * half + 64)
                            last = nc.scalar.activation(
                                q_diag[b][rows, :, :, half, :],
                                ps_t[rows, 0:512].rearrange("p (h r t) -> p h r t", r=2, t=SEQ), ACT.Copy)
                        last.then_inc(S["q_diag_ready"], 1)
                        nc.scalar.activation(kT[b][:], ps_t[:, 512:1024].rearrange("p (h t) -> p h t", t=P),
                                             ACT.Copy).then_inc(S["kT_ready"], 1)
                    if live(s, N):
                        act.wait_ge(S["v_in_psum"], s + 1)
                        need(act, S["mixed_in_psum"], s - 1)
                        nc.scalar.activation(v[k % 2][:], heads(ps_vg[:]), ACT.Copy).then_inc(S["v_ready"], 1)
                    m, b = s - 2, k % 2
                    if live(m, N):
                        act.wait_ge(S["gate_in_psum"], m + 1)
                        need(act, S["gated_ready"], m - 1)
                        nc.scalar.activation(gate[b][:], heads(ps_vg[:]), ACT.Silu).then_inc(S["gate_ready"], 1)
                    m = s - 1
                    if live(m, N):
                        act.wait_ge(S["mixed_in_psum"], m + 1)
                        need(act, S["sum_ready"], m)
                        nc.scalar.activation(square[:], heads(ps_o[:]), ACT.Square).then_inc(S["square_ready"], 1)
                skewed(act, N, 2, step, UNROLL)

            @block.tensor
            def _(pe):
                pe.wait_ge(S["wv_ready"], 1)
                pe.wait_ge(S["loaded"], 16 * 9)

                def step(i, k):
                    s = UNROLL * i + k
                    if live(s, N):
                        pe.wait_ge(S["xn_ready"], s + 1)
                        need(pe, S["turned_ready"], s)
                        pe.transpose(ps_qk[:, 0:P], xn[k % 2][:], g.ident[:]).then_inc(S["xnT_in_psum"], 1)
                    if live(s, N):
                        pe.wait_ge(S["xnT_ready"], s + 1)
                        for half in range(2):
                            cols = slice(512 * half, 512 * half + 512)
                            last = pe.matmul(ps_qk[:, cols], xnT[k][:], wqk[:, cols], start=True, stop=True)
                        last.then_inc(S["qk_in_psum"], 1)
                    m, b = s - 3, (k - 3) % 2
                    if live(m, N):
                        pe.wait_ge(S["gated_ready"], m + 1)
                        pe.wait_ge(S["gate_ready"], m + 1)
                        for h in range(H):
                            last = pe.matmul(ps_vg[:, 0:D], gated[b][:, h, :], wo[:, h, :],
                                             start=(h == 0), stop=(h == H - 1))
                        last.then_inc(S["out_in_psum"], 1)
                    m, b = s - 1, (k - 1) % 2
                    if live(m, N):
                        pe.wait_ge(S["qk_ready"], m + 1)
                        need(pe, S["scaled"], m - 1)
                        need(pe, S["s_ready"], m)
                        for which in range(2):
                            for hp in range(HP):
                                last = pe.transpose(
                                    ps_t[:, 512 * which + 128 * hp:512 * which + 128 * hp + 128],
                                    qk[b][:, which, 2 * hp:2 * hp + 2, :].rearrange("p h e -> p (h e)"),
                                    g.ident[:])
                        last.then_inc(S["qkT_in_psum"], 1)
                    if live(s, N):
                        need(pe, S["v_ready"], s)
                        need(pe, S["gate_ready"], s - 2)
                        need(pe, S["x_updated"], s - 2)
                        for half in range(2):
                            cols = slice(512 * half, 512 * half + 512)
                            last = pe.matmul(ps_vg[:, cols], xnT[k][:],
                                             wv[:].rearrange("p h c -> p (h c)")[:, cols], start=True, stop=True)
                        last.then_inc(S["v_in_psum"], 1)
                    m, b = s - 1, (k - 1) % 2
                    if live(m, N):
                        pe.wait_ge(S["q_diag_ready"], m + 1)
                        pe.wait_ge(S["kT_ready"], m + 1)
                        for hp in range(HP):
                            for row in range(2):
                                last = pe.matmul(ps_t[64 * row:64 * row + 64, 128 * hp:128 * hp + 128],
                                                 kT[b][:, hp, 64 * row:64 * row + 64],
                                                 q_diag[b][:, hp, row, :, :].rearrange("p h t -> p (h t)"),
                                                 start=True, stop=True)
                        last.then_inc(S["scores_in_psum"], 1)
                    m, b = s - 2, (k - 2) % 4
                    if live(m, N):
                        if live(s, N):
                            pe.wait_ge(S["v_ready"], s + 1)
                        else:
                            need(pe, S["x_updated"], s - 2)
                        for h in range(H):
                            last = pe.matmul(ps_vg[:, 128 * h:128 * h + 128], wg[:, 128 * h:128 * h + 128],
                                             xnT[b][:], start=True, stop=True)
                        last.then_inc(S["gate_in_psum"], 1)
                        pe.wait_ge(S["normed_ready"], m + 1)
                        if live(s - 1, N):
                            pe.wait_ge(S["s_ready"], m + 2)
                        else:
                            need(pe, S["scaled"], m)
                        for h in range(H):
                            last = pe.transpose(ps_t[:, 128 * h:128 * h + 128], normed[k % 2][:, h, :], g.ident[:])
                        last.then_inc(S["normedT_in_psum"], 1)
                    m, b = s - 1, (k - 1) % 2
                    if live(m, N):
                        pe.wait_ge(S["s_ready"], m + 1)
                        pe.wait_ge(S["v_ready"], m + 1)
                        need(pe, S["normed_ready"], m)
                        for h in range(H):
                            last = pe.matmul(ps_o[:, 128 * h:128 * h + 128],
                                             s_diag[b][:, h, :, :].rearrange("p r t -> p (r t)"),
                                             v[b][:, h, :], start=True, stop=True)
                        last.then_inc(S["mixed_in_psum"], 1)
                skewed(pe, N, DEPTH, step, UNROLL)


EXPERTS, FFN = 8, 512
FT = FFN // P
BIG = 1.0e38


def route(g, name, ctx, spec, xnT_all):
    nc, dram = g.nc, g.dram
    row_statistics(g, name)
    combine = g.sbuf(f"{name}_combine", [P, TILES, EXPERTS], ctx=ctx)
    with ExitStack() as own:
        def sb(n, shape):
            return g.sbuf(f"{name}_{n}", shape, ctx=own)

        gate_w, gate_b = sb("gate_w", [D, EXPERTS]), sb("gate_b", [P, EXPERTS])
        rank = sb("rank", [P, EXPERTS])
        xn, xnT = [sb(f"xn{k}", [P, D]) for k in range(2)], [sb(f"xnT{k}", [D, P]) for k in range(2)]
        logit, raw = sb("logit", [P, TILES, EXPERTS]), sb("raw", [P, TILES, EXPERTS])
        first, key = sb("first", [P, TILES, EXPERTS]), sb("key", [P, TILES, EXPERTS])
        second, score = sb("second", [P, TILES, EXPERTS]), sb("score", [P, TILES, EXPERTS])
        top, top2, rec = sb("top", [P, TILES]), sb("top2", [P, TILES]), sb("rec", [P, TILES])
        bank_x = [own.enter_context(nc.psum_tensor(f"{name}_xT_psum{k}", [P, 512], F32)) for k in range(2)]
        bank_l = own.enter_context(nc.psum_tensor(f"{name}_logit_psum", [P, 2, 512], F32))
        names = ("loaded", "xn_ready", "xnT_in_psum", "xnT_ready", "logits_in_psum", "step", "exp_in", "exp_out",
                 "logit_saved", "kept", "xn_added")
        S = {k: g.sem(f"{name}_r_{k}") for k in names}
        bc = lambda ap: ap[:].unsqueeze(2).to_broadcast([P, TILES, EXPERTS])
        with nc.Block() as block:

            @block.sync
            def _(sp):
                sp.dma_start(gate_w[:], dram[spec["gate_w"]]).then_inc(S["loaded"], 16)
                sp.dma_start(gate_b[:], dram[spec["gate_b"]].to_broadcast([P, EXPERTS])).then_inc(S["loaded"], 16)
                sp.dma_start(rank[:], dram["rank"]).then_inc(S["loaded"], 16)

            @block.vector
            def _(dve):
                done = [0]

                def seq(ins):
                    done[0] += 1
                    ins.then_inc(S["step"], 1)
                    dve.wait_ge(S["step"], done[0])

                def xn_step(i, k):
                    s = 2 * i + k
                    if live(s, TILES):
                        need(dve, S["xnT_in_psum"], s - 1)
                        if spec["plus_xn"]:
                            need(dve, S["xn_added"], s - 1)
                        dve.tensor_scalar(xn[k][:], g.X[:, s, :], g.mean[:, bass.ds(s, 1)],
                                          g.rstd[:, bass.ds(s, 1)], ALU.subtract, ALU.mult)\
                            .then_inc(S["xn_ready"], 1)
                    m = s - 1
                    if live(m, TILES):
                        dve.wait_ge(S["logits_in_psum"], m + 1)
                        dve.tensor_copy(raw[:, m, :], bank_l[:, (k - 1) % 2, 0:EXPERTS]).then_inc(S["logit_saved"], 1)
                skewed(dve, TILES, 1, xn_step)
                dve.wait_ge(S["loaded"], 48)
                dve.wait_ge(S["logit_saved"], TILES)
                seq(dve.tensor_tensor(logit[:], raw[:], gate_b[:].unsqueeze(1).to_broadcast([P, TILES, EXPERTS]),
                                      ALU.add))

                def one_hot_of_max(out, values, peak):
                    seq(dve.tensor_reduce(peak[:], values[:], AXIS.X, ALU.max))
                    seq(dve.tensor_tensor(key[:], values[:], bc(peak), ALU.is_equal))
                    seq(dve.tensor_tensor(key[:], key[:], rank[:].unsqueeze(1).to_broadcast([P, TILES, EXPERTS]),
                                          ALU.mult))
                    seq(dve.tensor_reduce(rec[:], key[:], AXIS.X, ALU.max))
                    seq(dve.tensor_tensor(out[:], key[:], bc(rec), ALU.is_equal))

                one_hot_of_max(first, logit, top)
                seq(dve.scalar_tensor_tensor(out=score[:], in0=first[:], scalar=-BIG, in1=logit[:],
                                             op0=ALU.mult, op1=ALU.add))
                one_hot_of_max(second, score, top2)
                if spec["kind"] == "sigmoid":
                    dve.tensor_copy(key[:], raw[:]).then_inc(S["exp_in"], 1)
                    dve.wait_ge(S["exp_out"], 1)
                    seq(dve.tensor_scalar(score[:], score[:], 1.0, None, ALU.add))
                    seq(dve.reciprocal(score[:], score[:]))
                    seq(dve.tensor_tensor(key[:], score[:], first[:], ALU.mult))
                    seq(dve.tensor_reduce(top[:], key[:], AXIS.X, ALU.add))
                    seq(dve.tensor_tensor(key[:], score[:], second[:], ALU.mult))
                    seq(dve.tensor_reduce(top2[:], key[:], AXIS.X, ALU.add))
                    seq(dve.tensor_tensor(first[:], first[:], second[:], ALU.add))
                    seq(dve.tensor_tensor(top[:], top[:], top2[:], ALU.max))
                    dve.tensor_tensor(key[:], score[:], bc(top), ALU.subtract).then_inc(S["exp_in"], 1)
                    dve.wait_ge(S["exp_out"], 2)
                else:
                    dve.tensor_tensor(key[:], logit[:], bc(top), ALU.subtract).then_inc(S["exp_in"], 1)
                    dve.wait_ge(S["exp_out"], 1)
                    seq(dve.tensor_reduce(rec[:], score[:], AXIS.X, ALU.add))
                    seq(dve.reciprocal(rec[:], rec[:]))
                    seq(dve.tensor_tensor(score[:], score[:], bc(rec), ALU.mult))
                    seq(dve.tensor_tensor(first[:], first[:], second[:], ALU.add))
                seq(dve.tensor_tensor(combine[:], score[:], first[:], ALU.mult))
                seq(dve.tensor_reduce(rec[:], combine[:], AXIS.X, ALU.add))
                if spec["kind"] == "softmax":
                    seq(dve.tensor_scalar(rec[:], rec[:], 1e-8, None, ALU.add))
                seq(dve.reciprocal(rec[:], rec[:]))
                dve.tensor_tensor(combine[:], combine[:], bc(rec), ALU.mult)

            @block.gpsimd
            def _(pool):
                def step(i, k):
                    s = 2 * i + k
                    pool.wait_ge(S["xn_ready"], s + 1)
                    pool.tensor_tensor(g.X[:, s, :], g.X[:, s, :], xn[k][:], ALU.add).then_inc(S["xn_added"], 1)
                if spec["plus_xn"]:
                    skewed(pool, TILES, 0, step)

            @block.scalar
            def _(act):
                def step(i, k):
                    s = 2 * i + k
                    act.wait_ge(S["xnT_in_psum"], s + 1)
                    need(act, S["logits_in_psum"], s - 1)
                    nc.scalar.activation(xnT[k][:], bank_x[k][:, 0:P], ACT.Copy).then_inc(S["xnT_ready"], 1)
                    nc.scalar.activation(xnT_all[:, bass.ds(s * P, P)], bank_x[k][:, 0:P], ACT.Copy)\
                        .then_inc(S["kept"], 1)
                skewed(act, TILES, 0, step)
                for n in range(2 if spec["kind"] == "sigmoid" else 1):
                    act.wait_ge(S["exp_in"], n + 1)
                    scale = -1.0 if spec["kind"] == "sigmoid" and n == 0 else 1.0
                    nc.scalar.activation(score[:], key[:], ACT.Exp, scale=scale).then_inc(S["exp_out"], 1)

            @block.tensor
            def _(pe):
                pe.wait_ge(S["loaded"], 48)

                def step(i, k):
                    s = 2 * i + k
                    if live(s, TILES):
                        pe.wait_ge(S["xn_ready"], s + 1)
                        need(pe, S["kept"], s - 1)
                        pe.transpose(bank_x[k][:, 0:P], xn[k][:], g.ident[:]).then_inc(S["xnT_in_psum"], 1)
                    m, b = s - 1, (k - 1) % 2
                    if live(m, TILES):
                        pe.wait_ge(S["xnT_ready"], m + 1)
                        need(pe, S["logit_saved"], m - 1)
                        pe.matmul(bank_l[:, b, 0:EXPERTS], xnT[b][:], gate_w[:], start=True, stop=True)\
                            .then_inc(S["logits_in_psum"], 1)
                skewed(pe, TILES, 1, step, peeled=2)
    return combine


def ffn_phase(g, name, spec):
    nc, dram = g.nc, g.dram
    with ExitStack() as ctx:
        xnT_all = g.sbuf(f"{name}_xnT_all", [D, TOKENS], ctx=ctx)
        combine = route(g, name, ctx, spec, xnT_all)
        shared, GT = spec["shared"], 512
        E = shared + EXPERTS
        w_up = g.sbuf(f"{name}_w_up", [D, E, FFN], ctx=ctx)
        w_down = g.sbuf(f"{name}_w_down", [P, E, FT, D], ctx=ctx)
        hidden = [g.sbuf(f"{name}_hidden{k}", [P, FT, GT], ctx=ctx) for k in range(2)]
        biased = spec["b_up"] is not None
        if biased:
            b_up, b_down = g.sbuf(f"{name}_b_up", [P, E, FT], ctx=ctx), g.sbuf(f"{name}_b_down", [EXPERTS, D], ctx=ctx)
            combT = [g.sbuf(f"{name}_combT{k}", [EXPERTS, P], ctx=ctx) for k in range(2)]
        bank_h = [ctx.enter_context(nc.psum_tensor(f"{name}_hidden_psum{k}", [P, GT], F32)) for k in range(4)]
        bank_y = [ctx.enter_context(nc.psum_tensor(f"{name}_y_psum{k}", [P, 4, D], F32)) for k in range(2)]
        bank_c = ctx.enter_context(nc.psum_tensor(f"{name}_comb_psum", [P, 512], F32))
        bank_b = ctx.enter_context(nc.psum_tensor(f"{name}_bias_psum", [P, 512], F32))
        names = ("loaded", "up_done", "hidden_ready", "y_in_psum", "y_added", "combT_in_psum", "combT_ready",
                 "bias_in_psum", "bias_done")
        S = {k: g.sem(f"{name}_{k}") for k in names}
        groups, tiles = TOKENS // GT, GT // P
        n_loads = 2 + 2 * biased
        with nc.Block() as block:

            @block.sync
            def _(sp):
                sp.dma_start(w_up[:], dram[spec["w_up"]]).then_inc(S["loaded"], 16)
                sp.dma_start(w_down[:], dram[spec["w_down"]]).then_inc(S["loaded"], 16)
                if biased:
                    sp.dma_start(b_up[:], dram[spec["b_up"]]).then_inc(S["loaded"], 16)
                    sp.dma_start(b_down[:], dram[spec["b_down"]]).then_inc(S["loaded"], 16)

            @block.tensor
            def _(pe):
                pe.wait_ge(S["loaded"], 16 * n_loads)
                if biased:
                    for s in range(TILES):
                        need(pe, S["combT_ready"], s)
                        pe.transpose(bank_c[0:EXPERTS, 0:P], combine[:, s, :], g.ident[:])\
                            .then_inc(S["combT_in_psum"], 1)
                        pe.wait_ge(S["combT_ready"], s + 1)
                        need(pe, S["bias_done"], s)
                        pe.matmul(bank_b[:, 0:D], combT[s % 2][:], b_down[:], start=True, stop=True)\
                            .then_inc(S["bias_in_psum"], 1)

                def group(grp):
                    def up(e):
                        for j in range(FT):
                            n = FT * (E * grp + e) + j
                            need(pe, S["hidden_ready"], n - 3)
                            pe.matmul(bank_h[j][:], w_up[:, e, j * P:(j + 1) * P], xnT_all[:, bass.ds(grp * GT, GT)],
                                      start=True, stop=True).then_inc(S["up_done"], 1)

                    def down(e):
                        count = E * grp + e
                        pe.wait_ge(S["hidden_ready"], FT * count + FT)
                        need(pe, S["y_added"], count - 1)
                        for t in range(tiles):
                            for j in range(FT):
                                last = pe.matmul(bank_y[e % 2][:, t, :], hidden[e % 2][:, j, t * P:(t + 1) * P],
                                                 w_down[:, e, j, :], start=(j == 0), stop=(j == FT - 1))
                        last.then_inc(S["y_in_psum"], 1)
                    up(0)
                    for e in range(1, E):
                        up(e)
                        down(e - 1)
                    down(E - 1)
                group(0)
                with pe.Fori(1, groups) as grp:
                    group(grp)

            @block.scalar
            def _(act):
                if biased:
                    act.wait_ge(S["loaded"], 16 * n_loads)
                    for s in range(TILES):
                        act.wait_ge(S["combT_in_psum"], s + 1)
                        need(act, S["bias_in_psum"], s - 1)
                        nc.scalar.activation(combT[s % 2][:], bank_c[0:EXPERTS, 0:P], ACT.Copy)\
                            .then_inc(S["combT_ready"], 1)

                def group(grp):
                    for e in range(E):
                        for j in range(FT):
                            n = FT * (E * grp + e) + j
                            act.wait_ge(S["up_done"], n + 1)
                            need(act, S["y_in_psum"], E * grp + e - 1)
                            bias = {"bias": b_up[:, e, j:j + 1]} if biased else {}
                            nc.scalar.activation(hidden[e % 2][:, j, :], bank_h[j][:], spec["gelu"], **bias)\
                                .then_inc(S["hidden_ready"], 1)
                group(0)
                with act.Fori(1, groups) as grp:
                    group(grp)

            @block.vector
            def _(dve):
                if biased:
                    for s in range(TILES):
                        dve.wait_ge(S["bias_in_psum"], s + 1)
                        dve.tensor_tensor(g.X[:, s, :], bank_b[:, 0:D], g.X[:, s, :], ALU.add)\
                            .then_inc(S["bias_done"], 1)
                    dve.wait_ge(S["bias_done"], TILES)

                def group(grp):
                    for e in range(E):
                        count = E * grp + e
                        dve.wait_ge(S["y_in_psum"], count + 1)
                        need(dve, S["y_added"], count)
                        for t in range(tiles):
                            x = g.X[:, tiles * grp + t, :]
                            if e < shared:
                                last = dve.tensor_tensor(x, bank_y[e % 2][:, t, :], x, ALU.add)
                            else:
                                w = combine[:, tiles * grp + t, e - shared:e - shared + 1]
                                last = dve.scalar_tensor_tensor(out=x, in0=bank_y[e % 2][:, t, :], scalar=w, in1=x,
                                                                op0=ALU.mult, op1=ALU.add)
                        last.then_inc(S["y_added"], 1)
                    dve.wait_ge(S["y_added"], E * grp + E)
                    for t in range(tiles):
                        dve.bn_stats(g.stats[:, tiles * grp + t, :], g.X[:, tiles * grp + t, :])
                group(0)
                with dve.Fori(1, groups) as grp:
                    group(grp)


def ffn0(g):
    ffn_phase(g, "f0", dict(kind="sigmoid", plus_xn=True, shared=2, gelu=ACT.Gelu, gate_w="f0_gate_w",
                            gate_b="L0_ffn_routing_bias", w_up="f0_up", w_down="f0_down", b_up=None))


def ffn1(g):
    ffn_phase(g, "f1", dict(kind="softmax", plus_xn=False, shared=0, gelu=ACT.Gelu_apprx_tanh,
                            gate_w="L1_ffn_Wg", gate_b="L1_ffn_bg", w_up="f1_up", w_down="f1_down",
                            b_up="f1_b_up", b_down="L1_ffn_b2"))


def xattn0(g):
    attention(g, "a0", False)


def xattn1(g):
    attention(g, "a1", True)


PHASES = (ssm_phase, xattn0, ffn0, retention_phase, xattn1, ffn1)


def launch_inputs(inputs):
    a = {k: np.ascontiguousarray(v) for k, v in inputs.items()}
    flip = lambda m: np.ascontiguousarray(m.T)
    out = {
        "x": a["x"].reshape(TOKENS, D),
        "ident": np.eye(P, dtype=np.float32),
        "time_row": np.tile(np.arange(SEQ, dtype=np.float32), (P, 1)),
        "ssm_b_re_im": flip(np.concatenate([a["L0_attn_B_real"], a["L0_attn_B_imag"]])),
        "ssm_b_im_re": flip(np.concatenate([a["L0_attn_B_imag"], a["L0_attn_B_real"]])),
        "ssm_c_re_im": np.concatenate([a["L0_attn_C_real"], a["L0_attn_C_imag"]], axis=1),
        "ssm_c_im_re": np.concatenate([a["L0_attn_C_imag"], a["L0_attn_C_real"]], axis=1),
        "ssm_w_out": flip(a["L0_attn_W_out"]),
        "L0_attn_log_Lam_real": a["L0_attn_log_Lam_real"].reshape(-1, 1),
        "L0_attn_Lam_imag": a["L0_attn_Lam_imag"].reshape(-1, 1),
        "L0_attn_log_dt": a["L0_attn_log_dt"].reshape(1, 1),
        "L0_attn_D": a["L0_attn_D"].reshape(-1, 1),
        "L0_attn_b_out": a["L0_attn_b_out"].reshape(1, -1),
        "ctxT": flip(a["ctx_1024"].reshape(TOKENS, D)).reshape(D, BATCH, SEQ),
        "ctx": a["ctx_1024"],
        "xa_wq": flip(a["L1_xattn_wq"]), "xa_wk": flip(a["L1_xattn_wk"]), "xa_wv": flip(a["L1_xattn_wv"]),
        "L1_xattn_bq": a["L1_xattn_bq"].reshape(-1, 1),
        "L1_xattn_bk": a["L1_xattn_bk"].reshape(-1, 1),
        "L1_xattn_bv": a["L1_xattn_bv"].reshape(1, -1),
        "rank": np.tile(np.arange(EXPERTS, 0, -1, dtype=np.float32), (P, 1)),
        "f0_gate_w": flip(a["L0_ffn_centroids"]),
        "L0_ffn_routing_bias": a["L0_ffn_routing_bias"].reshape(1, -1),
        "f0_up": np.concatenate([a["L0_ffn_Wfc_sh"], a["L0_ffn_Wfc_r"]]).transpose(2, 0, 1),
        "f0_down": np.concatenate([a["L0_ffn_Wproj_sh"], a["L0_ffn_Wproj_r"]])
        .reshape(-1, D, FT, P).transpose(3, 0, 2, 1),
        "L1_ffn_Wg": a["L1_ffn_Wg"], "L1_ffn_bg": a["L1_ffn_bg"].reshape(1, -1),
        "f1_up": a["L1_ffn_W1"].transpose(1, 0, 2),
        "f1_down": a["L1_ffn_W2"].reshape(EXPERTS, FT, P, D).transpose(2, 0, 1, 3),
        "f1_b_up": a["L1_ffn_b1"].reshape(EXPERTS, FT, P).transpose(2, 0, 1), "L1_ffn_b2": a["L1_ffn_b2"],
        "ret_wqk": flip(np.concatenate([a["L1_attn_Wq"], a["L1_attn_Wk"]])),
        "ret_wv": flip(a["L1_attn_Wv"]).reshape(D, R_HEADS, R_VAL),
        "ret_wg": flip(a["L1_attn_Wg"]),
        "ret_wo": np.ascontiguousarray(a["L1_attn_Wo"].reshape(D, R_HEADS, R_VAL).transpose(2, 1, 0)),
        "ret_gn_w": flip(a["L1_attn_gn_weight"].reshape(R_HEADS, R_VAL)),
        "ret_gn_b": flip(a["L1_attn_gn_bias"].reshape(R_HEADS, R_VAL)),
    }
    out["ret_cos"], out["ret_sin"], out["ret_decay"] = retention_tables()
    return {k: np.ascontiguousarray(v) for k, v in out.items()}


def build(nc, dram, out):
    with ExitStack() as ctx:
        g = Program(nc, ctx, dram)
        for phase in PHASES:
            g.run(phase)
        stored = ctx.enter_context(nc.semaphore("stored"))
        with nc.Block() as block:

            @block.sync
            def _(sp):
                for i in range(4):
                    sp.dma_start(out.rearrange("(i p) d -> p i d", p=P)[:, 8 * i:8 * i + 8, :],
                                 g.X[:, 8 * i:8 * i + 8, :]).then_inc(stored, 16)
                sp.wait_ge(stored, 64)


def kernel(**inputs):
    import concourse.bacc as bacc
    from concourse.bass_utils import run_bass_kernel_spmd

    nc = bacc.Bacc("TRN2", target_bir_lowering=False, num_devices=1)
    arrays = launch_inputs(inputs)
    dram = {k: nc.dram_tensor(f"in_{k}", a.shape, mybir.dt.from_np(a.dtype), kind="ExternalInput").ap()
            for k, a in arrays.items()}
    out = nc.dram_tensor("out", (TOKENS, D), F32, kind="ExternalOutput").ap()
    build(nc, dram, out)
    result = run_bass_kernel_spmd(nc, [{f"in_{k}": a for k, a in arrays.items()}], core_ids=[0])
    return result.results[0]["out"].reshape(BATCH, SEQ, D)
```

```python
from contextlib import ExitStack
import math

import numpy as np
import concourse.bass as bass
from concourse import mybir

F32 = mybir.dt.float32
I32 = mybir.dt.int32
ACT = mybir.ActivationFunctionType
ALU = mybir.AluOpType
AXIS = mybir.AxisListType

P = 128
D = 128
BATCH, SEQ = 64, 64
TOKENS = BATCH * SEQ
TILES = TOKENS // P
EPS = 1e-5


def need(eng, sem, value):
    if isinstance(value, int) and value <= 0:
        return
    eng.wait_ge(sem, value)


def skewed(eng, items, depth, step, unroll=2, peeled=1):
    for s in range(peeled * unroll):
        step(s // unroll, s % unroll)
    with eng.Fori(peeled, items // unroll) as i:
        for k in range(unroll):
            step(i, k)
    for s in range(items, items + depth):
        step(s // unroll, s % unroll)


def live(m, items):
    return not isinstance(m, int) or 0 <= m < items


class Program:

    def __init__(self, nc, ctx, dram):
        self.nc, self.ctx, self.dram = nc, ctx, dram
        self.phase_ctx, self.phase_sems = None, []
        self.indirect_done = [ctx.enter_context(nc.semaphore(f"indirect_done{k}")) for k in range(2)]
        self.indirect_uses = 0
        self.X = self.sbuf("X", [P, TILES, D])
        self.stats = self.sbuf("stats", [P, TILES, 6])
        self.mean = self.sbuf("mean", [P, TILES])
        self.rstd = self.sbuf("rstd", [P, TILES])
        self.ident = self.sbuf("ident", [P, P])
        self.slots_x = nc.dram_tensor("slots_x", (SLOTS, D), F32, kind="Internal").ap()
        self.slots_y = nc.dram_tensor("slots_y", (SLOTS, D), F32, kind="Internal").ap()

    def sem(self, name):
        handle = self.phase_ctx.enter_context(self.nc.semaphore(name))
        self.phase_sems.append(handle.num)
        return handle

    def indirect_transfers(self):
        self.indirect_uses += 1
        return self.indirect_done, (self.indirect_uses - 1) * 16 * TOP_K * TILES // 2

    def run(self, phase):
        self.phase_sems = []
        with ExitStack() as self.phase_ctx:
            phase(self)
        numbers = sorted(self.phase_sems)
        starts = [n for n in numbers if n - 1 not in numbers]
        ends = [n + 1 for n in numbers if n + 1 not in numbers]
        with self.nc.Block() as block:

            @block.sync
            def _(sp):
                for low, high in zip(starts, ends):
                    sp.sem_clear(range(low, high))

    def sbuf(self, name, shape, dt=F32, ctx=None):
        return (ctx or self.ctx).enter_context(self.nc.sbuf_tensor(name, shape, dt))

    def banks(self, name, ctx):
        return [ctx.enter_context(self.nc.psum_tensor(f"{name}_bank{b}", [P, 512], F32)) for b in range(8)]


def row_statistics(g, name):
    nc = g.nc
    with ExitStack() as ctx:
        diff = g.sbuf(f"{name}_ln_diff", [P, TILES], ctx=ctx)
        var = g.sbuf(f"{name}_ln_var", [P, TILES], ctx=ctx)
        minus_half = g.sbuf(f"{name}_ln_minus_half", [P, TILES], ctx=ctx)
        step = g.sem(f"{name}_ln_stat_step")
        var_ready = g.sem(f"{name}_ln_var_ready")
        filled = g.sem(f"{name}_ln_minus_half_filled")
        rstd_ready = g.sem(f"{name}_ln_rstd_ready")
        st = g.stats
        with nc.Block() as block:

            @block.vector
            def _(dve):
                dve.tensor_tensor(g.mean[:], st[:, :, 1], st[:, :, 4], ALU.add)
                dve.tensor_tensor(diff[:], st[:, :, 1], st[:, :, 4], ALU.subtract)
                dve.tensor_tensor(var[:], st[:, :, 2], st[:, :, 5], ALU.add).then_inc(step, 1)
                dve.wait_ge(step, 1)
                dve.tensor_scalar(g.mean[:], g.mean[:], 0.5, None, ALU.mult)
                dve.tensor_tensor(diff[:], diff[:], diff[:], ALU.mult)
                dve.tensor_scalar(var[:], var[:], 1.0 / D, EPS, ALU.mult, ALU.add).then_inc(step, 1)
                dve.wait_ge(step, 2)
                dve.scalar_tensor_tensor(out=var[:], in0=diff[:], scalar=0.25, in1=var[:],
                                         op0=ALU.mult, op1=ALU.add).then_inc(var_ready, 1)

            @block.gpsimd
            def _(pool):
                pool.memset(minus_half[:], -0.5).then_inc(filled, 1)
                pool.wait_ge(filled, 1)
                pool.wait_ge(var_ready, 1)
                pool.tensor_tensor(g.rstd[:], var[:], minus_half[:], ALU.pow).then_inc(rstd_ready, 1)


GROUP = 4
GROUPS = TILES // GROUP
GT = GROUP * P
STATES = 64
TWO_PI_HI = 201.0 / 32.0
TWO_PI_LO = 2.0 * math.pi - TWO_PI_HI
TWO_PI_MID = float(np.float32(round(TWO_PI_LO * 2**21) / 2**21))
TWO_PI_END = TWO_PI_LO - TWO_PI_MID
ROUND_1 = 1.5 * 2**23
LN2_HI = 0.693359375
LN2_LO = math.log(2.0) - LN2_HI


def ssm_tables(g, t):
    nc, dram = g.nc, g.dram
    with ExitStack() as ctx:
        def sb(name, shape, dt=F32):
            return g.sbuf(f"ssm_{name}", shape, dt, ctx)

        log_lam, lam_im, log_dt = sb("log_lam", [P, 1]), sb("lam_im", [P, 1]), sb("log_dt", [P, 1])
        b_re_im, b_im_re = sb("b_re_im", [D, P]), sb("b_im_re", [D, P])
        c_re_im, c_im_re = sb("c_re_im", [D, P]), sb("c_im_re", [D, P])
        w_out, d_col = sb("w_out", [D, D]), sb("d_col", [D, 1])
        time_row = sb("time_row", [P, SEQ])
        dt, n, r, poly = sb("dt", [P, 1]), sb("n", [P, 1]), sb("r", [P, 1]), sb("poly", [P, 1])
        n_int = sb("n_int", [P, 1], I32)
        lam, mag = sb("lam", [P, 1]), sb("mag", [P, 1])
        theta, theta_hi, theta_lo = sb("theta", [P, 1]), sb("theta_hi", [P, 1]), sb("theta_lo", [P, 1])
        turn, ang, ang_lo, ang_cos = (sb(k, [P, SEQ]) for k in ("turn", "ang", "ang_lo", "ang_cos"))
        folded = [ctx.enter_context(nc.psum_tensor(f"ssm_folded{i}", [P, 512], F32)) for i in range(2)]
        loaded = g.sem("ssm_parameters_loaded")
        step = g.sem("ssm_table_step")
        lam_ready, arg_ready, mag_ready = g.sem("ssm_lam_ready"), g.sem("ssm_arg_ready"), g.sem("ssm_mag_ready")
        ang_ready, sin_ready = g.sem("ssm_angles_ready"), g.sem("ssm_sines_ready")
        c_ready, fold_done = g.sem("ssm_c_ready"), g.sem("ssm_fold_done")
        with nc.Block() as block:

            @block.sync
            def _(sp):
                for i in range(4):
                    sp.dma_start(g.X[:, 8 * i:8 * i + 8, :],
                                 dram["x"].rearrange("(i p) d -> p i d", p=P)[:, 8 * i:8 * i + 8, :])\
                        .then_inc(t["x_loaded"][i], 16)

            @block.scalar
            def _(act):
                loads = [
                    (log_lam[0:STATES, :], dram["L0_attn_log_Lam_real"]),
                    (log_lam[STATES:P, :], dram["L0_attn_log_Lam_real"]),
                    (lam_im[0:STATES, :], dram["L0_attn_Lam_imag"]),
                    (lam_im[STATES:P, :], dram["L0_attn_Lam_imag"]),
                    (log_dt[:], dram["L0_attn_log_dt"].to_broadcast([P, 1])),
                    (b_re_im[:], dram["ssm_b_re_im"]), (b_im_re[:], dram["ssm_b_im_re"]),
                    (c_re_im[:], dram["ssm_c_re_im"]), (c_im_re[:], dram["ssm_c_im_re"]),
                    (w_out[:], dram["ssm_w_out"]), (d_col[:], dram["L0_attn_D"]),
                    (time_row[:], dram["time_row"]), (g.ident[:], dram["ident"]),
                    (t["b_out"][:], dram["L0_attn_b_out"].to_broadcast([P, D])),
                ]
                for dst, src in loads:
                    act.dma_start(dst, src).then_inc(loaded, 16)
                act.wait_ge(loaded, 16 * 14)
                nc.scalar.activation(lam[:], log_lam[:], ACT.Exp).then_inc(lam_ready, 1)
                act.wait_ge(arg_ready, 1)
                nc.scalar.activation(mag[:], lam[:], ACT.Exp, scale=-1.0).then_inc(mag_ready, 1)
                act.wait_ge(ang_ready, 1)
                nc.scalar.activation(t["sin"][:], ang[:], ACT.Sin)
                nc.scalar.activation(t["cos"][:], ang_cos[:], ACT.Sin).then_inc(sin_ready, 1)

            @block.vector
            def _(dve):
                done = [0]

                def seq(ins):
                    done[0] += 1
                    ins.then_inc(step, 1)
                    dve.wait_ge(step, done[0])

                dve.wait_ge(loaded, 16 * 14)
                seq(dve.tensor_scalar(n[:], log_dt[:], 1.0 / math.log(2.0), ROUND_1, ALU.mult, ALU.add))
                seq(dve.tensor_scalar(n[:], n[:], ROUND_1, None, ALU.subtract))
                seq(dve.tensor_scalar(n[:], n[:], -126.0, 127.0, ALU.max, ALU.min))
                seq(dve.scalar_tensor_tensor(out=r[:], in0=n[:], scalar=-LN2_HI, in1=log_dt[:],
                                             op0=ALU.mult, op1=ALU.add))
                seq(dve.scalar_tensor_tensor(out=r[:], in0=n[:], scalar=-LN2_LO, in1=r[:],
                                             op0=ALU.mult, op1=ALU.add))
                seq(dve.tensor_scalar(poly[:], r[:], 1.0 / math.factorial(8), 1.0 / math.factorial(7),
                                      ALU.mult, ALU.add))
                for k in range(6, -1, -1):
                    seq(dve.tensor_scalar(poly[:], poly[:], r[:], 1.0 / math.factorial(k), ALU.mult, ALU.add))
                seq(dve.tensor_scalar(n[:], n[:], 127.0, 2.0**23, ALU.add, ALU.mult))
                seq(dve.tensor_copy(n_int[:], n[:]))
                seq(dve.tensor_tensor(dt[:], poly[:], n_int[:].bitcast(F32), ALU.mult))
                seq(dve.tensor_tensor(theta[:], lam_im[:], dt[:], ALU.mult))
                seq(dve.tensor_scalar(n[:], theta[:], 1.0 / (2 * math.pi), ROUND_1, ALU.mult, ALU.add))
                seq(dve.tensor_scalar(n[:], n[:], ROUND_1, None, ALU.subtract))
                for part in (TWO_PI_HI, TWO_PI_MID, TWO_PI_END):
                    seq(dve.scalar_tensor_tensor(out=theta[:], in0=n[:], scalar=-part, in1=theta[:],
                                                 op0=ALU.mult, op1=ALU.add))
                seq(dve.tensor_scalar(theta_hi[:], theta[:], 1.5 * 2**13, 1.5 * 2**13, ALU.add, ALU.subtract))
                seq(dve.tensor_tensor(theta_lo[:], theta[:], theta_hi[:], ALU.subtract))
                seq(dve.tensor_scalar(turn[:], time_row[:], theta[:], 1.0 / (2 * math.pi), ALU.mult, ALU.mult))
                seq(dve.tensor_scalar(turn[:], turn[:], ROUND_1, ROUND_1, ALU.add, ALU.subtract))
                seq(dve.tensor_scalar(ang[:], time_row[:], theta_hi[:], None, ALU.mult))
                seq(dve.tensor_scalar(ang_lo[:], time_row[:], theta_lo[:], None, ALU.mult))
                seq(dve.scalar_tensor_tensor(out=ang[:], in0=turn[:], scalar=-TWO_PI_HI, in1=ang[:],
                                             op0=ALU.mult, op1=ALU.add))
                seq(dve.scalar_tensor_tensor(out=ang[:], in0=turn[:], scalar=-TWO_PI_LO, in1=ang[:],
                                             op0=ALU.mult, op1=ALU.add))
                seq(dve.tensor_tensor(ang[:], ang[:], ang_lo[:], ALU.add))
                seq(dve.tensor_scalar(ang_cos[:], ang[:], math.pi / 2, -2 * math.pi, ALU.is_gt, ALU.mult))
                seq(dve.scalar_tensor_tensor(out=ang_cos[:], in0=ang[:], scalar=math.pi / 2, in1=ang_cos[:],
                                             op0=ALU.add, op1=ALU.add))
                top = 3.1415925
                seq(dve.tensor_scalar(ang[:], ang[:], -top, top, ALU.max, ALU.min))
                seq(dve.tensor_scalar(ang_cos[:], ang_cos[:], -top, top, ALU.max, ALU.min))
                dve.tensor_copy(turn[:], turn[:]).then_inc(ang_ready, 1)
                seq(dve.tensor_scalar(t["u_cos"][:], b_re_im[:], dt[:], None, ALU.mult))
                seq(dve.tensor_scalar(t["u_sin"][:], b_im_re[:], dt[:], None, ALU.mult))
                seq(dve.tensor_scalar(c_re_im[:, STATES:P], c_re_im[:, STATES:P], -1.0, None, ALU.mult))
                dve.tensor_scalar(c_im_re[:, 0:STATES], c_im_re[:, 0:STATES], -1.0, None, ALU.mult)\
                    .then_inc(c_ready, 1)
                seq(dve.tensor_scalar(t["w_skip"][:], w_out[:], d_col[:], None, ALU.mult))
                dve.wait_ge(fold_done, 1)
                dve.tensor_copy(t["w_cos"][:], folded[0][:, 0:D])
                seq(dve.tensor_copy(t["w_sin"][:], folded[1][:, 0:D]))
                dve.wait_ge(lam_ready, 1)
                dve.tensor_tensor(lam[:], lam[:], dt[:], ALU.mult).then_inc(arg_ready, 1)
                seq(dve.memset(t["decay"][:], 0.0))
                dve.wait_ge(mag_ready, 1)
                dve.tensor_scalar(t["decay"][:, :, 1:SEQ], t["decay"][:, :, 1:SEQ], mag[:], None, ALU.add)
                dve.wait_ge(sin_ready, 1)
                seq(dve.tensor_scalar(t["sin"][STATES:P, :], t["sin"][STATES:P, :], -1.0, None, ALU.mult))
                for i in range(TILES):
                    if i % 8 == 0:
                        dve.wait_ge(t["x_loaded"][i // 8], 16)
                    dve.bn_stats(g.stats[:, i, :], g.X[:, i, :])

            @block.tensor
            def _(pe):
                pe.wait_ge(loaded, 16 * 14)
                pe.wait_ge(c_ready, 1)
                pe.matmul(folded[0][:, 0:D], c_re_im[:], w_out[:], start=True, stop=True)
                pe.matmul(folded[1][:, 0:D], c_im_re[:], w_out[:], start=True, stop=True).then_inc(fold_done, 1)


def ssm_phase(g):
    nc = g.nc
    with ExitStack() as ctx:
        def sb(name, shape):
            return g.sbuf(f"ssm_{name}", shape, ctx=ctx)

        t = {"x_loaded": [g.sem(f"x_loaded{i}") for i in range(4)]}
        for name, shape in (("cos", [P, SEQ]), ("sin", [P, SEQ]), ("decay", [P, GT // SEQ, SEQ]),
                            ("u_cos", [D, P]), ("u_sin", [D, P]), ("w_cos", [P, D]), ("w_sin", [P, D]),
                            ("w_skip", [D, D]), ("b_out", [P, D])):
            t[name] = sb(name, shape)
        ssm_tables(g, t)
        row_statistics(g, "ssm")
        xn = [sb(f"xn{k}", [P, GROUP, D]) for k in range(2)]
        xnT = [sb(f"xnT{k}", [D, GT]) for k in range(3)]
        part_cos = [sb(f"part_cos{k}", [P, GT]) for k in range(2)]
        part_sin = [sb(f"part_sin{k}", [P, GT]) for k in range(2)]
        z = [sb(f"z{k}", [P, GT]) for k in range(2)]
        z_cos = [sb(f"z_cos{k}", [P, GT]) for k in range(2)]
        z_sin = [sb(f"z_sin{k}", [P, GT]) for k in range(2)]
        banks = g.banks("ssm", ctx)
        bank_t, bank_uc, bank_us, bank_o = banks[0:2], banks[2:4], banks[4:6], banks[6:8]
        names = ("xn_ready", "xnT_in_psum", "xnT_ready", "inputs_in_psum", "parts_ready", "drive_ready",
                 "z_ready", "z_cos_ready", "z_sin_ready", "out_in_psum", "bias_added", "x_updated")
        S = {k: g.sem(f"ssm_{k}") for k in names}
        batch = lambda ap: ap.rearrange("p (b t) -> p b t", t=SEQ)
        over = lambda ap: ap.unsqueeze(1).to_broadcast([P, GT // SEQ, SEQ])
        N = GROUPS
        with nc.Block() as block:

            @block.vector
            def _(dve):
                for s in range(N + 2):
                    if s < N:
                        need(dve, S["xnT_in_psum"], s - 1)
                        for j in range(GROUP):
                            i = GROUP * s + j
                            last = dve.tensor_scalar(xn[s % 2][:, j, :], g.X[:, i, :], g.mean[:, i:i + 1],
                                                     g.rstd[:, i:i + 1], ALU.subtract, ALU.mult)
                        last.then_inc(S["xn_ready"], 1)
                    m = s - 1
                    if 0 <= m < N:
                        dve.wait_ge(S["drive_ready"], m + 1)
                        need(dve, S["z_sin_ready"], m - 1)
                        dve.tensor_tensor_scan(z[m % 2][:], t["decay"][:].rearrange("p b t -> p (b t)"),
                                               part_cos[m % 2][:], 0.0, ALU.mult, ALU.add)\
                            .then_inc(S["z_ready"], 1)
                        dve.wait_ge(S["z_ready"], m + 1)
                        need(dve, S["out_in_psum"], m - 1)
                        dve.tensor_tensor(batch(z_cos[m % 2][:]), batch(z[m % 2][:]), over(t["cos"][:]),
                                          ALU.mult).then_inc(S["z_cos_ready"], 1)
                    if s < N:
                        dve.wait_ge(S["inputs_in_psum"], s + 1)
                        need(dve, S["z_ready"], s - 1)
                        dve.tensor_tensor(batch(part_cos[s % 2][:]), batch(bank_uc[s % 2][:]), over(t["cos"][:]),
                                          ALU.mult)
                        dve.tensor_tensor(batch(part_sin[s % 2][:]), batch(bank_us[s % 2][:]), over(t["sin"][:]),
                                          ALU.mult).then_inc(S["parts_ready"], 1)
                    m = s - 2
                    if 0 <= m < N:
                        dve.wait_ge(S["out_in_psum"], m + 1)
                        dve.wait_ge(S["bias_added"], m + 1)
                        tiles = g.X[:, GROUP * m:GROUP * m + GROUP, :]
                        dve.tensor_tensor(tiles, bank_o[m % 2][:].rearrange("p (j d) -> p j d", d=D), tiles,
                                          ALU.add).then_inc(S["x_updated"], 1)
                        dve.wait_ge(S["x_updated"], m + 1)
                        for i in range(GROUP * m, GROUP * m + GROUP):
                            dve.bn_stats(g.stats[:, i, :], g.X[:, i, :])

            @block.gpsimd
            def _(pool):
                for s in range(N + 1):
                    if s < N:
                        pool.wait_ge(S["parts_ready"], s + 1)
                        pool.tensor_tensor(part_cos[s % 2][:], part_cos[s % 2][:], part_sin[s % 2][:], ALU.add)\
                            .then_inc(S["drive_ready"], 1)
                        tiles = g.X[:, GROUP * s:GROUP * s + GROUP, :]
                        pool.tensor_tensor(tiles, tiles, t["b_out"][:].unsqueeze(1).to_broadcast([P, GROUP, D]),
                                           ALU.add).then_inc(S["bias_added"], 1)
                    m = s - 1
                    if 0 <= m < N:
                        pool.wait_ge(S["z_ready"], m + 1)
                        need(pool, S["out_in_psum"], m - 1)
                        pool.tensor_tensor(batch(z_sin[m % 2][:]), batch(z[m % 2][:]), over(t["sin"][:]),
                                           ALU.mult).then_inc(S["z_sin_ready"], 1)

            @block.scalar
            def _(act):
                for s in range(N):
                    act.wait_ge(S["xnT_in_psum"], s + 1)
                    need(act, S["out_in_psum"], s - 2)
                    nc.scalar.activation(xnT[s % 3][:], bank_t[s % 2][:], ACT.Copy).then_inc(S["xnT_ready"], 1)

            @block.tensor
            def _(pe):
                for s in range(N + 2):
                    if s < N:
                        pe.wait_ge(S["xn_ready"], s + 1)
                        need(pe, S["xnT_ready"], s - 1)
                        for j in range(GROUP):
                            last = pe.transpose(bank_t[s % 2][:, j * P:(j + 1) * P], xn[s % 2][:, j, :], g.ident[:])
                        last.then_inc(S["xnT_in_psum"], 1)
                    m = s - 2
                    if 0 <= m < N:
                        pe.wait_ge(S["z_cos_ready"], m + 1)
                        pe.wait_ge(S["z_sin_ready"], m + 1)
                        need(pe, S["x_updated"], m - 1)
                        for j in range(GROUP):
                            cols = slice(j * P, (j + 1) * P)
                            out = bank_o[m % 2][:, cols]
                            pe.matmul(out, z_cos[m % 2][:, cols], t["w_cos"][:], start=True, stop=False)
                            pe.matmul(out, z_sin[m % 2][:, cols], t["w_sin"][:], start=False, stop=False)
                            last = pe.matmul(out, xnT[m % 3][:, cols], t["w_skip"][:], start=False, stop=True)
                        last.then_inc(S["out_in_psum"], 1)
                    if s < N:
                        pe.wait_ge(S["xnT_ready"], s + 1)
                        need(pe, S["parts_ready"], s - 1)
                        pe.matmul(bank_uc[s % 2][:], t["u_cos"][:], xnT[s % 3][:], start=True, stop=True)
                        pe.matmul(bank_us[s % 2][:], t["u_sin"][:], xnT[s % 3][:], start=True, stop=True)\
                            .then_inc(S["inputs_in_psum"], 1)


HEADS, HEAD = 16, 8
QUAD = 4
QUADS = BATCH // QUAD
QKEYS = QUAD * SEQ
OCT = 8
OCTS = BATCH // OCT
OKEYS = OCT * SEQ
OTILES = OKEYS // P


def project_context(g, kT, v_twice):
    nc, dram = g.nc, g.dram
    with ExitStack() as ctx:
        ctxT = [g.sbuf(f"kv_ctxT{k}", [D, OCT, 2, SEQ], ctx=ctx) for k in range(2)]
        wk, wv = g.sbuf("kv_wk", [D, D], ctx=ctx), g.sbuf("kv_wv", [D, D], ctx=ctx)
        bk = g.sbuf("kv_bk", [D, 1], ctx=ctx)
        banks = g.banks("kv", ctx)
        weights = g.sem("kv_weights_loaded")
        loaded = [g.sem(f"kv_context_loaded{k}") for k in range(2)]
        done, k_ready, v_ready = g.sem("kv_products_done"), g.sem("kv_k_ready"), g.sem("kv_v_ready")
        with nc.Block() as block:

            @block.sync
            def _(sp):
                for dst, src in ((wk, "xa_wk"), (wv, "xa_wv"), (bk, "L1_xattn_bk")):
                    sp.dma_start(dst[:], dram[src]).then_inc(weights, 16)

                def step(i, k):
                    s = 2 * i + k
                    need(sp, done, 2 * (s - 1))
                    for copy in range(2):
                        sp.dma_start(ctxT[k][:, :, copy, :], dram["ctxT"][:, bass.ds(s * OCT, OCT), :])\
                            .then_inc(loaded[k], 16)
                skewed(sp, OCTS, 0, step)

            @block.tensor
            def _(pe):
                pe.wait_ge(weights, 48)

                def step(i, k):
                    s = 4 * i + k
                    octet, row = k // 2, k % 2 * QUAD
                    pe.wait_ge(loaded[octet], 32 * (i + 1))
                    need(pe, k_ready, s - 1)
                    need(pe, v_ready, s - 1)
                    pe.matmul(banks[k % 2][:, 0:QKEYS], wk[:], ctxT[octet][:, row:row + QUAD, 0, :],
                              start=True, stop=True)
                    for b in range(QUAD):
                        last = pe.matmul(banks[2 + k % 2][:, b * D:(b + 1) * D], ctxT[octet][:, row + b, :, :], wv[:],
                                         start=True, stop=True)
                    last.then_inc(done, 1)
                skewed(pe, QUADS, 0, step, 4)

            @block.scalar
            def _(act):
                act.wait_ge(weights, 48)

                def step(i, k):
                    s = 2 * i + k
                    act.wait_ge(done, s + 1)
                    nc.scalar.activation(kT[:, bass.ds(s * QKEYS, QKEYS)], banks[k][:, 0:QKEYS], ACT.Identity,
                                         bias=bk[:]).then_inc(k_ready, 1)
                skewed(act, QUADS, 0, step)

            @block.vector
            def _(dve):
                def step(i, k):
                    s = 2 * i + k
                    dve.wait_ge(done, s + 1)
                    dve.tensor_copy(v_twice[:, bass.ds(s * QUAD, QUAD), :],
                                    banks[2 + k][:].rearrange("p (b d) -> p b d", d=D)).then_inc(v_ready, 1)
                skewed(dve, QUADS, 0, step)


def attention(g, name, projected):
    nc, dram = g.nc, g.dram
    row_statistics(g, name)
    with ExitStack() as ctx:
        def sb(n, shape):
            return g.sbuf(f"{name}_{n}", shape, ctx=ctx)

        if projected:
            kT, v_twice = sb("kT", [D, TOKENS]), sb("v_twice", [P, BATCH, D])
            project_context(g, kT, v_twice)
            wq, bq, bv = sb("wq", [D, D]), sb("bq", [D, 1]), sb("bv", [P, D])
            q = [sb(f"q{k}", [D, P]) for k in range(2)]
        else:
            v_rows = [sb(f"v_rows{k}", [P, OCT, D]) for k in range(2)]
        xn = [sb(f"xn{k}", [P, D]) for k in range(2)]
        xnT = [sb(f"xnT{k}", [D, P]) for k in range(2)]
        qT = q if projected else xnT
        k_diag = [sb(f"k_diag{k}", [D, HEADS, OCT, SEQ]) for k in range(2)]
        v_diag = [sb(f"v_diag{k}", [P, OCT, HEADS // 2, 2, HEAD + 1]) for k in range(2)]
        top = [sb(f"top{k}", [P, HEADS]) for k in range(2)]
        prob = [sb(f"prob{k}", [P, HEADS, SEQ]) for k in range(2)]
        probT = [sb(f"probT{k}", [P, HEADS // 2, P]) for k in range(2)]
        ones = sb("ones", [P, OCT, HEADS // 2, HEAD])
        recip = sb("recip", [P, HEADS])
        mixed = sb("mixed", [P, HEADS, HEAD])
        bank_s = [ctx.enter_context(nc.psum_tensor(f"{name}_scores{k}", [P, HEADS, SEQ], F32)) for k in range(2)]
        bank_t = ctx.enter_context(nc.psum_tensor(f"{name}_probT_psum", [P, HEADS // 2, P], F32))
        bank_o = ctx.enter_context(nc.psum_tensor(f"{name}_mixed_psum", [P, 512], F32))
        bank_x = ctx.enter_context(nc.psum_tensor(f"{name}_xT_psum", [P, 512], F32))
        names = ("weights_loaded", "first_cleared", "second_cleared", "v_cleared", "ones_set", "xn_ready", "xnT_in_psum", "xnT_ready", "q_in_psum",
                 "q_ready", "scores_in_psum", "top_ready", "shifted", "exp_ready", "probT_in_psum",
                 "probT_ready", "mixed_in_psum", "recip_ready", "mixed_ready", "x_updated", "v_diag_ready",
                 "bias_added")
        S = {k: g.sem(f"{name}_{k}") for k in names}
        k_loaded = [g.sem(f"{name}_k_loaded{k}") for k in range(2)]
        v_loaded = [g.sem(f"{name}_v_loaded{k}") for k in range(2)]
        q_ready = S["q_ready"] if projected else S["xnT_ready"]
        N, UNROLL = TILES, 2 * OTILES

        with nc.Block() as block:

            @block.sync
            def _(sp):
                if projected:
                    for dst, src in ((wq[:], dram["xa_wq"]), (bq[:], dram["L1_xattn_bq"]),
                                     (bv[:], dram["L1_xattn_bv"].to_broadcast([P, D]))):
                        sp.dma_start(dst, src).then_inc(S["weights_loaded"], 16)
                sp.wait_ge(S["first_cleared"], 1)

                def step(i, k):
                    j = 2 * i + k
                    if isinstance(j, int) and j == 1:
                        sp.wait_ge(S["second_cleared"], 1)
                    need(sp, S["scores_in_psum"], OTILES * (j - 1))
                    for h in range(HEADS):
                        rows = slice(h * HEAD, (h + 1) * HEAD)
                        if projected:
                            src = kT[rows, bass.ds(j * OKEYS, OKEYS)].rearrange("p (b t) -> p b t", t=SEQ)
                        else:
                            src = dram["ctxT"][rows, bass.ds(j * OCT, OCT), :]
                        sp.dma_start(k_diag[k][rows, h, :, :], src).then_inc(k_loaded[k], 16)
                    if not projected:
                        need(sp, S["v_diag_ready"], j - 1)
                        for half in range(2):
                            sp.dma_start(v_rows[k][half * SEQ:(half + 1) * SEQ, :, :],
                                         dram["ctx"].rearrange("b t d -> t b d")[:, bass.ds(j * OCT, OCT), :])\
                                .then_inc(v_loaded[k], 16)
                skewed(sp, OCTS, 0, step)

            @block.gpsimd
            def _(pool):
                pool.memset(k_diag[0][:], 0.0).then_inc(S["first_cleared"], 1)
                for k in range(2):
                    pool.memset(v_diag[k][:], 0.0).then_inc(S["v_cleared"], 1)
                pool.memset(ones[:], 1.0).then_inc(S["v_cleared"], 1)
                pool.wait_ge(S["v_cleared"], 3)
                for k in range(2):
                    for half in range(2):
                        pool.memset(v_diag[k][half * SEQ:(half + 1) * SEQ, :, :, half, HEAD:HEAD + 1], 1.0)\
                            .then_inc(S["ones_set"], 1)
                if projected:
                    pool.wait_ge(S["weights_loaded"], 48)

                def step(i, k):
                    j = 2 * i + k
                    need(pool, S["mixed_in_psum"], OTILES * (j - 1))
                    if not projected:
                        pool.wait_ge(v_loaded[k], 32 * (i + 1))
                    else:
                        need(pool, S["bias_added"], OTILES * j)
                    for half in range(2):
                        rows = slice(half * SEQ, (half + 1) * SEQ)
                        src = v_twice[rows, bass.ds(j * OCT, OCT), :] if projected else v_rows[k][rows, :, :]
                        src = src.rearrange("p b (h c d) -> p b h c d", c=2, d=HEAD)[:, :, :, half, :]
                        last = pool.tensor_tensor(v_diag[k][rows, :, :, half, 0:HEAD], src,
                                                  ones[rows, :, :, :], ALU.mult)
                    last.then_inc(S["v_diag_ready"], 1)
                    if projected:
                        pool.wait_ge(S["v_diag_ready"], j + 1)
                        for m in [OTILES * j + t for t in range(OTILES)]:
                            pool.wait_ge(S["xn_ready"], m + 1)
                            pool.tensor_tensor(g.X[:, m, :], g.X[:, m, :], bv[:], ALU.add)\
                                .then_inc(S["bias_added"], 1)
                skewed(pool, OCTS, 0, step)

            @block.vector
            def _(dve):
                dve.memset(k_diag[1][:], 0.0).then_inc(S["second_cleared"], 1)

                def step(i, k):
                    s = UNROLL * i + k
                    m = s - 5
                    if live(m, N):
                        dve.wait_ge(S["mixed_in_psum"], m + 1)
                        need(dve, S["mixed_ready"], m)
                        out = bank_o[:, 0:HEADS * (HEAD + 1)].rearrange("p (h c) -> p h c", c=HEAD + 1)
                        dve.reciprocal(recip[:], out[:, :, HEAD]).then_inc(S["recip_ready"], 1)
                        dve.wait_ge(S["recip_ready"], m + 1)
                        need(dve, S["x_updated"], m)
                        dve.tensor_tensor(mixed[:], out[:, :, 0:HEAD],
                                          recip[:].unsqueeze(2).to_broadcast([P, HEADS, HEAD]), ALU.mult)\
                            .then_inc(S["mixed_ready"], 1)
                        dve.wait_ge(S["mixed_ready"], m + 1)
                        if projected:
                            dve.wait_ge(S["bias_added"], m + 1)
                        dve.tensor_tensor(g.X[:, m, :], g.X[:, m, :], mixed[:].rearrange("p h c -> p (h c)"),
                                          ALU.add).then_inc(S["x_updated"], 1)
                    if live(s, N):
                        need(dve, S["xnT_in_psum"], s - 1)
                        dve.tensor_scalar(xn[k % 2][:], g.X[:, s, :], g.mean[:, bass.ds(s, 1)],
                                          g.rstd[:, bass.ds(s, 1)], ALU.subtract, ALU.mult)\
                            .then_inc(S["xn_ready"], 1)
                    m, b = s - 2, (k - 2) % 2
                    if live(m, N):
                        dve.wait_ge(S["scores_in_psum"], m + 1)
                        need(dve, S["shifted"], m - 1)
                        dve.tensor_reduce(top[b][:], bank_s[b][:], AXIS.X, ALU.max).then_inc(S["top_ready"], 1)
                        dve.wait_ge(S["top_ready"], m + 1)
                        need(dve, S["probT_in_psum"], m - 1)
                        dve.tensor_tensor(prob[b][:], bank_s[b][:],
                                          top[b][:].unsqueeze(2).to_broadcast([P, HEADS, SEQ]), ALU.subtract)\
                            .then_inc(S["shifted"], 1)
                    m = s - 5
                    if live(m, N):
                        dve.wait_ge(S["x_updated"], m + 1)
                        dve.bn_stats(g.stats[:, m, :], g.X[:, m, :])
                skewed(dve, N, 5, step, UNROLL)

            @block.scalar
            def _(act):
                if projected:
                    act.wait_ge(S["weights_loaded"], 48)

                def step(i, k):
                    s = UNROLL * i + k
                    if live(s, N):
                        act.wait_ge(S["xnT_in_psum"], s + 1)
                        need(act, S["q_in_psum"] if projected else S["scores_in_psum"], s - 1)
                        nc.scalar.activation(xnT[k % 2][:], bank_x[:, 0:P], ACT.Copy).then_inc(S["xnT_ready"], 1)
                    if projected and live(s, N):
                        act.wait_ge(S["q_in_psum"], s + 1)
                        need(act, S["scores_in_psum"], s - 1)
                        nc.scalar.activation(qT[k % 2][:], bank_x[:, P:2 * P], ACT.Identity, bias=bq[:])\
                            .then_inc(S["q_ready"], 1)
                    m = s - 2
                    if live(m, N):
                        act.wait_ge(S["probT_in_psum"], m + 1)
                        need(act, S["mixed_in_psum"], m - 1)
                        nc.scalar.activation(probT[k % 2][:], bank_t[:], ACT.Copy).then_inc(S["probT_ready"], 1)
                    m, b = s - 1, (k - 1) % 2
                    if live(m, N):
                        act.wait_ge(S["shifted"], m + 1)
                        nc.scalar.activation(prob[b][:], prob[b][:], ACT.Exp, scale=1.0 / math.sqrt(HEAD))\
                            .then_inc(S["exp_ready"], 1)
                skewed(act, N, 2, step, UNROLL)

            @block.tensor
            def _(pe):
                pe.wait_ge(S["ones_set"], 4)
                if projected:
                    pe.wait_ge(S["weights_loaded"], 48)

                def step(i, k):
                    s = UNROLL * i + k
                    if live(s, N):
                        pe.wait_ge(S["xn_ready"], s + 1)
                        need(pe, q_ready, s)
                        pe.transpose(bank_x[:, 0:P], xn[k % 2][:], g.ident[:]).then_inc(S["xnT_in_psum"], 1)
                    m, b = s - 1, (k - 1) % 2
                    if live(m, N):
                        octet = ((k - 1) // OTILES) % 2
                        pe.wait_ge(k_loaded[octet], 16 * HEADS * (i + (k - 1) // UNROLL + 1))
                        pe.wait_ge(q_ready, m + 1)
                        need(pe, S["shifted"], m - 1)
                        for row in range(2):
                            for half in range(2):
                                heads = slice(8 * half, 8 * half + 8)
                                last = pe.matmul(bank_s[b][64 * row:64 * row + 64, heads, :],
                                                 qT[b][:, 64 * row:64 * row + 64],
                                                 k_diag[octet][:, heads, 2 * ((k - 1) % OTILES) + row, :], start=True, stop=True)
                        last.then_inc(S["scores_in_psum"], 1)
                    if projected and live(s, N):
                        pe.wait_ge(S["xnT_ready"], s + 1)
                        pe.matmul(bank_x[:, P:2 * P], wq[:], xnT[k % 2][:], start=True, stop=True)\
                            .then_inc(S["q_in_psum"], 1)
                    m, b = s - 2, (k - 2) % 2
                    if live(m, N):
                        pe.wait_ge(S["exp_ready"], m + 1)
                        need(pe, S["probT_ready"], m)
                        for hp in range(HEADS // 2):
                            last = pe.transpose(bank_t[:, hp, :],
                                                prob[b][:, 2 * hp:2 * hp + 2, :].rearrange("p h t -> p (h t)"),
                                                g.ident[:])
                        last.then_inc(S["probT_in_psum"], 1)
                    m, b = s - 3, (k - 3) % 2
                    if live(m, N):
                        octet = ((k - 3) // OTILES) % 2
                        pe.wait_ge(S["probT_ready"], m + 1)
                        pe.wait_ge(S["v_diag_ready"], 2 * i + (k - 3) // OTILES + 1)
                        need(pe, S["mixed_ready"], m)
                        for hp in range(HEADS // 2):
                            for row in range(2):
                                last = pe.matmul(
                                    bank_o[64 * row:64 * row + 64, 18 * hp:18 * hp + 18],
                                    probT[b][:, hp, 64 * row:64 * row + 64],
                                    v_diag[octet][:, 2 * ((k - 3) % OTILES) + row, hp, :, :].rearrange("p c d -> p (c d)"),
                                    start=True, stop=True)
                        last.then_inc(S["mixed_in_psum"], 1)
                skewed(pe, N, 3, step, UNROLL)


R_HEADS, R_KEY, R_VAL = 8, 64, 128


def retention_tables():
    freq = 1.0 / 10000.0 ** (np.arange(0, R_KEY, 2, dtype=np.float32) / np.float32(R_KEY))
    angle = (np.arange(P) % SEQ).astype(np.float32)[:, None] * freq[None, :].astype(np.float32)
    cos, sin = np.cos(angle.astype(np.float64)), np.sin(angle.astype(np.float64))
    gamma = 1.0 - np.exp2(-5.0 - np.arange(R_HEADS))
    rel = np.arange(SEQ)[None, :] - np.arange(SEQ)[:, None]
    decay = np.where(rel >= 0, gamma[:, None, None] ** np.maximum(rel, 0), 0.0) * R_KEY ** -0.5
    decay = np.tile(decay.transpose(1, 0, 2), (2, 1, 1))
    return (np.concatenate([cos, cos], 1).astype(np.float32), np.concatenate([-sin, sin], 1).astype(np.float32),
            decay.astype(np.float32))


def retention_phase(g):
    nc, dram = g.nc, g.dram
    row_statistics(g, "ret")
    with ExitStack() as ctx:
        def sb(n, shape):
            return g.sbuf(f"ret_{n}", shape, ctx=ctx)

        def ring(n, shape, size=2):
            return [sb(f"{n}{k}", shape) for k in range(size)]

        H, HP, W = R_HEADS, R_HEADS // 2, R_HEADS * R_VAL
        wqk, wv, wg = sb("wqk", [D, 1024]), sb("wv", [D, H, R_VAL]), sb("wg", [D, W])
        wo = sb("wo", [R_VAL, H, D])
        cos, sin, decay = sb("cos", [P, R_KEY]), sb("sin", [P, R_KEY]), sb("decay", [P, H, SEQ])
        gn_w, gn_b = sb("gn_w", [R_VAL, H]), sb("gn_b", [R_VAL, H])
        wv_mean = sb("wv_mean", [D, H])
        xn, xnT = ring("xn", [P, D]), ring("xnT", [D, P], 4)
        qk, turned = ring("qk", [P, 2, H, R_KEY]), ring("turned", [P, 2, H, R_KEY])
        q_diag, kT = ring("q_diag", [P, HP, 2, 2, SEQ]), ring("kT", [P, HP, P])
        v = ring("v", [P, H, R_VAL])
        s_diag = ring("s_diag", [P, H, 2, SEQ])
        square, normed = sb("square", [P, H, R_VAL]), ring("normed", [P, H, R_VAL])
        var, rstd = ring("var", [P, H]), ring("rstd", [P, H])
        minus_half = sb("minus_half", [P, H])
        gate, gated = ring("gate", [R_VAL, H, P]), ring("gated", [R_VAL, H, P])
        ps_qk, ps_vg, ps_t, ps_o = (ctx.enter_context(nc.psum_tensor(f"ret_ps{k}", [P, 1024], F32))
                                    for k in range(4))
        names = ("loaded", "cleared", "wv_step", "wv_ready", "xn_ready", "xnT_in_psum", "xnT_ready", "qk_in_psum",
                 "turned_ready", "qk_ready", "qkT_in_psum", "q_diag_ready", "kT_ready", "scores_in_psum",
                 "s_ready", "v_in_psum", "v_ready", "gate_in_psum", "gate_ready", "mixed_in_psum", "square_ready",
                 "sum_ready", "var_ready", "rstd_ready", "normed_ready", "normedT_in_psum",
                 "affine_dve", "affine_act", "gated_ready", "out_in_psum", "x_updated", "half_set")
        S = {k: g.sem(f"ret_{k}") for k in names}
        N, UNROLL = TILES, 4
        DVE_HEADS = H // 2
        heads = lambda ap: ap.rearrange("p (h c) -> p h c", c=R_VAL)

        with nc.Block() as block:

            @block.sync
            def _(sp):
                for dst, src in ((wv, "ret_wv"), (wqk, "ret_wqk"), (cos, "ret_cos"), (sin, "ret_sin"),
                                 (decay, "ret_decay"), (wg, "ret_wg"), (wo, "ret_wo"), (gn_w, "ret_gn_w"),
                                 (gn_b, "ret_gn_b")):
                    sp.dma_start(dst[:], dram[src]).then_inc(S["loaded"], 16)

            @block.gpsimd
            def _(pool):
                for k in range(2):
                    pool.memset(q_diag[k][:], 0.0).then_inc(S["cleared"], 1)
                    pool.memset(s_diag[k][:], 0.0).then_inc(S["cleared"], 1)
                pool.memset(minus_half[:], -0.5).then_inc(S["half_set"], 1)
                pool.wait_ge(S["loaded"], 16 * 9)
                pool.wait_ge(S["half_set"], 1)

                def step(i, k):
                    s = UNROLL * i + k
                    m, b = s - 2, k % 2
                    if live(m, N):
                        pool.wait_ge(S["var_ready"], m + 1)
                        need(pool, S["normed_ready"], m - 1)
                        pool.tensor_tensor(rstd[b][:], var[b][:], minus_half[:], ALU.pow).then_inc(S["rstd_ready"], 1)
                    if live(s, N):
                        pool.wait_ge(S["turned_ready"], s + 1)
                        pool.tensor_tensor(qk[k % 2][:], qk[k % 2][:], turned[k % 2][:], ALU.add)\
                            .then_inc(S["qk_ready"], 1)
                skewed(pool, N, 2, step, UNROLL)

            @block.vector
            def _(dve):
                dve.wait_ge(S["loaded"], 16 * 9)
                dve.tensor_reduce(wv_mean[:], wv[:], AXIS.X, ALU.add).then_inc(S["wv_step"], 1)
                dve.wait_ge(S["wv_step"], 1)
                dve.tensor_scalar(wv_mean[:], wv_mean[:], 1.0 / R_VAL, None, ALU.mult).then_inc(S["wv_step"], 1)
                dve.wait_ge(S["wv_step"], 2)
                dve.tensor_tensor(wv[:], wv[:], wv_mean[:].unsqueeze(2).to_broadcast([D, H, R_VAL]),
                                  ALU.subtract).then_inc(S["wv_ready"], 1)
                dve.wait_ge(S["cleared"], 4)

                def step(i, k):
                    s = UNROLL * i + k
                    m, b = s - 4, k % 2
                    if live(m, N):
                        dve.wait_ge(S["affine_dve"], m + 1)
                        dve.wait_ge(S["affine_act"], m + 1)
                        dve.wait_ge(S["gate_ready"], m + 1)
                        dve.tensor_tensor(gated[b][:], gated[b][:], gate[b][:], ALU.mult)\
                            .then_inc(S["gated_ready"], 1)
                    m, b = s - 3, (k - 3) % 2
                    if live(m, N):
                        dve.wait_ge(S["square_ready"], m + 1)
                        need(dve, S["rstd_ready"], m - 1)
                        dve.tensor_reduce(var[b][:], square[:], AXIS.X, ALU.add).then_inc(S["sum_ready"], 1)
                        dve.wait_ge(S["sum_ready"], m + 1)
                        dve.tensor_scalar(var[b][:], var[b][:], 1.0 / R_VAL, EPS, ALU.mult, ALU.add)\
                            .then_inc(S["var_ready"], 1)
                    m = s - 4
                    if live(m, N):
                        dve.wait_ge(S["out_in_psum"], m + 1)
                        dve.tensor_tensor(g.X[:, m, :], ps_vg[:, 0:D], g.X[:, m, :], ALU.add)\
                            .then_inc(S["x_updated"], 1)
                    m, b = s - 1, (k - 1) % 2
                    if live(m, N):
                        dve.wait_ge(S["qk_in_psum"], m + 1)
                        need(dve, S["qkT_in_psum"], m - 1)
                        src = ps_qk[:].rearrange("p (a e) -> p a e", e=R_KEY)
                        fold = lambda ap: ap.rearrange("p q h e -> p (q h) e")
                        dve.tensor_tensor(fold(qk[b][:]), src,
                                          cos[:].unsqueeze(1).to_broadcast([P, 2 * H, R_KEY]), ALU.mult)
                        for part in range(2):
                            to, of = slice(32 * part, 32 * part + 32), slice(32 - 32 * part, 64 - 32 * part)
                            last = dve.tensor_tensor(fold(turned[b][:])[:, :, to], src[:, :, of],
                                                     sin[:, to].unsqueeze(1).to_broadcast([P, 2 * H, 32]), ALU.mult)
                        last.then_inc(S["turned_ready"], 1)
                    m, b = s - 3, (k - 3) % 2
                    if live(m, N):
                        dve.wait_ge(S["rstd_ready"], m + 1)
                        need(dve, S["normedT_in_psum"], m - 1)
                        dve.tensor_tensor(normed[b][:], heads(ps_o[:]),
                                          rstd[b][:].unsqueeze(2).to_broadcast([P, H, R_VAL]), ALU.mult)\
                            .then_inc(S["normed_ready"], 1)
                    m, b = s - 2, k % 2
                    if live(m, N):
                        dve.wait_ge(S["scores_in_psum"], m + 1)
                        need(dve, S["mixed_in_psum"], m - 1)
                        for row in range(2):
                            rows = slice(64 * row, 64 * row + 64)
                            last = dve.tensor_tensor(s_diag[b][rows, :, row, :],
                                                     ps_t[rows, 0:512].rearrange("p (h t) -> p h t", t=SEQ),
                                                     decay[rows, :, :], ALU.mult)
                        last.then_inc(S["s_ready"], 1)
                    if live(s, N):
                        need(dve, S["xnT_in_psum"], s - 1)
                        dve.tensor_scalar(xn[k % 2][:], g.X[:, s, :], g.mean[:, bass.ds(s, 1)],
                                          g.rstd[:, bass.ds(s, 1)], ALU.subtract, ALU.mult)\
                            .then_inc(S["xn_ready"], 1)
                    m = s - 4
                    if live(m, N):
                        dve.wait_ge(S["x_updated"], m + 1)
                        dve.bn_stats(g.stats[:, m, :], g.X[:, m, :])
                    m, b = s - 3, (k - 3) % 2
                    if live(m, N):
                        dve.wait_ge(S["normedT_in_psum"], m + 1)
                        need(dve, S["out_in_psum"], m - 1)
                        for h in range(DVE_HEADS):
                            last = dve.tensor_scalar(gated[b][:, h, :], ps_t[:, h * P:(h + 1) * P], gn_w[:, h:h + 1],
                                                     gn_b[:, h:h + 1], ALU.mult, ALU.add)
                        last.then_inc(S["affine_dve"], 1)
                skewed(dve, N, 4, step, UNROLL)

            @block.scalar
            def _(act):
                act.wait_ge(S["cleared"], 4)

                def step(i, k):
                    s = UNROLL * i + k
                    if live(s, N):
                        act.wait_ge(S["xnT_in_psum"], s + 1)
                        need(act, S["gate_in_psum"], s - 3)
                        nc.scalar.activation(xnT[k][:], ps_qk[:, 0:P], ACT.Copy).then_inc(S["xnT_ready"], 1)
                    m = s - 2
                    if live(m, N):
                        act.wait_ge(S["mixed_in_psum"], m + 1)
                        need(act, S["sum_ready"], m)
                        nc.scalar.activation(square[:], heads(ps_o[:]), ACT.Square).then_inc(S["square_ready"], 1)
                    m, b = s - 1, (k - 1) % 2
                    if live(m, N):
                        act.wait_ge(S["qkT_in_psum"], m + 1)
                        need(act, S["scores_in_psum"], m - 1)
                        for half in range(2):
                            rows = slice(64 * half, 64 * half + 64)
                            last = nc.scalar.activation(
                                q_diag[b][rows, :, :, half, :],
                                ps_t[rows, 0:512].rearrange("p (h r t) -> p h r t", r=2, t=SEQ), ACT.Copy)
                        last.then_inc(S["q_diag_ready"], 1)
                        nc.scalar.activation(kT[b][:], ps_t[:, 512:1024].rearrange("p (h t) -> p h t", t=P),
                                             ACT.Copy).then_inc(S["kT_ready"], 1)
                    if live(s, N):
                        act.wait_ge(S["v_in_psum"], s + 1)
                        need(act, S["mixed_in_psum"], s - 1)
                        nc.scalar.activation(v[k % 2][:], heads(ps_vg[:]), ACT.Copy).then_inc(S["v_ready"], 1)
                    m, b = s - 2, k % 2
                    if live(m, N):
                        act.wait_ge(S["gate_in_psum"], m + 1)
                        need(act, S["gated_ready"], m - 1)
                        nc.scalar.activation(gate[b][:], heads(ps_vg[:]), ACT.Silu).then_inc(S["gate_ready"], 1)
                    if live(m, N):
                        act.wait_ge(S["normedT_in_psum"], m + 1)
                        need(act, S["out_in_psum"], m - 1)
                        for h in range(DVE_HEADS, H):
                            last = nc.scalar.activation(gated[b][:, h, :], ps_t[:, h * P:(h + 1) * P], ACT.Identity,
                                                        bias=gn_b[:, h:h + 1], scale=gn_w[:, h:h + 1])
                        last.then_inc(S["affine_act"], 1)
                skewed(act, N, 2, step, UNROLL)

            @block.tensor
            def _(pe):
                pe.wait_ge(S["wv_ready"], 1)
                pe.wait_ge(S["loaded"], 16 * 9)

                def step(i, k):
                    ahead, even = UNROLL * i + k, k % 2
                    s, k = ahead - 1, (k - 1) % UNROLL
                    if live(s, N):
                        pe.wait_ge(S["xnT_ready"], s + 1)
                        for half in range(2):
                            cols = slice(512 * half, 512 * half + 512)
                            last = pe.matmul(ps_qk[:, cols], xnT[k][:], wqk[:, cols], start=True, stop=True)
                        last.then_inc(S["qk_in_psum"], 1)
                    m, b = s - 3, (k - 3) % 2
                    if live(m, N):
                        pe.wait_ge(S["gated_ready"], m + 1)
                        pe.wait_ge(S["gate_ready"], m + 1)
                        for h in range(H):
                            last = pe.matmul(ps_vg[:, 0:D], gated[b][:, h, :], wo[:, h, :],
                                             start=(h == 0), stop=(h == H - 1))
                        last.then_inc(S["out_in_psum"], 1)
                    m, b = s - 1, (k - 1) % 2
                    if live(m, N):
                        pe.wait_ge(S["qk_ready"], m + 1)
                        need(pe, S["affine_dve"], m - 1)
                        need(pe, S["affine_act"], m - 1)
                        need(pe, S["s_ready"], m)
                        for which in range(2):
                            for hp in range(HP):
                                last = pe.transpose(
                                    ps_t[:, 512 * which + 128 * hp:512 * which + 128 * hp + 128],
                                    qk[b][:, which, 2 * hp:2 * hp + 2, :].rearrange("p h e -> p (h e)"),
                                    g.ident[:])
                        last.then_inc(S["qkT_in_psum"], 1)
                    if live(s, N):
                        need(pe, S["v_ready"], s)
                        need(pe, S["gate_ready"], s - 2)
                        need(pe, S["x_updated"], s - 2)
                        for half in range(2):
                            cols = slice(512 * half, 512 * half + 512)
                            last = pe.matmul(ps_vg[:, cols], xnT[k][:],
                                             wv[:].rearrange("p h c -> p (h c)")[:, cols], start=True, stop=True)
                        last.then_inc(S["v_in_psum"], 1)
                    m, b = s - 1, (k - 1) % 2
                    if live(m, N):
                        pe.wait_ge(S["q_diag_ready"], m + 1)
                        pe.wait_ge(S["kT_ready"], m + 1)
                        for hp in range(HP):
                            for row in range(2):
                                last = pe.matmul(ps_t[64 * row:64 * row + 64, 128 * hp:128 * hp + 128],
                                                 kT[b][:, hp, 64 * row:64 * row + 64],
                                                 q_diag[b][:, hp, row, :, :].rearrange("p h t -> p (h t)"),
                                                 start=True, stop=True)
                        last.then_inc(S["scores_in_psum"], 1)
                    m, b = s - 2, (k - 2) % 4
                    if live(m, N):
                        if live(s, N):
                            pe.wait_ge(S["v_ready"], s + 1)
                        else:
                            need(pe, S["x_updated"], s - 2)
                        for h in range(H):
                            last = pe.matmul(ps_vg[:, 128 * h:128 * h + 128], wg[:, 128 * h:128 * h + 128],
                                             xnT[b][:], start=True, stop=True)
                        last.then_inc(S["gate_in_psum"], 1)
                        pe.wait_ge(S["normed_ready"], m + 1)
                        if live(s - 1, N):
                            pe.wait_ge(S["s_ready"], m + 2)
                        else:
                            need(pe, S["affine_dve"], m)
                            need(pe, S["affine_act"], m)
                        for h in range(H):
                            last = pe.transpose(ps_t[:, 128 * h:128 * h + 128], normed[k % 2][:, h, :], g.ident[:])
                        last.then_inc(S["normedT_in_psum"], 1)
                    if live(ahead, N):
                        pe.wait_ge(S["xn_ready"], ahead + 1)
                        need(pe, S["turned_ready"], ahead)
                        pe.transpose(ps_qk[:, 0:P], xn[even][:], g.ident[:]).then_inc(S["xnT_in_psum"], 1)
                    m, b = s - 1, (k - 1) % 2
                    if live(m, N):
                        pe.wait_ge(S["s_ready"], m + 1)
                        pe.wait_ge(S["v_ready"], m + 1)
                        need(pe, S["normed_ready"], m)
                        for h in range(H):
                            last = pe.matmul(ps_o[:, 128 * h:128 * h + 128],
                                             s_diag[b][:, h, :, :].rearrange("p r t -> p (r t)"),
                                             v[b][:, h, :], start=True, stop=True)
                        last.then_inc(S["mixed_in_psum"], 1)
                skewed(pe, N, 4, step, UNROLL)


EXPERTS, FFN = 8, 512
FT = FFN // P
BIG = 1.0e38
TOP_K = 2
SLOT_TILES = (TOP_K * TOKENS + EXPERTS * (P - 1)) // P + 1
SLOTS = SLOT_TILES * P
MOVED = 4
GT = 512
GROUPS, GTILES = TOKENS // GT, GT // P


def route(g, name, spec, f):
    nc, dram = g.nc, g.dram
    row_statistics(g, name)
    with ExitStack() as own:
        def sb(n, shape):
            return g.sbuf(f"{name}_{n}", shape, ctx=own)

        by_token = [P, TILES, EXPERTS]
        gate_w, gate_b = sb("gate_w", [D, EXPERTS]), sb("gate_b", [P, EXPERTS])
        rank, before, all_ones = sb("rank", [P, EXPERTS]), sb("before", [P, P]), sb("all_ones", [P, P])
        tile_starts, tile_numbers = sb("tile_starts", [P, TILES]), sb("tile_numbers", [1, SLOT_TILES])
        xn, xnT = [sb(f"xn_tile{k}", [P, D]) for k in range(2)], [sb(f"xnT{k}", [D, P]) for k in range(2)]
        zeros = sb("zeros", [P, 1024])
        logit, key, score, both = sb("logit", by_token), sb("key", by_token), sb("score", by_token), sb("both", by_token)
        first, second, place = sb("first", by_token), sb("second", by_token), sb("place", by_token)
        top, rec = sb("top", [P, TILES]), sb("rec", [P, TILES])
        ones_row = sb("ones_row", [P, EXPERTS, TILES])
        per_tile, running = sb("per_tile", [P, EXPERTS, TILES]), sb("running", [P, EXPERTS, TILES])
        over = sb("over", [P, EXPERTS, TILES])
        earlier, count, tiles = sb("earlier", [P, EXPERTS]), sb("count", [P, EXPERTS]), sb("tiles", [P, EXPERTS])
        tile_end, offset = sb("tile_end", [P, EXPERTS]), sb("offset", [P, EXPERTS])
        ended, owner = sb("ended", [1, SLOT_TILES, EXPERTS]), sb("tile_owner", [1, SLOT_TILES])
        bank_x = [own.enter_context(nc.psum_tensor(f"{name}_xT_psum{k}", [P, 512], F32)) for k in range(2)]
        bank_l = own.enter_context(nc.psum_tensor(f"{name}_logit_psum", [P, TILES, EXPERTS], F32))
        bank_p = own.enter_context(nc.psum_tensor(f"{name}_prefix_psum", [P, TILES, EXPERTS], F32))
        bank_c = own.enter_context(nc.psum_tensor(f"{name}_count_psum", [P, TILES, EXPERTS], F32))
        names = ("loaded", "xn_ready", "xnT_in_psum", "xnT_ready", "logits_in_psum", "step", "exp_in", "exp_out",
                 "kept", "both_ready", "counts_in_psum", "constants_set", "zeros_set", "slots_zeroed")
        S = {k: g.sem(f"{name}_r_{k}") for k in names}
        bc = lambda ap: ap[:].unsqueeze(2).to_broadcast(by_token)
        per_token = lambda ap: ap[:].unsqueeze(1).to_broadcast(by_token)
        n_loads = 6
        with nc.Block() as block:

            @block.sync
            def _(sp):
                sp.dma_start(gate_w[:], dram[spec["gate_w"]]).then_inc(S["loaded"], 16)
                sp.dma_start(gate_b[:], dram[spec["gate_b"]].to_broadcast([P, EXPERTS])).then_inc(S["loaded"], 16)
                sp.dma_start(rank[:], dram["rank"]).then_inc(S["loaded"], 16)
                sp.dma_start(before[:], dram["before"]).then_inc(S["loaded"], 16)
                sp.dma_start(tile_starts[:], dram["tile_starts"]).then_inc(S["loaded"], 16)
                sp.dma_start(tile_numbers[:], dram["tile_numbers"]).then_inc(S["loaded"], 16)
                if spec["zero_slots"]:
                    sp.wait_ge(S["zeros_set"], 1)
                    flat = g.slots_x.rearrange("(p a) d -> p (a d)", p=P)
                    for c in range(SLOTS * D // P // 1024):
                        sp.dma_start(flat[:, 1024 * c:1024 * c + 1024], zeros[:]).then_inc(S["slots_zeroed"], 16)
                    sp.wait_ge(S["slots_zeroed"], 16 * (SLOTS * D // P // 1024))

            @block.vector
            def _(dve):
                done = [0]

                def seq(ins):
                    done[0] += 1
                    ins.then_inc(S["step"], 1)
                    dve.wait_ge(S["step"], done[0])

                def xn_step(i, k):
                    s = 2 * i + k
                    if live(s, TILES):
                        need(dve, S["xnT_in_psum"], s - 1)
                        dve.tensor_scalar(xn[k][:], g.X[:, s, :], g.mean[:, bass.ds(s, 1)],
                                          g.rstd[:, bass.ds(s, 1)], ALU.subtract, ALU.mult)\
                            .then_inc(S["xn_ready"], 1)
                skewed(dve, TILES, 0, xn_step)
                dve.wait_ge(S["loaded"], 16 * n_loads)
                dve.wait_ge(S["logits_in_psum"], TILES)
                seq(dve.tensor_tensor(logit[:], bank_l[:], per_token(gate_b), ALU.add))

                def one_hot_of_max(out, values, peak):
                    seq(dve.tensor_reduce(peak[:], values[:], AXIS.X, ALU.max))
                    seq(dve.tensor_tensor(key[:], values[:], bc(peak), ALU.is_equal))
                    seq(dve.tensor_tensor(key[:], key[:], per_token(rank), ALU.mult))
                    seq(dve.tensor_reduce(rec[:], key[:], AXIS.X, ALU.max))
                    seq(dve.tensor_tensor(out[:], key[:], bc(rec), ALU.is_equal))

                one_hot_of_max(first, logit, top)
                seq(dve.scalar_tensor_tensor(out=score[:], in0=first[:], scalar=-BIG, in1=logit[:],
                                             op0=ALU.mult, op1=ALU.add))
                one_hot_of_max(second, score, rec)
                dve.tensor_tensor(both[:], first[:], second[:], ALU.add).then_inc(S["both_ready"], 1)

                def total(out, values, one_hot):
                    seq(dve.tensor_tensor(key[:], values[:], one_hot[:], ALU.mult))
                    seq(dve.tensor_reduce(out[:], key[:], AXIS.X, ALU.add))

                w = [f["weight0"], f["weight1"]]
                if spec["kind"] == "sigmoid":
                    dve.wait_ge(S["exp_out"], 1)
                    seq(dve.tensor_scalar(score[:], score[:], 1.0, None, ALU.add))
                    seq(dve.reciprocal(score[:], score[:]))
                    total(w[0], score, first)
                    total(w[1], score, second)
                    seq(dve.tensor_tensor(top[:], w[0], w[1], ALU.max))
                    dve.tensor_tensor(f["pair"][:], f["pair"][:], top[:].unsqueeze(1).to_broadcast([P, TOP_K, TILES]),
                                      ALU.subtract).then_inc(S["exp_in"], 1)
                    dve.wait_ge(S["exp_out"], 2)
                else:
                    dve.tensor_tensor(place[:], logit[:], bc(top), ALU.subtract).then_inc(S["exp_in"], 1)
                    dve.wait_ge(S["exp_out"], 1)
                    seq(dve.tensor_reduce(rec[:], score[:], AXIS.X, ALU.add))
                    seq(dve.reciprocal(rec[:], rec[:]))
                    seq(dve.tensor_tensor(score[:], score[:], bc(rec), ALU.mult))
                    total(w[0], score, first)
                    total(w[1], score, second)
                seq(dve.tensor_tensor(rec[:], w[0], w[1], ALU.add))
                if spec["kind"] == "softmax":
                    seq(dve.tensor_scalar(rec[:], rec[:], 1e-8, None, ALU.add))
                seq(dve.reciprocal(rec[:], rec[:]))
                dve.tensor_tensor(f["pair"][:], f["pair"][:], rec[:].unsqueeze(1).to_broadcast([P, TOP_K, TILES]),
                                  ALU.mult)

                dve.wait_ge(S["counts_in_psum"], 1)
                dve.wait_ge(S["constants_set"], 3)
                seq(dve.tensor_copy(per_tile[:], bank_c[:].rearrange("p t e -> p e t")))
                flat = lambda ap: ap[:].rearrange("p e t -> p (e t)")
                seq(dve.tensor_tensor_scan(flat(running), flat(ones_row), flat(per_tile), 0.0, ALU.mult, ALU.add))
                seq(dve.tensor_copy(earlier[:, 1:EXPERTS], running[:, 0:EXPERTS - 1, TILES - 1]))
                seq(dve.tensor_tensor(count[:], running[:, :, TILES - 1], earlier[:], ALU.subtract))
                shape = [P, EXPERTS, TILES]
                seq(dve.tensor_tensor(over[:], count[:].unsqueeze(2).to_broadcast(shape),
                                      tile_starts[:].unsqueeze(1).to_broadcast(shape), ALU.is_gt))
                seq(dve.tensor_reduce(tiles[:], over[:], AXIS.X, ALU.add))
                seq(dve.tensor_tensor_scan(tile_end[:], ones_row[:, 0, 0:EXPERTS], tiles[:], 0.0, ALU.mult, ALU.add))
                seq(dve.tensor_tensor(offset[:], tile_end[:], tiles[:], ALU.subtract))
                seq(dve.scalar_tensor_tensor(out=offset[:], in0=offset[:], scalar=float(P), in1=earlier[:],
                                             op0=ALU.mult, op1=ALU.subtract))
                seq(dve.tensor_tensor(running[:], running[:], per_tile[:], ALU.subtract))
                seq(dve.tensor_tensor(place[:], bank_p[:], running[:].rearrange("p e t -> p t e"), ALU.add))
                seq(dve.tensor_tensor(place[:], place[:], per_token(offset), ALU.add))
                for n, one_hot in enumerate((first, second)):
                    total(rec, place, one_hot)
                    seq(dve.tensor_copy(f["slots"][:, n, :], rec[:]))
                shape = [1, SLOT_TILES, EXPERTS]
                seq(dve.tensor_tensor(ended[:], tile_end[0:1, :].unsqueeze(1).to_broadcast(shape),
                                      tile_numbers[:].unsqueeze(2).to_broadcast(shape), ALU.is_le))
                seq(dve.tensor_reduce(owner[:], ended[:], AXIS.X, ALU.add))
                seq(dve.tensor_scalar(owner[:], owner[:], float(EXPERTS - 1), None, ALU.min))
                dve.tensor_copy(f["owner"][:], owner[:])

            @block.gpsimd
            def _(pool):
                if spec["zero_slots"]:
                    pool.memset(zeros[:], 0.0).then_inc(S["zeros_set"], 1)
                pool.memset(all_ones[:], 1.0).then_inc(S["constants_set"], 1)
                pool.memset(ones_row[:], 1.0).then_inc(S["constants_set"], 1)
                pool.memset(earlier[:], 0.0).then_inc(S["constants_set"], 1)

            @block.scalar
            def _(act):
                def step(i, k):
                    s = 2 * i + k
                    act.wait_ge(S["xnT_in_psum"], s + 1)
                    need(act, S["logits_in_psum"], s - 1)
                    nc.scalar.activation(xnT[k][:], bank_x[k][:, 0:P], ACT.Copy).then_inc(S["xnT_ready"], 1)
                    if spec["shared"]:
                        nc.scalar.activation(f["xnT"][:, bass.ds(s * P, P)], bank_x[k][:, 0:P], ACT.Copy)\
                            .then_inc(S["kept"], 1)
                skewed(act, TILES, 0, step)
                if spec["kind"] == "sigmoid":
                    act.wait_ge(S["both_ready"], 1)
                    nc.scalar.activation(score[:], bank_l[:], ACT.Exp, scale=-1.0).then_inc(S["exp_out"], 1)
                    act.wait_ge(S["exp_in"], 1)
                    nc.scalar.activation(f["pair"][:], f["pair"][:], ACT.Exp).then_inc(S["exp_out"], 1)
                else:
                    act.wait_ge(S["exp_in"], 1)
                    nc.scalar.activation(score[:], place[:], ACT.Exp).then_inc(S["exp_out"], 1)

            @block.tensor
            def _(pe):
                pe.wait_ge(S["loaded"], 16 * n_loads)

                def step(i, k):
                    s = 2 * i + k
                    if live(s, TILES):
                        pe.wait_ge(S["xn_ready"], s + 1)
                        need(pe, S["kept"] if spec["shared"] else S["xnT_ready"], s - 1)
                        pe.transpose(bank_x[k][:, 0:P], xn[k][:], g.ident[:]).then_inc(S["xnT_in_psum"], 1)
                    m, b = s - 1, (k - 1) % 2
                    if live(m, TILES):
                        pe.wait_ge(S["xnT_ready"], m + 1)
                        pe.matmul(bank_l[:, m, :], xnT[b][:], gate_w[:], start=True, stop=True)\
                            .then_inc(S["logits_in_psum"], 1)
                skewed(pe, TILES, 1, step, peeled=2)
                pe.wait_ge(S["both_ready"], 1)
                pe.wait_ge(S["constants_set"], 1)
                pe.matmul(bank_p[:], before[:], both[:], start=True, stop=True)
                pe.matmul(bank_c[:], all_ones[:], both[:], start=True, stop=True).then_inc(S["counts_in_psum"], 1)


class SharedExpert:

    def __init__(self, g, name, ctx, spec, f, e):
        self.g, self.spec, self.f, self.e = g, spec, f, e
        self.hidden = [g.sbuf(f"{name}_hidden{k}", [P, FT, GT], ctx=ctx) for k in range(2)]
        self.bank_h = [ctx.enter_context(g.nc.psum_tensor(f"{name}_hidden_psum{k}", [P, GT], F32)) for k in range(4)]
        self.bank_y = [ctx.enter_context(g.nc.psum_tensor(f"{name}_y_psum{k}", [P, 4, D], F32)) for k in range(2)]
        self.up_done, self.hidden_ready = g.sem(f"{name}_up_done"), g.sem(f"{name}_hidden_ready")
        self.y_in_psum, self.y_added = g.sem(f"{name}_y_in_psum"), g.sem(f"{name}_y_added")

    def tensor(self, pe):
        f, e = self.f, self.e

        def step(i, k):
            s = 2 * i + k
            if live(s, GROUPS):
                for j in range(FT):
                    need(pe, self.hidden_ready, FT * (s - 1) + j + 1)
                    pe.matmul(self.bank_h[j][:], f["w_up"][:, e, j * P:(j + 1) * P], f["xnT"][:, bass.ds(s * GT, GT)],
                              start=True, stop=True).then_inc(self.up_done, 1)
            m, b = s - 1, (k - 1) % 2
            if live(m, GROUPS):
                pe.wait_ge(self.hidden_ready, FT * (m + 1))
                need(pe, self.y_added, m - 1)
                for t in range(GTILES):
                    for j in range(FT):
                        last = pe.matmul(self.bank_y[b][:, t, :], self.hidden[b][:, j, t * P:(t + 1) * P],
                                         f["w_down"][:, e, j, :], start=(j == 0), stop=(j == FT - 1))
                last.then_inc(self.y_in_psum, 1)
        skewed(pe, GROUPS, 1, step, peeled=2)

    def scalar(self, act):
        def step(i, k):
            s = 2 * i + k
            for j in range(FT):
                act.wait_ge(self.up_done, FT * s + j + 1)
                need(act, self.y_in_psum, s - 1)
                self.g.nc.scalar.activation(self.hidden[k][:, j, :], self.bank_h[j][:], self.spec["gelu"])\
                    .then_inc(self.hidden_ready, 1)
        skewed(act, GROUPS, 0, step, peeled=2)

    def vector(self, dve, s, k):
        dve.wait_ge(self.y_in_psum, s + 1)
        x = self.g.X[:, bass.ds(GTILES * s, GTILES), :]
        dve.tensor_tensor(x, self.bank_y[k][:], x, ALU.add).then_inc(self.y_added, 1)


class Turn:

    def __init__(self, g, name, ctx):
        self.cell = g.sbuf(f"{name}_turn_cell", [P, 1], ctx=ctx)
        self.done = g.sem(f"{name}_turn_done")
        self.source = g.ident

    def __call__(self, pool, number, *waits):
        need(pool, self.done, number)
        for sem, value in waits:
            need(pool, sem, value)
        pool.tensor_tensor(self.cell[:], self.source[:, 0:1], self.source[:, 0:1], ALU.add).then_inc(self.done, 1)


def dispatch(g, name, spec, f):
    nc, dram = g.nc, g.dram
    with ExitStack() as ctx:
        shared = SharedExpert(g, f"{name}_s0", ctx, spec, f, 0) if spec["shared"] else None
        turn = Turn(g, name, ctx)
        group_slots = [g.sbuf(f"{name}_group_slots{k}", [P, TOP_K, GTILES], I32, ctx=ctx) for k in range(2)]
        loaded, slots_ready = g.sem(f"{name}_w_loaded"), g.sem(f"{name}_slots_ready")
        xn = [g.sbuf(f"{name}_xn{k}", [P, GTILES, D], ctx=ctx) for k in range(2)]
        xn_ready, xn_added = g.sem(f"{name}_xn_ready"), g.sem(f"{name}_xn_added")
        scattered, base = g.indirect_transfers()
        loads = [(f["w_up"], dram[spec["w_up"]]), (f["w_down"], dram[spec["w_down"]])]
        if spec["b_up"]:
            loads += [(f["b_up"], dram[spec["b_up"]].partition_broadcast(P)),
                      (f["b_down"], dram[spec["b_down"]].partition_broadcast(P))]
        with nc.Block() as block:

            @block.sync
            def _(sp):
                for dst, src in loads:
                    sp.dma_start(dst[:], src).then_inc(loaded, 16)
                sp.wait_ge(loaded, 16 * len(loads))

            @block.gpsimd
            def _(pool):
                def step(i, k):
                    s = 2 * i + k
                    turn(pool, s, (xn_ready, s + 1), (slots_ready, s + 1))
                    for t in range(GTILES):
                        for n in range(TOP_K):
                            pool.indirect_dma_start(
                                out=g.slots_x[:, :],
                                out_offset=bass.IndirectOffsetOnAxis(ap=group_slots[k][:, n, t:t + 1], axis=0),
                                in_=xn[k][:, t, :], in_offset=None).then_inc(scattered[k], 16)
                skewed(pool, GROUPS, 0, step)
                for k in range(2):
                    pool.wait_ge(scattered[k], base + 16 * TOP_K * TILES // 2)

            @block.vector
            def _(dve):
                def step(i, k):
                    s = 2 * i + k
                    if live(s, GROUPS):
                        need(dve, scattered[k], base + 16 * TOP_K * GTILES * i)
                        dve.tensor_copy(group_slots[k][:], f["slots"][:, :, bass.ds(GTILES * s, GTILES)])\
                            .then_inc(slots_ready, 1)
                        x = g.X[:, bass.ds(GTILES * s, GTILES), :]
                        for t in range(GTILES):
                            tile = GTILES * s + t
                            last = dve.tensor_scalar(xn[k][:, t, :], g.X[:, tile, :], g.mean[:, bass.ds(tile, 1)],
                                                     g.rstd[:, bass.ds(tile, 1)], ALU.subtract, ALU.mult)
                        last.then_inc(xn_ready, 1)
                        if spec["plus_xn"]:
                            dve.wait_ge(xn_ready, s + 1)
                            dve.tensor_tensor(x, x, xn[k][:], ALU.add).then_inc(xn_added, 1)
                    m, b = s - 1, (k - 1) % 2
                    if shared and live(m, GROUPS):
                        dve.wait_ge(xn_added, m + 1)
                        shared.vector(dve, m, b)
                skewed(dve, GROUPS, 1, step, peeled=2)

            if shared:
                @block.tensor
                def _(pe):
                    pe.wait_ge(loaded, 16 * len(loads))
                    shared.tensor(pe)

                @block.scalar
                def _(act):
                    shared.scalar(act)


class Owners:

    def __init__(self, eng, f):
        self.eng, self.f, self.held = eng, f, {}

    def new_round(self):
        self.held = {}

    def of(self, place, tile):
        if place not in self.held:
            self.held[place] = self.eng.value_load(self.f["owner"][0:1, bass.ds(tile, 1)], min_val=0,
                                                   max_val=EXPERTS - 1)
        return self.held[place]


def run_experts(g, name, spec, f):
    nc = g.nc
    biased, N, E0 = spec["b_up"] is not None, SLOT_TILES, spec["shared"]
    with ExitStack() as ctx:
        def sb(n, shape):
            return g.sbuf(f"{name}_{n}", shape, ctx=ctx)

        x_in, y_out = [sb(f"x_in{k}", [P, MOVED, D]) for k in range(2)], [sb(f"y_out{k}", [P, MOVED, D]) for k in range(2)]
        xT, hidden = [sb(f"xT{k}", [D, P]) for k in range(2)], [sb(f"hid{k}", [P, FFN]) for k in range(2)]
        hT = [sb(f"hT{k}", [P, FT, P]) for k in range(2)]
        before_gelu = [sb(f"before_gelu{k}", [P, FFN]) for k in range(2)] if biased else None

        def ps(n, shape):
            return [ctx.enter_context(nc.psum_tensor(f"{name}_{n}_psum{k}", shape, F32)) for k in range(2)]

        bank_x, bank_h, bank_t, bank_y = ps("x", [P, 512]), ps("h", [P, FFN]), ps("hT", [P, FT, P]), ps("yt", [P, 512])
        names = ("xT_in_psum", "xT_ready", "up_done", "biased", "hidden_ready", "hT_in_psum", "hT_ready",
                 "y_in_psum", "y_ready")
        S = {k: g.sem(f"{name}_{k}") for k in names}
        x_loaded = [g.sem(f"{name}_x_loaded{k}") for k in range(2)]
        stored = [g.sem(f"{name}_y_stored{k}") for k in range(2)]
        h_read = S["biased"] if biased else S["hidden_ready"]

        def tiles(slots):
            return slots.rearrange("(j p) d -> p j d", p=P)

        with nc.Block() as block:

            @block.sync
            def _(sp):
                def step(i, k):
                    s = 2 * i + k
                    if live(s, N // MOVED):
                        need(sp, S["xT_in_psum"], MOVED * (s - 1))
                        sp.dma_start(x_in[k][:], tiles(g.slots_x)[:, bass.ds(MOVED * s, MOVED), :])\
                            .then_inc(x_loaded[k], 16)
                    m, b = s - 3, (k - 3) % 2
                    if live(m, N // MOVED):
                        sp.wait_ge(S["y_ready"], MOVED * (m + 1))
                        sp.dma_start(tiles(g.slots_y)[:, bass.ds(MOVED * m, MOVED), :], y_out[b][:])\
                            .then_inc(stored[b], 16)
                skewed(sp, N // MOVED, 3, step, peeled=2)
                for k in range(2):
                    sp.wait_ge(stored[k], 16 * N // (2 * MOVED))

            @block.tensor
            def _(pe):
                owners = Owners(pe, f)

                def step(i, k):
                    s = 2 * MOVED * i + k
                    if k == 0:
                        owners.new_round()
                    m, b = s - 1, (k - 1) % 2
                    if live(m, N):
                        expert = owners.of(k - 1, m)
                        pe.wait_ge(S["xT_ready"], m + 1)
                        need(pe, h_read, m - 1)
                        pe.matmul(bank_h[b][:], xT[b][:], f["w_up"][:, bass.ds(expert + E0, 1), :],
                                  start=True, stop=True).then_inc(S["up_done"], 1)
                    if k < 2 * MOVED - 1 and live(s, N):
                        owners.of(k, s)
                    if live(s, N):
                        if k % MOVED == 0:
                            pe.wait_ge(x_loaded[k // MOVED], 16 * (i + 1))
                        need(pe, S["xT_ready"], s - 1)
                        pe.transpose(bank_x[k % 2][:, 0:P], x_in[k // MOVED][:, k % MOVED, :], g.ident[:])\
                            .then_inc(S["xT_in_psum"], 1)
                    m, b = s - 2, k % 2
                    if live(m, N):
                        pe.wait_ge(S["hidden_ready"], m + 1)
                        need(pe, S["hT_ready"], m - 1)
                        for j in range(FT):
                            last = pe.transpose(bank_t[b][:, j, :], hidden[b][:, j * P:(j + 1) * P], g.ident[:])
                        last.then_inc(S["hT_in_psum"], 1)
                    m, b = s - 3, (k - 3) % 2
                    if live(m, N):
                        expert = owners.of(k - 3, m)
                        pe.wait_ge(S["hT_ready"], m + 1)
                        need(pe, S["y_ready"], m - 1)
                        for j in range(FT):
                            last = pe.matmul(bank_y[b][:, 0:D], hT[b][:, j, :],
                                             f["w_down"][:, bass.ds(expert + E0, 1), j, :],
                                             start=(j == 0), stop=(j == FT - 1))
                        last.then_inc(S["y_in_psum"], 1)
                skewed(pe, N, 3, step, 2 * MOVED)

            @block.scalar
            def _(act):
                def step(i, k):
                    s = 2 * i + k
                    if live(s, N):
                        act.wait_ge(S["xT_in_psum"], s + 1)
                        need(act, S["up_done"], s - 1)
                        nc.scalar.activation(xT[k][:], bank_x[k][:, 0:P], ACT.Copy).then_inc(S["xT_ready"], 1)
                    m, b = s - 1, (k - 1) % 2
                    if live(m, N):
                        act.wait_ge(h_read if biased else S["up_done"], m + 1)
                        need(act, S["hT_in_psum"], m - 1)
                        nc.scalar.activation(hidden[b][:], before_gelu[b][:] if biased else bank_h[b][:],
                                             spec["gelu"]).then_inc(S["hidden_ready"], 1)
                    m, b = s - 2, k
                    if live(m, N):
                        act.wait_ge(S["hT_in_psum"], m + 1)
                        need(act, S["y_in_psum"], m - 1)
                        nc.scalar.activation(hT[b][:], bank_t[b][:], ACT.Copy).then_inc(S["hT_ready"], 1)
                skewed(act, N, 2, step, peeled=2)

            @block.vector
            def _(dve):
                owners = Owners(dve, f)

                def step(i, k):
                    s = 2 * MOVED * i + k
                    if k == 0:
                        owners.new_round()
                    m, b = s, k % 2
                    if biased and live(m, N):
                        expert = owners.of(k, m)
                        dve.wait_ge(S["up_done"], m + 1)
                        need(dve, S["hidden_ready"], m - 1)
                        dve.tensor_tensor(before_gelu[b][:].unsqueeze(1), bank_h[b][:].unsqueeze(1),
                                          f["b_up"][:, bass.ds(expert, 1), :], ALU.add).then_inc(S["biased"], 1)
                    m, b = s - 2, k % 2
                    if live(m, N):
                        if biased:
                            expert = owners.of(k - 2, m)
                        dve.wait_ge(S["y_in_psum"], m + 1)
                        turn, place = (k - 2) // MOVED, (k - 2) % MOVED
                        if place == 0:
                            need(dve, stored[turn % 2], 16 * (i + turn // 2))
                        y, out = bank_y[b][:, 0:D].unsqueeze(1), y_out[turn % 2][:, place:place + 1, :]
                        if biased:
                            ins = dve.tensor_tensor(out, y, f["b_down"][:, bass.ds(expert, 1), :], ALU.add)
                        else:
                            ins = dve.tensor_copy(out, y)
                        ins.then_inc(S["y_ready"], 1)
                skewed(dve, N, 2, step, 2 * MOVED)


def combine(g, name, spec, f):
    nc = g.nc
    with ExitStack() as ctx:
        shared = SharedExpert(g, f"{name}_s1", ctx, spec, f, 1) if spec["shared"] else None
        rows = [g.sbuf(f"{name}_rows{k}", [P, GTILES, TOP_K, D], ctx=ctx) for k in range(2)]
        turn = Turn(g, name, ctx)
        group_slots = [g.sbuf(f"{name}_group_slots{k}", [P, TOP_K, GTILES], I32, ctx=ctx) for k in range(2)]
        slots_ready = g.sem(f"{name}_slots_ready")
        gathered, base = g.indirect_transfers()
        added = [g.sem(f"{name}_added{n}") for n in range(TOP_K)]
        with nc.Block() as block:

            @block.gpsimd
            def _(pool):
                def step(i, k):
                    s = 2 * i + k
                    turn(pool, s, (added[1], GTILES * (s - 1)), (slots_ready, s + 1))
                    for t in range(GTILES):
                        for n in range(TOP_K):
                            pool.indirect_dma_start(
                                out=rows[k][:, t, n, :], out_offset=None, in_=g.slots_y[:, :],
                                in_offset=bass.IndirectOffsetOnAxis(ap=group_slots[k][:, n, t:t + 1], axis=0))\
                                .then_inc(gathered[k], 16)
                skewed(pool, GROUPS, 0, step, peeled=2)

            if shared:
                @block.tensor
                def _(pe):
                    shared.tensor(pe)

                @block.scalar
                def _(act):
                    shared.scalar(act)

            @block.vector
            def _(dve):
                def step(i, k):
                    s = 2 * i + k
                    if live(s, GROUPS):
                        need(dve, gathered[k], base + 16 * TOP_K * GTILES * i)
                        dve.tensor_copy(group_slots[k][:], f["slots"][:, :, bass.ds(GTILES * s, GTILES)])\
                            .then_inc(slots_ready, 1)
                    m, b = s - 1, (k - 1) % 2
                    if not live(m, GROUPS):
                        return
                    if shared:
                        shared.vector(dve, m, b)
                    dve.wait_ge(gathered[b], base + 16 * TOP_K * GTILES * (i + (k - 1) // 2 + 1))
                    for n, weight in enumerate((f["weight0"], f["weight1"])):
                        if n:
                            dve.wait_ge(added[0], GTILES * (m + 1))
                        elif shared:
                            dve.wait_ge(shared.y_added, m + 1)
                        for t in range(GTILES):
                            x = g.X[:, GTILES * m + t, :]
                            dve.scalar_tensor_tensor(out=x, in0=rows[b][:, t, n, :],
                                                     scalar=weight[:, bass.ds(GTILES * m + t, 1)], in1=x,
                                                     op0=ALU.mult, op1=ALU.add).then_inc(added[n], 1)
                    dve.wait_ge(added[1], GTILES * (m + 1))
                    for t in range(GTILES):
                        dve.bn_stats(g.stats[:, GTILES * m + t, :], g.X[:, GTILES * m + t, :])
                skewed(dve, GROUPS, 1, step, peeled=2)


def ffn_phase(g, name, spec):
    with ExitStack() as ctx:
        E = spec["shared"] + EXPERTS
        f = {"pair": g.sbuf(f"{name}_weights", [P, TOP_K, TILES], ctx=ctx),
             "slots": g.sbuf(f"{name}_slots", [P, TOP_K, TILES], I32, ctx=ctx),
             "owner": g.sbuf(f"{name}_owner", [1, SLOT_TILES], I32, ctx=ctx),
             "w_up": g.sbuf(f"{name}_w_up", [D, E, FFN], ctx=ctx),
             "w_down": g.sbuf(f"{name}_w_down", [P, E, FT, D], ctx=ctx)}
        f["weight0"], f["weight1"] = f["pair"][:, 0, :], f["pair"][:, 1, :]
        if spec["b_up"]:
            f["b_up"] = g.sbuf(f"{name}_b_up", [P, EXPERTS, FFN], ctx=ctx)
            f["b_down"] = g.sbuf(f"{name}_b_down", [P, EXPERTS, D], ctx=ctx)
        if spec["shared"]:
            f["xnT"] = g.sbuf(f"{name}_xnT", [D, TOKENS], ctx=ctx)
        route(g, name, spec, f)
        dispatch(g, f"{name}_d", spec, f)
        run_experts(g, f"{name}_e", spec, f)
        combine(g, f"{name}_c", spec, f)


def ffn0(g):
    ffn_phase(g, "f0", dict(kind="sigmoid", plus_xn=True, zero_slots=True, shared=2, gelu=ACT.Gelu, gate_w="f0_gate_w",
                            gate_b="L0_ffn_routing_bias", w_up="f0_up", w_down="f0_down", b_up=None))


def ffn1(g):
    ffn_phase(g, "f1", dict(kind="softmax", plus_xn=False, zero_slots=False, shared=0, gelu=ACT.Gelu_apprx_tanh,
                            gate_w="L1_ffn_Wg", gate_b="L1_ffn_bg", w_up="f1_up", w_down="f1_down",
                            b_up="L1_ffn_b1", b_down="L1_ffn_b2"))


def xattn0(g):
    attention(g, "a0", False)


def xattn1(g):
    attention(g, "a1", True)


PHASES = (ssm_phase, xattn0, ffn0, retention_phase, xattn1, ffn1)


def launch_inputs(inputs):
    a = {k: np.ascontiguousarray(v) for k, v in inputs.items()}
    flip = lambda m: np.ascontiguousarray(m.T)
    out = {
        "x": a["x"].reshape(TOKENS, D),
        "ident": np.eye(P, dtype=np.float32),
        "time_row": np.tile(np.arange(SEQ, dtype=np.float32), (P, 1)),
        "ssm_b_re_im": flip(np.concatenate([a["L0_attn_B_real"], a["L0_attn_B_imag"]])),
        "ssm_b_im_re": flip(np.concatenate([a["L0_attn_B_imag"], a["L0_attn_B_real"]])),
        "ssm_c_re_im": np.concatenate([a["L0_attn_C_real"], a["L0_attn_C_imag"]], axis=1),
        "ssm_c_im_re": np.concatenate([a["L0_attn_C_imag"], a["L0_attn_C_real"]], axis=1),
        "ssm_w_out": flip(a["L0_attn_W_out"]),
        "L0_attn_log_Lam_real": a["L0_attn_log_Lam_real"].reshape(-1, 1),
        "L0_attn_Lam_imag": a["L0_attn_Lam_imag"].reshape(-1, 1),
        "L0_attn_log_dt": a["L0_attn_log_dt"].reshape(1, 1),
        "L0_attn_D": a["L0_attn_D"].reshape(-1, 1),
        "L0_attn_b_out": a["L0_attn_b_out"].reshape(1, -1),
        "ctxT": flip(a["ctx_1024"].reshape(TOKENS, D)).reshape(D, BATCH, SEQ),
        "ctx": a["ctx_1024"],
        "xa_wq": flip(a["L1_xattn_wq"]), "xa_wk": flip(a["L1_xattn_wk"]), "xa_wv": flip(a["L1_xattn_wv"]),
        "L1_xattn_bq": a["L1_xattn_bq"].reshape(-1, 1),
        "L1_xattn_bk": a["L1_xattn_bk"].reshape(-1, 1),
        "L1_xattn_bv": a["L1_xattn_bv"].reshape(1, -1),
        "rank": np.tile(np.arange(EXPERTS, 0, -1, dtype=np.float32), (P, 1)),
        "f0_gate_w": flip(a["L0_ffn_centroids"]),
        "L0_ffn_routing_bias": a["L0_ffn_routing_bias"].reshape(1, -1),
        "f0_up": np.concatenate([a["L0_ffn_Wfc_sh"], a["L0_ffn_Wfc_r"]]).transpose(2, 0, 1),
        "f0_down": np.concatenate([a["L0_ffn_Wproj_sh"], a["L0_ffn_Wproj_r"]])
        .reshape(-1, D, FT, P).transpose(3, 0, 2, 1),
        "L1_ffn_Wg": a["L1_ffn_Wg"], "L1_ffn_bg": a["L1_ffn_bg"].reshape(1, -1),
        "f1_up": a["L1_ffn_W1"].transpose(1, 0, 2),
        "f1_down": a["L1_ffn_W2"].reshape(EXPERTS, FT, P, D).transpose(2, 0, 1, 3),
        "L1_ffn_b1": a["L1_ffn_b1"], "L1_ffn_b2": a["L1_ffn_b2"],
        "before": np.triu(np.ones((P, P), np.float32), 1),
        "tile_starts": np.tile(P * np.arange(TILES, dtype=np.float32), (P, 1)),
        "tile_numbers": np.arange(SLOT_TILES, dtype=np.float32).reshape(1, -1),
        "ret_wqk": flip(np.concatenate([a["L1_attn_Wq"], a["L1_attn_Wk"]])),
        "ret_wv": flip(a["L1_attn_Wv"]).reshape(D, R_HEADS, R_VAL),
        "ret_wg": flip(a["L1_attn_Wg"]),
        "ret_wo": np.ascontiguousarray(a["L1_attn_Wo"].reshape(D, R_HEADS, R_VAL).transpose(2, 1, 0)),
        "ret_gn_w": flip(a["L1_attn_gn_weight"].reshape(R_HEADS, R_VAL)),
        "ret_gn_b": flip(a["L1_attn_gn_bias"].reshape(R_HEADS, R_VAL)),
    }
    out["ret_cos"], out["ret_sin"], out["ret_decay"] = retention_tables()
    return {k: np.ascontiguousarray(v) for k, v in out.items()}


def build(nc, dram, out):
    with ExitStack() as ctx:
        g = Program(nc, ctx, dram)
        for phase in PHASES:
            g.run(phase)
        stored = ctx.enter_context(nc.semaphore("stored"))
        with nc.Block() as block:

            @block.sync
            def _(sp):
                for i in range(4):
                    sp.dma_start(out.rearrange("(i p) d -> p i d", p=P)[:, 8 * i:8 * i + 8, :],
                                 g.X[:, 8 * i:8 * i + 8, :]).then_inc(stored, 16)
                sp.wait_ge(stored, 64)


def kernel(**inputs):
    import concourse.bacc as bacc
    from concourse.bass_utils import run_bass_kernel_spmd

    nc = bacc.Bacc("TRN2", target_bir_lowering=False, num_devices=1)
    arrays = launch_inputs(inputs)
    dram = {k: nc.dram_tensor(f"in_{k}", a.shape, mybir.dt.from_np(a.dtype), kind="ExternalInput").ap()
            for k, a in arrays.items()}
    out = nc.dram_tensor("out", (TOKENS, D), F32, kind="ExternalOutput").ap()
    build(nc, dram, out)
    result = run_bass_kernel_spmd(nc, [{f"in_{k}": a for k, a in arrays.items()}], core_ids=[0])
    return result.results[0]["out"].reshape(BATCH, SEQ, D)
```

```python
from contextlib import ExitStack
import math

import numpy as np
import concourse.bass as bass
from concourse import mybir

F32 = mybir.dt.float32
F32R = mybir.dt.float32r
I32 = mybir.dt.int32
ACT = mybir.ActivationFunctionType
ALU = mybir.AluOpType
AXIS = mybir.AxisListType

P = 128
D = 128
BATCH, SEQ = 64, 64
TOKENS = BATCH * SEQ
TILES = TOKENS // P
EPS = 1e-5


def need(eng, sem, value):
    if isinstance(value, int) and value <= 0:
        return
    eng.wait_ge(sem, value)


def skewed(eng, items, depth, step, unroll=2, peeled=1, between=None):
    for s in range(peeled * unroll):
        step(s // unroll, s % unroll)
    if between:
        between()
    with eng.Fori(peeled, items // unroll) as i:
        for k in range(unroll):
            step(i, k)
    for s in range(items, items + depth):
        step(s // unroll, s % unroll)


def live(m, items):
    return not isinstance(m, int) or 0 <= m < items


class Program:

    def __init__(self, nc, ctx, dram, out):
        self.nc, self.ctx, self.dram, self.out = nc, ctx, dram, out
        self.stored = ctx.enter_context(nc.semaphore("stored"))
        self.phase_ctx, self.phase_sems = None, []
        self.indirect_done = [ctx.enter_context(nc.semaphore(f"indirect_done{k}")) for k in range(2)]
        self.indirect_count = 0
        self.X = self.sbuf("X", [P, TILES, D])
        self.stats = self.sbuf("stats", [P, TILES, 6])
        self.mean = self.sbuf("mean", [P, TILES])
        self.rstd = self.sbuf("rstd", [P, TILES])
        self.var = self.sbuf("var", [P, TILES])
        self.minus_half = self.sbuf("minus_half", [P, TILES])
        self.ident = self.sbuf("ident", [P, P])
        self.kT = self.sbuf("kT", [D, TOKENS])
        self.v_twice = self.sbuf("v_twice", [P, BATCH, D])

    def sem(self, name):
        handle = self.phase_ctx.enter_context(self.nc.semaphore(name))
        self.phase_sems.append(handle.num)
        return handle

    def indirect_transfers(self, groups):
        before, self.indirect_count = self.indirect_count, self.indirect_count + 16 * TOP_K * GTILES * groups // 2
        return self.indirect_done, before

    def run(self, phase):
        self.phase_sems = []
        with ExitStack() as self.phase_ctx:
            phase(self)
        numbers = sorted(self.phase_sems)
        starts = [n for n in numbers if n - 1 not in numbers]
        ends = [n + 1 for n in numbers if n + 1 not in numbers]
        with self.nc.Block() as block:

            @block.sync
            def _(sp):
                for low, high in zip(starts, ends):
                    sp.sem_clear(range(low, high))

    def sbuf(self, name, shape, dt=F32, ctx=None):
        return (ctx or self.ctx).enter_context(self.nc.sbuf_tensor(name, shape, dt))

    def banks(self, name, ctx):
        return [ctx.enter_context(self.nc.psum_tensor(f"{name}_bank{b}", [P, 512], F32)) for b in range(8)]


FIRST = 8


def row_statistics(g, name, sync=None, vector=None, split=False):
    nc = g.nc
    with ExitStack() as ctx:
        diff = g.sbuf(f"{name}_ln_diff", [P, TILES], ctx=ctx)
        var, minus_half, now = g.var, g.minus_half, FIRST if split else TILES
        step = g.sem(f"{name}_ln_stat_step")
        var_ready = g.sem(f"{name}_ln_var_ready")
        filled = g.sem(f"{name}_ln_minus_half_filled")
        rstd_ready = g.sem(f"{name}_ln_rstd_ready")
        st = g.stats
        with nc.Block() as block:

            @block.vector
            def _(dve):
                dve.tensor_tensor(g.mean[:], st[:, :, 1], st[:, :, 4], ALU.add)
                dve.tensor_tensor(diff[:], st[:, :, 1], st[:, :, 4], ALU.subtract)
                dve.tensor_tensor(var[:], st[:, :, 2], st[:, :, 5], ALU.add).then_inc(step, 1)
                dve.wait_ge(step, 1)
                dve.tensor_scalar(g.mean[:], g.mean[:], 0.5, None, ALU.mult)
                dve.tensor_tensor(diff[:], diff[:], diff[:], ALU.mult)
                dve.tensor_scalar(var[:], var[:], 1.0 / D, EPS, ALU.mult, ALU.add).then_inc(step, 1)
                dve.wait_ge(step, 2)
                dve.scalar_tensor_tensor(out=var[:], in0=diff[:], scalar=0.25, in1=var[:],
                                         op0=ALU.mult, op1=ALU.add).then_inc(var_ready, 1)
                if vector:
                    vector(dve)

            if sync:
                @block.sync
                def _(sp):
                    sync(sp)

            @block.gpsimd
            def _(pool):
                pool.memset(minus_half[:], -0.5).then_inc(filled, 1)
                pool.wait_ge(filled, 1)
                pool.wait_ge(var_ready, 1)
                pool.tensor_tensor(g.rstd[:, 0:now], var[:, 0:now], minus_half[:, 0:now], ALU.pow)\
                    .then_inc(rstd_ready, 1)


def rest_of_rstd(g, pool, ready):
    pool.tensor_tensor(g.rstd[:, FIRST:TILES], g.var[:, FIRST:TILES], g.minus_half[:, FIRST:TILES], ALU.pow)\
        .then_inc(ready, 1)


GROUP = 4
GROUPS = TILES // GROUP
GT = GROUP * P
STATES = 64
TWO_PI_HI = 201.0 / 32.0
TWO_PI_LO = 2.0 * math.pi - TWO_PI_HI
TWO_PI_MID = float(np.float32(round(TWO_PI_LO * 2**21) / 2**21))
TWO_PI_END = TWO_PI_LO - TWO_PI_MID
ROUND_1 = 1.5 * 2**23
LN2_HI = 0.693359375
LN2_LO = math.log(2.0) - LN2_HI


def ssm_tables(g, t):
    nc, dram = g.nc, g.dram
    with ExitStack() as ctx:
        def sb(name, shape, dt=F32):
            return g.sbuf(f"ssm_{name}", shape, dt, ctx)

        log_lam, lam_im, log_dt = sb("log_lam", [P, 1]), sb("lam_im", [P, 1]), sb("log_dt", [P, 1])
        b_re_im, b_im_re = sb("b_re_im", [D, P]), sb("b_im_re", [D, P])
        c_re_im, c_im_re = sb("c_re_im", [D, P]), sb("c_im_re", [D, P])
        w_out, d_col = sb("w_out", [D, D]), sb("d_col", [D, 1])
        time_row = sb("time_row", [P, SEQ])
        dt, n, r, poly = sb("dt", [P, 1]), sb("n", [P, 1]), sb("r", [P, 1]), sb("poly", [P, 1])
        n_int = sb("n_int", [P, 1], I32)
        lam, mag = sb("lam", [P, 1]), sb("mag", [P, 1])
        theta, theta_hi, theta_lo = sb("theta", [P, 1]), sb("theta_hi", [P, 1]), sb("theta_lo", [P, 1])
        turn, ang, ang_lo, ang_cos = (sb(k, [P, SEQ]) for k in ("turn", "ang", "ang_lo", "ang_cos"))
        folded = [ctx.enter_context(nc.psum_tensor(f"ssm_folded{i}", [P, 512], F32)) for i in range(2)]
        loaded = g.sem("ssm_parameters_loaded")
        step = g.sem("ssm_table_step")
        lam_ready, arg_ready, mag_ready = g.sem("ssm_lam_ready"), g.sem("ssm_arg_ready"), g.sem("ssm_mag_ready")
        ang_ready, sin_ready = g.sem("ssm_angles_ready"), g.sem("ssm_sines_ready")
        c_ready, fold_done = g.sem("ssm_c_ready"), g.sem("ssm_fold_done")
        projection = ContextProjection(g, ctx)
        with nc.Block() as block:

            @block.sync
            def _(sp):
                def load_x():
                    for i in range(4):
                        sp.dma_start(g.X[:, 8 * i:8 * i + 8, :],
                                     dram["x"].rearrange("(i p) d -> p i d", p=P)[:, 8 * i:8 * i + 8, :])\
                            .then_inc(t["x_loaded"][i], 16)
                projection.sync(sp, load_x)

            @block.scalar
            def _(act):
                loads = [
                    (log_lam[0:STATES, :], dram["L0_attn_log_Lam_real"]),
                    (log_lam[STATES:P, :], dram["L0_attn_log_Lam_real"]),
                    (lam_im[0:STATES, :], dram["L0_attn_Lam_imag"]),
                    (lam_im[STATES:P, :], dram["L0_attn_Lam_imag"]),
                    (log_dt[:], dram["L0_attn_log_dt"].to_broadcast([P, 1])),
                    (b_re_im[:], dram["ssm_b_re_im"]), (b_im_re[:], dram["ssm_b_im_re"]),
                    (c_re_im[:], dram["ssm_c_re_im"]), (c_im_re[:], dram["ssm_c_im_re"]),
                    (w_out[:], dram["ssm_w_out"]), (d_col[:], dram["L0_attn_D"]),
                    (time_row[:], dram["time_row"]), (g.ident[:], dram["ident"]),
                    (t["b_out"][:], dram["L0_attn_b_out"].to_broadcast([P, D])),
                ]
                for dst, src in loads:
                    act.dma_start(dst, src).then_inc(loaded, 16)
                act.wait_ge(loaded, 16 * 14)
                nc.scalar.activation(lam[:], log_lam[:], ACT.Exp).then_inc(lam_ready, 1)
                projection.scalar(act)
                act.wait_ge(arg_ready, 1)
                nc.scalar.activation(mag[:], lam[:], ACT.Exp, scale=-1.0).then_inc(mag_ready, 1)
                act.wait_ge(ang_ready, 1)
                nc.scalar.activation(t["sin"][:], ang[:], ACT.Sin)
                nc.scalar.activation(t["cos"][:], ang_cos[:], ACT.Sin).then_inc(sin_ready, 1)

            @block.vector
            def _(dve):
                done = [0]

                def seq(ins):
                    done[0] += 1
                    ins.then_inc(step, 1)
                    dve.wait_ge(step, done[0])

                dve.wait_ge(loaded, 16 * 14)
                seq(dve.tensor_scalar(n[:], log_dt[:], 1.0 / math.log(2.0), ROUND_1, ALU.mult, ALU.add))
                seq(dve.tensor_scalar(n[:], n[:], ROUND_1, None, ALU.subtract))
                seq(dve.tensor_scalar(n[:], n[:], -126.0, 127.0, ALU.max, ALU.min))
                seq(dve.scalar_tensor_tensor(out=r[:], in0=n[:], scalar=-LN2_HI, in1=log_dt[:],
                                             op0=ALU.mult, op1=ALU.add))
                seq(dve.scalar_tensor_tensor(out=r[:], in0=n[:], scalar=-LN2_LO, in1=r[:],
                                             op0=ALU.mult, op1=ALU.add))
                seq(dve.tensor_scalar(poly[:], r[:], 1.0 / math.factorial(8), 1.0 / math.factorial(7),
                                      ALU.mult, ALU.add))
                for k in range(6, -1, -1):
                    seq(dve.tensor_scalar(poly[:], poly[:], r[:], 1.0 / math.factorial(k), ALU.mult, ALU.add))
                seq(dve.tensor_scalar(n[:], n[:], 127.0, 2.0**23, ALU.add, ALU.mult))
                seq(dve.tensor_copy(n_int[:], n[:]))
                seq(dve.tensor_tensor(dt[:], poly[:], n_int[:].bitcast(F32), ALU.mult))
                seq(dve.tensor_tensor(theta[:], lam_im[:], dt[:], ALU.mult))
                seq(dve.tensor_scalar(n[:], theta[:], 1.0 / (2 * math.pi), ROUND_1, ALU.mult, ALU.add))
                seq(dve.tensor_scalar(n[:], n[:], ROUND_1, None, ALU.subtract))
                for part in (TWO_PI_HI, TWO_PI_MID, TWO_PI_END):
                    seq(dve.scalar_tensor_tensor(out=theta[:], in0=n[:], scalar=-part, in1=theta[:],
                                                 op0=ALU.mult, op1=ALU.add))
                seq(dve.tensor_scalar(theta_hi[:], theta[:], 1.5 * 2**13, 1.5 * 2**13, ALU.add, ALU.subtract))
                seq(dve.tensor_tensor(theta_lo[:], theta[:], theta_hi[:], ALU.subtract))
                seq(dve.tensor_scalar(turn[:], time_row[:], theta[:], 1.0 / (2 * math.pi), ALU.mult, ALU.mult))
                seq(dve.tensor_scalar(turn[:], turn[:], ROUND_1, ROUND_1, ALU.add, ALU.subtract))
                seq(dve.tensor_scalar(ang[:], time_row[:], theta_hi[:], None, ALU.mult))
                seq(dve.tensor_scalar(ang_lo[:], time_row[:], theta_lo[:], None, ALU.mult))
                seq(dve.scalar_tensor_tensor(out=ang[:], in0=turn[:], scalar=-TWO_PI_HI, in1=ang[:],
                                             op0=ALU.mult, op1=ALU.add))
                seq(dve.scalar_tensor_tensor(out=ang[:], in0=turn[:], scalar=-TWO_PI_LO, in1=ang[:],
                                             op0=ALU.mult, op1=ALU.add))
                seq(dve.tensor_tensor(ang[:], ang[:], ang_lo[:], ALU.add))
                seq(dve.tensor_scalar(ang_cos[:], ang[:], math.pi / 2, -2 * math.pi, ALU.is_gt, ALU.mult))
                seq(dve.scalar_tensor_tensor(out=ang_cos[:], in0=ang[:], scalar=math.pi / 2, in1=ang_cos[:],
                                             op0=ALU.add, op1=ALU.add))
                top = 3.1415925
                seq(dve.tensor_scalar(ang[:], ang[:], -top, top, ALU.max, ALU.min))
                seq(dve.tensor_scalar(ang_cos[:], ang_cos[:], -top, top, ALU.max, ALU.min))
                dve.tensor_copy(turn[:], turn[:]).then_inc(ang_ready, 1)
                seq(dve.tensor_scalar(t["u_cos"][:], b_re_im[:], dt[:], None, ALU.mult))
                seq(dve.tensor_scalar(t["u_sin"][:], b_im_re[:], dt[:], None, ALU.mult))
                seq(dve.tensor_scalar(c_re_im[:, STATES:P], c_re_im[:, STATES:P], -1.0, None, ALU.mult))
                dve.tensor_scalar(c_im_re[:, 0:STATES], c_im_re[:, 0:STATES], -1.0, None, ALU.mult)\
                    .then_inc(c_ready, 1)
                seq(dve.tensor_scalar(t["w_skip"][:], w_out[:], d_col[:], None, ALU.mult))
                for i in range(TILES):
                    if i % 8 == 0:
                        dve.wait_ge(t["x_loaded"][i // 8], 16)
                    dve.bn_stats(g.stats[:, i, :], g.X[:, i, :])
                dve.wait_ge(fold_done, 1)
                dve.tensor_copy(t["w_cos"][:], folded[0][:, 0:D])
                seq(dve.tensor_copy(t["w_sin"][:], folded[1][:, 0:D]))
                dve.wait_ge(lam_ready, 1)
                dve.tensor_tensor(lam[:], lam[:], dt[:], ALU.mult).then_inc(arg_ready, 1)
                seq(dve.memset(t["decay"][:], 0.0))
                dve.wait_ge(mag_ready, 1)
                dve.tensor_scalar(t["decay"][:, :, 1:SEQ], t["decay"][:, :, 1:SEQ], mag[:], None, ALU.add)
                dve.wait_ge(sin_ready, 1)
                seq(dve.tensor_scalar(t["sin"][STATES:P, :], t["sin"][STATES:P, :], -1.0, None, ALU.mult))

            @block.tensor
            def _(pe):
                def fold():
                    pe.wait_ge(loaded, 16 * 14)
                    pe.wait_ge(c_ready, 1)
                    pe.matmul(folded[0][:, 0:D], c_re_im[:], w_out[:], start=True, stop=True)
                    pe.matmul(folded[1][:, 0:D], c_im_re[:], w_out[:], start=True, stop=True).then_inc(fold_done, 1)
                projection.tensor(pe, fold)


def ssm_phase(g):
    nc = g.nc
    with ExitStack() as ctx:
        def sb(name, shape):
            return g.sbuf(f"ssm_{name}", shape, ctx=ctx)

        t = {"x_loaded": [g.sem(f"x_loaded{i}") for i in range(4)]}
        for name, shape in (("cos", [P, SEQ]), ("sin", [P, SEQ]), ("decay", [P, GT // SEQ, SEQ]),
                            ("u_cos", [D, P]), ("u_sin", [D, P]), ("w_cos", [P, D]), ("w_sin", [P, D]),
                            ("w_skip", [D, D]), ("b_out", [P, D])):
            t[name] = sb(name, shape)
        ssm_tables(g, t)
        row_statistics(g, "ssm", split=True)
        xn = [sb(f"xn{k}", [P, GROUP, D]) for k in range(2)]
        xnT = [sb(f"xnT{k}", [D, GT]) for k in range(3)]
        part_cos = [sb(f"part_cos{k}", [P, GT]) for k in range(2)]
        part_sin = [sb(f"part_sin{k}", [P, GT]) for k in range(2)]
        z = [sb(f"z{k}", [P, GT]) for k in range(2)]
        z_cos = [sb(f"z_cos{k}", [P, GT]) for k in range(2)]
        z_sin = [sb(f"z_sin{k}", [P, GT]) for k in range(2)]
        banks = g.banks("ssm", ctx)
        bank_t, bank_uc, bank_us, bank_o = banks[0:2], banks[2:4], banks[4:6], banks[6:8]
        names = ("rstd_ready", "xn_ready", "xnT_in_psum", "xnT_ready", "inputs_in_psum", "parts_ready", "drive_ready",
                 "z_ready", "z_cos_ready", "z_sin_ready", "out_in_psum", "bias_added", "x_updated")
        S = {k: g.sem(f"ssm_{k}") for k in names}
        batch = lambda ap: ap.rearrange("p (b t) -> p b t", t=SEQ)
        over = lambda ap: ap.unsqueeze(1).to_broadcast([P, GT // SEQ, SEQ])
        N = GROUPS
        with nc.Block() as block:

            @block.vector
            def _(dve):
                def layernorm(s):
                    if GROUP * s == FIRST:
                        dve.wait_ge(S["rstd_ready"], 1)
                    need(dve, S["xnT_in_psum"], s - 1)
                    for j in range(GROUP):
                        i = GROUP * s + j
                        last = dve.tensor_scalar(xn[s % 2][:, j, :], g.X[:, i, :], g.mean[:, i:i + 1],
                                                 g.rstd[:, i:i + 1], ALU.subtract, ALU.mult)
                    last.then_inc(S["xn_ready"], 1)
                layernorm(0)
                for s in range(N + 2):
                    m = s - 1
                    if 0 <= m < N:
                        dve.wait_ge(S["drive_ready"], m + 1)
                        need(dve, S["z_sin_ready"], m - 1)
                        dve.tensor_tensor_scan(z[m % 2][:], t["decay"][:].rearrange("p b t -> p (b t)"),
                                               part_cos[m % 2][:], 0.0, ALU.mult, ALU.add)\
                            .then_inc(S["z_ready"], 1)
                        dve.wait_ge(S["z_ready"], m + 1)
                        need(dve, S["out_in_psum"], m - 1)
                        dve.tensor_tensor(batch(z_cos[m % 2][:]), batch(z[m % 2][:]), over(t["cos"][:]),
                                          ALU.mult).then_inc(S["z_cos_ready"], 1)
                    if s + 1 < N:
                        layernorm(s + 1)
                    if s < N:
                        dve.wait_ge(S["inputs_in_psum"], s + 1)
                        need(dve, S["z_ready"], s - 1)
                        dve.tensor_tensor(batch(part_cos[s % 2][:]), batch(bank_uc[s % 2][:]), over(t["cos"][:]),
                                          ALU.mult)
                        dve.tensor_tensor(batch(part_sin[s % 2][:]), batch(bank_us[s % 2][:]), over(t["sin"][:]),
                                          ALU.mult).then_inc(S["parts_ready"], 1)
                    m = s - 2
                    if 0 <= m < N:
                        dve.wait_ge(S["out_in_psum"], m + 1)
                        dve.wait_ge(S["bias_added"], m + 1)
                        tiles = g.X[:, GROUP * m:GROUP * m + GROUP, :]
                        dve.tensor_tensor(tiles, bank_o[m % 2][:].rearrange("p (j d) -> p j d", d=D), tiles,
                                          ALU.add).then_inc(S["x_updated"], 1)
                        dve.wait_ge(S["x_updated"], m + 1)
                        for i in range(GROUP * m, GROUP * m + GROUP):
                            dve.bn_stats(g.stats[:, i, :], g.X[:, i, :])

            @block.gpsimd
            def _(pool):
                rest_of_rstd(g, pool, S["rstd_ready"])
                for s in range(N + 1):
                    m = s - 1
                    if 0 <= m < N:
                        pool.wait_ge(S["z_ready"], m + 1)
                        need(pool, S["out_in_psum"], m - 1)
                        pool.tensor_tensor(batch(z_sin[m % 2][:]), batch(z[m % 2][:]), over(t["sin"][:]),
                                           ALU.mult).then_inc(S["z_sin_ready"], 1)
                    if s < N:
                        pool.wait_ge(S["parts_ready"], s + 1)
                        pool.tensor_tensor(part_cos[s % 2][:], part_cos[s % 2][:], part_sin[s % 2][:], ALU.add)\
                            .then_inc(S["drive_ready"], 1)
                        tiles = g.X[:, GROUP * s:GROUP * s + GROUP, :]
                        pool.tensor_tensor(tiles, tiles, t["b_out"][:].unsqueeze(1).to_broadcast([P, GROUP, D]),
                                           ALU.add).then_inc(S["bias_added"], 1)

            @block.scalar
            def _(act):
                for s in range(N):
                    act.wait_ge(S["xnT_in_psum"], s + 1)
                    need(act, S["out_in_psum"], s - 2)
                    nc.scalar.activation(xnT[s % 3][:], bank_t[s % 2][:], ACT.Copy).then_inc(S["xnT_ready"], 1)

            @block.tensor
            def _(pe):
                def transpose(s):
                    pe.wait_ge(S["xn_ready"], s + 1)
                    need(pe, S["xnT_ready"], s - 1)
                    for j in range(GROUP):
                        last = pe.transpose(bank_t[s % 2][:, j * P:(j + 1) * P], xn[s % 2][:, j, :], g.ident[:])
                    last.then_inc(S["xnT_in_psum"], 1)
                transpose(0)
                for s in range(N + 2):
                    m = s - 2
                    if 0 <= m < N:
                        pe.wait_ge(S["z_cos_ready"], m + 1)
                        pe.wait_ge(S["z_sin_ready"], m + 1)
                        need(pe, S["x_updated"], m - 1)
                        for j in range(GROUP):
                            cols = slice(j * P, (j + 1) * P)
                            out = bank_o[m % 2][:, cols]
                            pe.matmul(out, z_cos[m % 2][:, cols], t["w_cos"][:], start=True, stop=False)
                            pe.matmul(out, z_sin[m % 2][:, cols], t["w_sin"][:], start=False, stop=False)
                            last = pe.matmul(out, xnT[m % 3][:, cols], t["w_skip"][:], start=False, stop=True)
                        last.then_inc(S["out_in_psum"], 1)
                    if s < N:
                        pe.wait_ge(S["xnT_ready"], s + 1)
                        need(pe, S["parts_ready"], s - 1)
                        pe.matmul(bank_uc[s % 2][:], t["u_cos"][:], xnT[s % 3][:], start=True, stop=True)
                        pe.matmul(bank_us[s % 2][:], t["u_sin"][:], xnT[s % 3][:], start=True, stop=True)\
                            .then_inc(S["inputs_in_psum"], 1)
                    if s + 1 < N:
                        transpose(s + 1)


HEADS, HEAD = 16, 8
QUAD = 4
QUADS = BATCH // QUAD
QKEYS = QUAD * SEQ
OCT = 8
OCTS = BATCH // OCT
OKEYS = OCT * SEQ
OTILES = OKEYS // P


class ContextProjection:

    def __init__(self, g, ctx):
        self.g = g
        self.ctxT = [g.sbuf(f"kv_ctxT{k}", [D, OCT, SEQ], ctx=ctx) for k in range(2)]
        self.wk, self.wv = g.sbuf("kv_wk", [D, D], ctx=ctx), g.sbuf("kv_wv", [D, D], ctx=ctx)
        self.bk = g.sbuf("kv_bk", [D, 1], ctx=ctx)
        self.bank_k = [ctx.enter_context(g.nc.psum_tensor(f"kv_k_psum{k}", [P, 512], F32)) for k in range(2)]
        self.bank_v = [ctx.enter_context(g.nc.psum_tensor(f"kv_v_psum{k}", [P, QUAD, D], F32)) for k in range(2)]
        self.weights = g.sem("kv_weights_loaded")
        self.loaded = [g.sem(f"kv_context_loaded{k}") for k in range(2)]
        self.done, self.copied = g.sem("kv_products_done"), g.sem("kv_copied")

    def sync(self, sp, between):
        dram = self.g.dram
        for dst, src in ((self.wk, "xa_wk"), (self.wv, "xa_wv"), (self.bk, "L1_xattn_bk")):
            sp.dma_start(dst[:], dram[src]).then_inc(self.weights, 16)

        def step(i, k):
            s = 2 * i + k
            need(sp, self.done, 2 * (s - 1))
            sp.dma_start(self.ctxT[k][:], dram["ctxT"][:, bass.ds(s * OCT, OCT), :]).then_inc(self.loaded[k], 16)
        skewed(sp, OCTS, 0, step, between=between)

    def tensor(self, pe, between):
        pe.wait_ge(self.weights, 48)

        def step(i, k):
            s = 4 * i + k
            octet, row = k // 2, k % 2 * QUAD
            pe.wait_ge(self.loaded[octet], 16 * (i + 1))
            need(pe, self.copied, s - 1)
            pe.matmul(self.bank_k[k % 2][:, 0:QKEYS], self.wk[:], self.ctxT[octet][:, row:row + QUAD, :],
                      start=True, stop=True)
            for b in range(QUAD):
                for half in range(2):
                    last = pe.matmul(self.bank_v[k % 2][64 * half:64 * half + 64, b, :],
                                     self.ctxT[octet][:, row + b, :], self.wv[:], start=True, stop=True)
            last.then_inc(self.done, 1)
        skewed(pe, QUADS, 0, step, 4, peeled=2, between=between)

    def scalar(self, act):
        act.wait_ge(self.weights, 48)
        g = self.g

        def step(i, k):
            s = 2 * i + k
            act.wait_ge(self.done, s + 1)
            g.nc.scalar.activation(g.kT[:, bass.ds(s * QKEYS, QKEYS)], self.bank_k[k][:, 0:QKEYS], ACT.Identity,
                                   bias=self.bk[:])
            g.nc.scalar.activation(g.v_twice[:, bass.ds(s * QUAD, QUAD), :], self.bank_v[k][:], ACT.Copy)\
                .then_inc(self.copied, 1)
        skewed(act, QUADS, 0, step)


def attention(g, name, projected):
    nc, dram, kT, v_twice = g.nc, g.dram, g.kT, g.v_twice
    with ExitStack() as ctx:
        def sb(n, shape):
            return g.sbuf(f"{name}_{n}", shape, ctx=ctx)

        if projected:
            wq, bq, bv = sb("wq", [D, D]), sb("bq", [D, 1]), sb("bv", [P, D])
            q = [sb(f"q{k}", [D, P]) for k in range(2)]
        else:
            v_rows = [sb(f"v_rows{k}", [P, OCT, D]) for k in range(2)]
        xn = [sb(f"xn{k}", [P, D]) for k in range(2)]
        xnT = [sb(f"xnT{k}", [D, P]) for k in range(2)]
        qT = q if projected else xnT
        k_diag = [sb(f"k_diag{k}", [D, HEADS, OCT, SEQ]) for k in range(2)]
        v_diag = [sb(f"v_diag{k}", [P, OCT, HEADS // 2, 2, HEAD + 1]) for k in range(2)]
        top = [sb(f"top{k}", [P, HEADS]) for k in range(2)]
        prob = [sb(f"prob{k}", [P, HEADS, SEQ]) for k in range(2)]
        probT = [sb(f"probT{k}", [P, HEADS // 2, P]) for k in range(2)]
        ones = sb("ones", [P, OCT, HEADS // 2, HEAD])
        recip = sb("recip", [P, HEADS])
        mixed = sb("mixed", [P, HEADS, HEAD])
        bank_s = [ctx.enter_context(nc.psum_tensor(f"{name}_scores{k}", [P, HEADS, SEQ], F32)) for k in range(2)]
        bank_t = ctx.enter_context(nc.psum_tensor(f"{name}_probT_psum", [P, HEADS // 2, P], F32))
        bank_o = ctx.enter_context(nc.psum_tensor(f"{name}_mixed_psum", [P, 512], F32))
        bank_x = ctx.enter_context(nc.psum_tensor(f"{name}_xT_psum", [P, 512], F32))
        names = ("weights_loaded", "first_cleared", "second_cleared", "v_cleared", "ones_set", "xn_ready",
                 "xnT_in_psum", "xnT_ready", "q_in_psum",
                 "q_ready", "scores_in_psum", "top_ready", "shifted", "exp_ready", "probT_in_psum",
                 "probT_ready", "mixed_in_psum", "recip_ready", "mixed_ready", "x_updated", "v_diag_ready",
                 "bias_added")
        S = {k: g.sem(f"{name}_{k}") for k in names}
        k_loaded = [g.sem(f"{name}_k_loaded{k}") for k in range(2)]
        v_loaded = [g.sem(f"{name}_v_loaded{k}") for k in range(2)]
        q_ready = S["q_ready"] if projected else S["xnT_ready"]
        N, UNROLL = TILES, 2 * OTILES

        CLEARED = 4

        def load_keys(sp, k, j, h):
            rows = slice(h * HEAD, (h + 1) * HEAD)
            if projected:
                src = kT[rows, bass.ds(j * OKEYS, OKEYS)].rearrange("p (b t) -> p b t", t=SEQ)
            else:
                src = dram["ctxT"][rows, bass.ds(j * OCT, OCT), :]
            sp.dma_start(k_diag[k][rows, h, :, :], src).then_inc(k_loaded[k], 16)

        def clear_first(dve):
            for h in range(0, HEADS, CLEARED):
                dve.memset(k_diag[0][:, h:h + CLEARED, :, :], 0.0).then_inc(S["first_cleared"], 1)

        def load_first(sp):
            for h in range(HEADS):
                sp.wait_ge(S["first_cleared"], h // CLEARED + 1)
                load_keys(sp, 0, 0, h)

        row_statistics(g, name, load_first, clear_first)
        with nc.Block() as block:

            @block.sync
            def _(sp):
                if projected:
                    for dst, src in ((wq[:], dram["xa_wq"]), (bq[:], dram["L1_xattn_bq"]),
                                     (bv[:], dram["L1_xattn_bv"].to_broadcast([P, D]))):
                        sp.dma_start(dst, src).then_inc(S["weights_loaded"], 16)
                def step(i, k):
                    j = 2 * i + k
                    if isinstance(j, int) and j == 1:
                        sp.wait_ge(S["second_cleared"], 1)
                    need(sp, S["scores_in_psum"], OTILES * (j - 1))
                    if not (isinstance(j, int) and j == 0):
                        for h in range(HEADS):
                            load_keys(sp, k, j, h)
                    if not projected:
                        need(sp, S["v_diag_ready"], j - 1)
                        for half in range(2):
                            sp.dma_start(v_rows[k][half * SEQ:(half + 1) * SEQ, :, :],
                                         dram["ctx"].rearrange("b t d -> t b d")[:, bass.ds(j * OCT, OCT), :])\
                                .then_inc(v_loaded[k], 16)
                skewed(sp, OCTS, 0, step)

            @block.gpsimd
            def _(pool):
                for k in range(2):
                    pool.memset(v_diag[k][:], 0.0).then_inc(S["v_cleared"], 1)
                pool.memset(ones[:], 1.0).then_inc(S["v_cleared"], 1)
                pool.wait_ge(S["v_cleared"], 3)
                for k in range(2):
                    for half in range(2):
                        pool.memset(v_diag[k][half * SEQ:(half + 1) * SEQ, :, :, half, HEAD:HEAD + 1], 1.0)\
                            .then_inc(S["ones_set"], 1)
                pool.wait_ge(S["ones_set"], 4)
                pool.memset(k_diag[1][:], 0.0).then_inc(S["second_cleared"], 1)
                pool.wait_ge(S["second_cleared"], 1)
                if projected:
                    pool.wait_ge(S["weights_loaded"], 48)

                def step(i, k):
                    j = 2 * i + k
                    need(pool, S["mixed_in_psum"], OTILES * (j - 1))
                    if not projected:
                        pool.wait_ge(v_loaded[k], 32 * (i + 1))
                    else:
                        need(pool, S["bias_added"], OTILES * j)
                    for half in range(2):
                        rows = slice(half * SEQ, (half + 1) * SEQ)
                        src = v_twice[rows, bass.ds(j * OCT, OCT), :] if projected else v_rows[k][rows, :, :]
                        src = src.rearrange("p b (h c d) -> p b h c d", c=2, d=HEAD)[:, :, :, half, :]
                        last = pool.tensor_tensor(v_diag[k][rows, :, :, half, 0:HEAD], src,
                                                  ones[rows, :, :, :], ALU.mult)
                    last.then_inc(S["v_diag_ready"], 1)
                    if projected:
                        pool.wait_ge(S["v_diag_ready"], j + 1)
                        for m in [OTILES * j + t for t in range(OTILES)]:
                            pool.wait_ge(S["xn_ready"], m + 1)
                            pool.tensor_tensor(g.X[:, m, :], g.X[:, m, :], bv[:], ALU.add)\
                                .then_inc(S["bias_added"], 1)
                skewed(pool, OCTS, 0, step)

            @block.vector
            def _(dve):
                def step(i, k):
                    s = UNROLL * i + k
                    m = s - 5
                    if live(m, N):
                        dve.wait_ge(S["mixed_in_psum"], m + 1)
                        need(dve, S["mixed_ready"], m)
                        out = bank_o[:, 0:HEADS * (HEAD + 1)].rearrange("p (h c) -> p h c", c=HEAD + 1)
                        dve.reciprocal(recip[:], out[:, :, HEAD]).then_inc(S["recip_ready"], 1)
                        dve.wait_ge(S["recip_ready"], m + 1)
                        need(dve, S["x_updated"], m)
                        dve.tensor_tensor(mixed[:], out[:, :, 0:HEAD],
                                          recip[:].unsqueeze(2).to_broadcast([P, HEADS, HEAD]), ALU.mult)\
                            .then_inc(S["mixed_ready"], 1)
                        dve.wait_ge(S["mixed_ready"], m + 1)
                        if projected:
                            dve.wait_ge(S["bias_added"], m + 1)
                        dve.tensor_tensor(g.X[:, m, :], g.X[:, m, :], mixed[:].rearrange("p h c -> p (h c)"),
                                          ALU.add).then_inc(S["x_updated"], 1)
                    if live(s, N):
                        need(dve, S["xnT_in_psum"], s - 1)
                        dve.tensor_scalar(xn[k % 2][:], g.X[:, s, :], g.mean[:, bass.ds(s, 1)],
                                          g.rstd[:, bass.ds(s, 1)], ALU.subtract, ALU.mult)\
                            .then_inc(S["xn_ready"], 1)
                    m, b = s - 2, (k - 2) % 2
                    if live(m, N):
                        dve.wait_ge(S["scores_in_psum"], m + 1)
                        need(dve, S["shifted"], m - 1)
                        dve.tensor_reduce(top[b][:], bank_s[b][:], AXIS.X, ALU.max).then_inc(S["top_ready"], 1)
                        dve.wait_ge(S["top_ready"], m + 1)
                        need(dve, S["probT_in_psum"], m - 1)
                        dve.tensor_tensor(prob[b][:], bank_s[b][:],
                                          top[b][:].unsqueeze(2).to_broadcast([P, HEADS, SEQ]), ALU.subtract)\
                            .then_inc(S["shifted"], 1)
                    m = s - 5
                    if live(m, N):
                        dve.wait_ge(S["x_updated"], m + 1)
                        dve.bn_stats(g.stats[:, m, :], g.X[:, m, :])
                skewed(dve, N, 5, step, UNROLL)

            @block.scalar
            def _(act):
                if projected:
                    act.wait_ge(S["weights_loaded"], 48)

                def step(i, k):
                    s = UNROLL * i + k
                    if live(s, N):
                        act.wait_ge(S["xnT_in_psum"], s + 1)
                        need(act, S["q_in_psum"] if projected else S["scores_in_psum"], s - 1)
                        nc.scalar.activation(xnT[k % 2][:], bank_x[:, 0:P], ACT.Copy).then_inc(S["xnT_ready"], 1)
                    if projected and live(s, N):
                        act.wait_ge(S["q_in_psum"], s + 1)
                        need(act, S["scores_in_psum"], s - 1)
                        nc.scalar.activation(qT[k % 2][:], bank_x[:, P:2 * P], ACT.Identity, bias=bq[:])\
                            .then_inc(S["q_ready"], 1)
                    m = s - 2
                    if live(m, N):
                        act.wait_ge(S["probT_in_psum"], m + 1)
                        need(act, S["mixed_in_psum"], m - 1)
                        nc.scalar.activation(probT[k % 2][:], bank_t[:], ACT.Copy).then_inc(S["probT_ready"], 1)
                    m, b = s - 1, (k - 1) % 2
                    if live(m, N):
                        act.wait_ge(S["shifted"], m + 1)
                        nc.scalar.activation(prob[b][:], prob[b][:], ACT.Exp, scale=1.0 / math.sqrt(HEAD))\
                            .then_inc(S["exp_ready"], 1)
                skewed(act, N, 2, step, UNROLL)

            @block.tensor
            def _(pe):
                pe.wait_ge(S["ones_set"], 4)
                if projected:
                    pe.wait_ge(S["weights_loaded"], 48)

                def step(i, k):
                    s = UNROLL * i + k
                    if live(s, N):
                        pe.wait_ge(S["xn_ready"], s + 1)
                        need(pe, q_ready, s)
                        pe.transpose(bank_x[:, 0:P], xn[k % 2][:], g.ident[:]).then_inc(S["xnT_in_psum"], 1)
                    m, b = s - 1, (k - 1) % 2
                    if live(m, N):
                        octet = ((k - 1) // OTILES) % 2
                        pe.wait_ge(k_loaded[octet], 16 * HEADS * (i + (k - 1) // UNROLL + 1))
                        pe.wait_ge(q_ready, m + 1)
                        need(pe, S["shifted"], m - 1)
                        for row in range(2):
                            for half in range(2):
                                heads = slice(8 * half, 8 * half + 8)
                                last = pe.matmul(bank_s[b][64 * row:64 * row + 64, heads, :],
                                                 qT[b][:, 64 * row:64 * row + 64],
                                                 k_diag[octet][:, heads, 2 * ((k - 1) % OTILES) + row, :], start=True, stop=True)
                        last.then_inc(S["scores_in_psum"], 1)
                    if projected and live(s, N):
                        pe.wait_ge(S["xnT_ready"], s + 1)
                        pe.matmul(bank_x[:, P:2 * P], wq[:], xnT[k % 2][:], start=True, stop=True)\
                            .then_inc(S["q_in_psum"], 1)
                    m, b = s - 2, (k - 2) % 2
                    if live(m, N):
                        pe.wait_ge(S["exp_ready"], m + 1)
                        need(pe, S["probT_ready"], m)
                        for hp in range(HEADS // 2):
                            last = pe.transpose(bank_t[:, hp, :],
                                                prob[b][:, 2 * hp:2 * hp + 2, :].rearrange("p h t -> p (h t)"),
                                                g.ident[:])
                        last.then_inc(S["probT_in_psum"], 1)
                    m, b = s - 3, (k - 3) % 2
                    if live(m, N):
                        octet = ((k - 3) // OTILES) % 2
                        pe.wait_ge(S["probT_ready"], m + 1)
                        pe.wait_ge(S["v_diag_ready"], 2 * i + (k - 3) // OTILES + 1)
                        need(pe, S["mixed_ready"], m)
                        for hp in range(HEADS // 2):
                            for row in range(2):
                                last = pe.matmul(
                                    bank_o[64 * row:64 * row + 64, 18 * hp:18 * hp + 18],
                                    probT[b][:, hp, 64 * row:64 * row + 64],
                                    v_diag[octet][:, 2 * ((k - 3) % OTILES) + row, hp, :, :].rearrange("p c d -> p (c d)"),
                                    start=True, stop=True)
                        last.then_inc(S["mixed_in_psum"], 1)
                skewed(pe, N, 3, step, UNROLL)


R_HEADS, R_KEY, R_VAL = 8, 64, 128


def retention_tables():
    freq = 1.0 / 10000.0 ** (np.arange(0, R_KEY, 2, dtype=np.float32) / np.float32(R_KEY))
    angle = (np.arange(P) % SEQ).astype(np.float32)[:, None] * freq[None, :].astype(np.float32)
    cos, sin = np.cos(angle.astype(np.float64)), np.sin(angle.astype(np.float64))
    gamma = 1.0 - np.exp2(-5.0 - np.arange(R_HEADS))
    rel = np.arange(SEQ)[None, :] - np.arange(SEQ)[:, None]
    decay = np.where(rel >= 0, gamma[:, None, None] ** np.maximum(rel, 0), 0.0) * R_KEY ** -0.5
    decay = np.tile(decay.transpose(1, 0, 2), (2, 1, 1))
    return (np.concatenate([cos, cos], 1).astype(np.float32), np.concatenate([-sin, sin], 1).astype(np.float32),
            decay.astype(np.float32))


def retention_phase(g):
    nc, dram = g.nc, g.dram
    with ExitStack() as ctx:
        def sb(n, shape):
            return g.sbuf(f"ret_{n}", shape, ctx=ctx)

        def ring(n, shape, size=2):
            return [sb(f"{n}{k}", shape) for k in range(size)]

        H, HP, W = R_HEADS, R_HEADS // 2, R_HEADS * R_VAL
        wqk, wv, wg = sb("wqk", [D, 1024]), sb("wv", [D, H, R_VAL]), sb("wg", [D, W])
        wo = sb("wo", [R_VAL, H, D])
        cos, sin, decay = sb("cos", [P, R_KEY]), sb("sin", [P, R_KEY]), sb("decay", [P, H, SEQ])
        gn_w, gn_b = sb("gn_w", [R_VAL, H]), sb("gn_b", [R_VAL, H])
        wv_mean = sb("wv_mean", [D, H])
        (wqk_high, wqk_low), (wv_high, wv_low) = (
            [g.sbuf(f"ret_{n}_{part}", [D, 1024], F32R, ctx=ctx) for part in ("high", "low")] for n in ("wqk", "wv"))
        x_high, x_low = ([g.sbuf(f"ret_x_{part}{k}", [D, P], F32R, ctx=ctx) for k in range(2)]
                         for part in ("high", "low"))
        xn, xnT = ring("xn", [P, D]), ring("xnT", [D, P], 4)
        qk, turned = ring("qk", [P, 2, H, R_KEY]), ring("turned", [P, 2, H, R_KEY])
        q_diag, kT = ring("q_diag", [P, HP, 2, 2, SEQ]), ring("kT", [P, HP, P])
        v = ring("v", [P, H, R_VAL])
        s_diag = ring("s_diag", [P, H, 2, SEQ])
        square, normed = sb("square", [P, H, R_VAL]), ring("normed", [P, H, R_VAL])
        var, rstd = ring("var", [P, H]), ring("rstd", [P, H])
        minus_half = sb("minus_half", [P, H])
        gate, gated = ring("gate", [R_VAL, H, P]), ring("gated", [R_VAL, H, P])
        ps_qk, ps_vg, ps_t, ps_o = (ctx.enter_context(nc.psum_tensor(f"ret_ps{k}", [P, 1024], F32))
                                    for k in range(4))
        names = ("loaded", "cleared", "wv_step", "wv_ready", "xn_ready", "xnT_in_psum", "xnT_ready", "high_ready",
                 "low_ready", "wqk_high_ready", "wv_high_ready", "w_low_ready", "qk_in_psum",
                 "turned_ready", "qk_ready", "qkT_in_psum", "q_diag_ready", "kT_ready", "scores_in_psum",
                 "s_ready", "v_in_psum", "v_ready", "gate_in_psum", "gate_ready", "mixed_in_psum", "square_ready",
                 "sum_ready", "var_ready", "rstd_ready", "normed_ready", "normedT_in_psum",
                 "affine_dve", "affine_act", "gated_ready", "out_in_psum", "x_updated", "half_set", "all_rstd_ready")
        S = {k: g.sem(f"ret_{k}") for k in names}
        N, UNROLL = TILES, 4
        DVE_HEADS = H // 2
        heads = lambda ap: ap.rearrange("p (h c) -> p h c", c=R_VAL)

        def load(sp):
            for dst, src in ((wv, "ret_wv"), (wqk, "ret_wqk"), (cos, "ret_cos"), (sin, "ret_sin"),
                             (decay, "ret_decay"), (wg, "ret_wg"), (wo, "ret_wo"), (gn_w, "ret_gn_w"),
                             (gn_b, "ret_gn_b")):
                sp.dma_start(dst[:], dram[src]).then_inc(S["loaded"], 16)

        row_statistics(g, "ret", load, split=True)
        with nc.Block() as block:

            @block.gpsimd
            def _(pool):
                for k in range(2):
                    pool.memset(q_diag[k][:], 0.0).then_inc(S["cleared"], 1)
                    pool.memset(s_diag[k][:], 0.0).then_inc(S["cleared"], 1)
                pool.memset(minus_half[:], -0.5).then_inc(S["half_set"], 1)
                rest_of_rstd(g, pool, S["all_rstd_ready"])
                pool.wait_ge(S["loaded"], 16 * 9)
                pool.wait_ge(S["half_set"], 1)

                def step(i, k):
                    s = UNROLL * i + k
                    m, b = s - 2, k % 2
                    if live(m, N):
                        pool.wait_ge(S["var_ready"], m + 1)
                        need(pool, S["normed_ready"], m - 1)
                        pool.tensor_tensor(rstd[b][:], var[b][:], minus_half[:], ALU.pow).then_inc(S["rstd_ready"], 1)
                    if live(s, N):
                        pool.wait_ge(S["turned_ready"], s + 1)
                        pool.tensor_tensor(qk[k % 2][:], qk[k % 2][:], turned[k % 2][:], ALU.add)\
                            .then_inc(S["qk_ready"], 1)
                skewed(pool, N, 2, step, UNROLL)

            @block.vector
            def _(dve):
                dve.wait_ge(S["loaded"], 16 * 9)
                dve.tensor_reduce(wv_mean[:], wv[:], AXIS.X, ALU.add).then_inc(S["wv_step"], 1)
                dve.wait_ge(S["wv_step"], 1)
                dve.tensor_scalar(wv_mean[:], wv_mean[:], 1.0 / R_VAL, None, ALU.mult).then_inc(S["wv_step"], 1)
                dve.wait_ge(S["wv_step"], 2)
                dve.tensor_tensor(wv[:], wv[:], wv_mean[:].unsqueeze(2).to_broadcast([D, H, R_VAL]),
                                  ALU.subtract).then_inc(S["wv_ready"], 1)
                flat_wv = wv[:].rearrange("p h c -> p (h c)")
                for low, full, high, ready in ((wqk_low[:], wqk[:], wqk_high[:], S["wqk_high_ready"]),
                                               (wv_low[:], flat_wv, wv_high[:], S["wv_high_ready"])):
                    dve.wait_ge(ready, 1)
                    dve.tensor_tensor(low, full, high, ALU.subtract).then_inc(S["w_low_ready"], 1)
                dve.wait_ge(S["cleared"], 4)

                def step(i, k):
                    s = UNROLL * i + k
                    m, b = s - 4, k % 2
                    if live(m, N):
                        dve.wait_ge(S["affine_dve"], m + 1)
                        dve.wait_ge(S["affine_act"], m + 1)
                        dve.wait_ge(S["gate_ready"], m + 1)
                        dve.tensor_tensor(gated[b][:], gated[b][:], gate[b][:], ALU.mult)\
                            .then_inc(S["gated_ready"], 1)
                    m, b = s - 3, (k - 3) % 2
                    if live(m, N):
                        dve.wait_ge(S["square_ready"], m + 1)
                        need(dve, S["rstd_ready"], m - 1)
                        dve.tensor_reduce(var[b][:], square[:], AXIS.X, ALU.add).then_inc(S["sum_ready"], 1)
                        dve.wait_ge(S["sum_ready"], m + 1)
                        dve.tensor_scalar(var[b][:], var[b][:], 1.0 / R_VAL, EPS, ALU.mult, ALU.add)\
                            .then_inc(S["var_ready"], 1)
                    m, b = s - 1, (k - 1) % 2
                    if live(m, N):
                        dve.wait_ge(S["qk_in_psum"], m + 1)
                        need(dve, S["qkT_in_psum"], m - 1)
                        src = ps_qk[:].rearrange("p (a e) -> p a e", e=R_KEY)
                        fold = lambda ap: ap.rearrange("p q h e -> p (q h) e")
                        dve.tensor_tensor(fold(qk[b][:]), src,
                                          cos[:].unsqueeze(1).to_broadcast([P, 2 * H, R_KEY]), ALU.mult)
                    m = s - 4
                    if live(m, N):
                        dve.wait_ge(S["out_in_psum"], m + 1)
                        dve.tensor_tensor(g.X[:, m, :], ps_vg[:, 0:D], g.X[:, m, :], ALU.add)\
                            .then_inc(S["x_updated"], 1)
                    m = s - 1
                    if live(m, N):
                        for part in range(2):
                            to, of = slice(32 * part, 32 * part + 32), slice(32 - 32 * part, 64 - 32 * part)
                            last = dve.tensor_tensor(fold(turned[b][:])[:, :, to], src[:, :, of],
                                                     sin[:, to].unsqueeze(1).to_broadcast([P, 2 * H, 32]), ALU.mult)
                        last.then_inc(S["turned_ready"], 1)
                    m, b = s - 3, (k - 3) % 2
                    if live(m, N):
                        dve.wait_ge(S["rstd_ready"], m + 1)
                        need(dve, S["normedT_in_psum"], m - 1)
                        dve.tensor_tensor(normed[b][:], heads(ps_o[:]),
                                          rstd[b][:].unsqueeze(2).to_broadcast([P, H, R_VAL]), ALU.mult)\
                            .then_inc(S["normed_ready"], 1)
                    m, b = s - 2, k % 2
                    if live(m, N):
                        dve.wait_ge(S["scores_in_psum"], m + 1)
                        need(dve, S["mixed_in_psum"], m - 1)
                        for row in range(2):
                            rows = slice(64 * row, 64 * row + 64)
                            last = dve.tensor_tensor(s_diag[b][rows, :, row, :],
                                                     ps_t[rows, 0:512].rearrange("p (h t) -> p h t", t=SEQ),
                                                     decay[rows, :, :], ALU.mult)
                        last.then_inc(S["s_ready"], 1)
                    if live(s, N):
                        need(dve, S["xnT_in_psum"], s - 1)
                        dve.tensor_scalar(xn[k % 2][:], g.X[:, s, :], g.mean[:, bass.ds(s, 1)],
                                          g.rstd[:, bass.ds(s, 1)], ALU.subtract, ALU.mult)\
                            .then_inc(S["xn_ready"], 1)
                    m = s - 4
                    if live(m, N):
                        dve.wait_ge(S["x_updated"], m + 1)
                        dve.bn_stats(g.stats[:, m, :], g.X[:, m, :])
                    m, b = s - 3, (k - 3) % 2
                    if live(m, N):
                        dve.wait_ge(S["normedT_in_psum"], m + 1)
                        need(dve, S["out_in_psum"], m - 1)
                        for h in range(DVE_HEADS):
                            last = dve.tensor_scalar(gated[b][:, h, :], ps_t[:, h * P:(h + 1) * P], gn_w[:, h:h + 1],
                                                     gn_b[:, h:h + 1], ALU.mult, ALU.add)
                        last.then_inc(S["affine_dve"], 1)
                    if live(s, N):
                        dve.wait_ge(S["xnT_ready"], s + 1)
                        dve.wait_ge(S["high_ready"], s + 1)
                        need(dve, S["v_in_psum"], s - 1)
                        dve.tensor_tensor(x_low[k % 2][:], ps_qk[:, 0:P], x_high[k % 2][:], ALU.subtract)\
                            .then_inc(S["low_ready"], 1)
                skewed(dve, N, 4, step, UNROLL, between=lambda: dve.wait_ge(S["all_rstd_ready"], 1))

            @block.scalar
            def _(act):
                act.wait_ge(S["loaded"], 16 * 9)
                nc.scalar.activation(wqk_high[:], wqk[:], ACT.Copy).then_inc(S["wqk_high_ready"], 1)
                act.wait_ge(S["wv_ready"], 1)
                nc.scalar.activation(wv_high[:], wv[:].rearrange("p h c -> p (h c)"), ACT.Copy)\
                    .then_inc(S["wv_high_ready"], 1)
                act.wait_ge(S["cleared"], 4)

                def step(i, k):
                    ahead, place = UNROLL * i + k, k
                    s, k = ahead - 1, (k - 1) % UNROLL
                    m = s - 2
                    if live(m, N):
                        act.wait_ge(S["mixed_in_psum"], m + 1)
                        need(act, S["sum_ready"], m)
                        nc.scalar.activation(square[:], heads(ps_o[:]), ACT.Square).then_inc(S["square_ready"], 1)
                    m, b = s - 1, (k - 1) % 2
                    if live(m, N):
                        act.wait_ge(S["qkT_in_psum"], m + 1)
                        need(act, S["scores_in_psum"], m - 1)
                        for half in range(2):
                            rows = slice(64 * half, 64 * half + 64)
                            last = nc.scalar.activation(
                                q_diag[b][rows, :, :, half, :],
                                ps_t[rows, 0:512].rearrange("p (h r t) -> p h r t", r=2, t=SEQ), ACT.Copy)
                        last.then_inc(S["q_diag_ready"], 1)
                        nc.scalar.activation(kT[b][:], ps_t[:, 512:1024].rearrange("p (h t) -> p h t", t=P),
                                             ACT.Copy).then_inc(S["kT_ready"], 1)
                    if live(s, N):
                        act.wait_ge(S["v_in_psum"], s + 1)
                        need(act, S["mixed_in_psum"], s - 1)
                        nc.scalar.activation(v[k % 2][:], heads(ps_vg[:]), ACT.Copy).then_inc(S["v_ready"], 1)
                    m, b = s - 2, k % 2
                    if live(m, N):
                        act.wait_ge(S["gate_in_psum"], m + 1)
                        need(act, S["gated_ready"], m - 1)
                        nc.scalar.activation(gate[b][:], heads(ps_vg[:]), ACT.Silu).then_inc(S["gate_ready"], 1)
                    if live(ahead, N):
                        act.wait_ge(S["xnT_in_psum"], ahead + 1)
                        need(act, S["v_in_psum"], ahead - 1)
                        nc.scalar.activation(x_high[place % 2][:], ps_qk[:, 0:P], ACT.Copy).then_inc(S["high_ready"], 1)
                        need(act, S["gate_in_psum"], ahead - 3)
                        nc.scalar.activation(xnT[place][:], ps_qk[:, 0:P], ACT.Copy).then_inc(S["xnT_ready"], 1)
                    if live(m, N):
                        act.wait_ge(S["normedT_in_psum"], m + 1)
                        need(act, S["out_in_psum"], m - 1)
                        for h in range(DVE_HEADS, H):
                            last = nc.scalar.activation(gated[b][:, h, :], ps_t[:, h * P:(h + 1) * P], ACT.Identity,
                                                        bias=gn_b[:, h:h + 1], scale=gn_w[:, h:h + 1])
                        last.then_inc(S["affine_act"], 1)
                skewed(act, N, 3, step, UNROLL)

            @block.tensor
            def _(pe):
                pe.wait_ge(S["w_low_ready"], 2)
                pe.wait_ge(S["loaded"], 16 * 9)

                def product(out, which, high, low):
                    pe.matmul(out, x_high[which][:], high, start=True, stop=False)
                    pe.matmul(out, x_high[which][:], low, start=False, stop=False)
                    return pe.matmul(out, x_low[which][:], high, start=False, stop=True)

                def step(i, k):
                    ahead, even = UNROLL * i + k, k % 2
                    s, k = ahead - 1, (k - 1) % UNROLL
                    if live(s, N):
                        pe.wait_ge(S["low_ready"], s + 1)
                        for half in range(2):
                            cols = slice(512 * half, 512 * half + 512)
                            last = product(ps_qk[:, cols], k % 2, wqk_high[:, cols], wqk_low[:, cols])
                        last.then_inc(S["qk_in_psum"], 1)
                    m, b = s - 1, (k - 1) % 2
                    if live(m, N):
                        pe.wait_ge(S["qk_ready"], m + 1)
                        need(pe, S["affine_dve"], m - 1)
                        need(pe, S["affine_act"], m - 1)
                        need(pe, S["s_ready"], m)
                        for which in range(2):
                            for hp in range(HP):
                                last = pe.transpose(
                                    ps_t[:, 512 * which + 128 * hp:512 * which + 128 * hp + 128],
                                    qk[b][:, which, 2 * hp:2 * hp + 2, :].rearrange("p h e -> p (h e)"),
                                    g.ident[:])
                        last.then_inc(S["qkT_in_psum"], 1)
                    m, b = s - 3, (k - 3) % 2
                    if live(m, N):
                        pe.wait_ge(S["gated_ready"], m + 1)
                        pe.wait_ge(S["gate_ready"], m + 1)
                        for h in range(H):
                            last = pe.matmul(ps_vg[:, 0:D], gated[b][:, h, :], wo[:, h, :],
                                             start=(h == 0), stop=(h == H - 1))
                        last.then_inc(S["out_in_psum"], 1)
                    if live(s, N):
                        need(pe, S["v_ready"], s)
                        need(pe, S["gate_ready"], s - 2)
                        for half in (1, 0):
                            if half == 0:
                                need(pe, S["x_updated"], s - 2)
                            cols = slice(512 * half, 512 * half + 512)
                            last = product(ps_vg[:, cols], k % 2, wv_high[:, cols], wv_low[:, cols])
                        last.then_inc(S["v_in_psum"], 1)
                    m, b = s - 1, (k - 1) % 2
                    if live(m, N):
                        pe.wait_ge(S["q_diag_ready"], m + 1)
                        pe.wait_ge(S["kT_ready"], m + 1)
                        for hp in range(HP):
                            for row in range(2):
                                last = pe.matmul(ps_t[64 * row:64 * row + 64, 128 * hp:128 * hp + 128],
                                                 kT[b][:, hp, 64 * row:64 * row + 64],
                                                 q_diag[b][:, hp, row, :, :].rearrange("p h t -> p (h t)"),
                                                 start=True, stop=True)
                        last.then_inc(S["scores_in_psum"], 1)
                    m, b = s - 2, (k - 2) % 4
                    if live(m, N):
                        if live(s, N):
                            pe.wait_ge(S["v_ready"], s + 1)
                        else:
                            need(pe, S["x_updated"], s - 2)
                        for h in range(H):
                            last = pe.matmul(ps_vg[:, 128 * h:128 * h + 128], wg[:, 128 * h:128 * h + 128],
                                             xnT[b][:], start=True, stop=True)
                        last.then_inc(S["gate_in_psum"], 1)
                        pe.wait_ge(S["normed_ready"], m + 1)
                        if live(s - 1, N):
                            pe.wait_ge(S["s_ready"], m + 2)
                        else:
                            need(pe, S["affine_dve"], m)
                            need(pe, S["affine_act"], m)
                        for h in range(H):
                            last = pe.transpose(ps_t[:, 128 * h:128 * h + 128], normed[k % 2][:, h, :], g.ident[:])
                        last.then_inc(S["normedT_in_psum"], 1)
                    if live(ahead, N):
                        pe.wait_ge(S["xn_ready"], ahead + 1)
                        need(pe, S["turned_ready"], ahead)
                        pe.transpose(ps_qk[:, 0:P], xn[even][:], g.ident[:]).then_inc(S["xnT_in_psum"], 1)
                    m, b = s - 1, (k - 1) % 2
                    if live(m, N):
                        pe.wait_ge(S["s_ready"], m + 1)
                        pe.wait_ge(S["v_ready"], m + 1)
                        need(pe, S["normed_ready"], m)
                        for h in range(H):
                            last = pe.matmul(ps_o[:, 128 * h:128 * h + 128],
                                             s_diag[b][:, h, :, :].rearrange("p r t -> p (r t)"),
                                             v[b][:, h, :], start=True, stop=True)
                        last.then_inc(S["mixed_in_psum"], 1)
                skewed(pe, N, 4, step, UNROLL)


EXPERTS, FFN = 8, 512
FT = FFN // P
BIG = 1.0e38
TOP_K = 2
MOVED = 4
LAG = 3
GTILES = GROUP


def slot_tiles(parts):
    used = (TOP_K * TOKENS // parts + EXPERTS * (P - 1)) // P
    return -(-used // (2 * MOVED)) * 2 * MOVED


def route(g, name, spec, f):
    nc, dram = g.nc, g.dram
    with ExitStack() as own:
        def sb(n, shape):
            return g.sbuf(f"{name}_{n}", shape, ctx=own)

        by_token = [P, TILES, EXPERTS]
        gate_w, gate_b = sb("gate_w", [D, EXPERTS]), sb("gate_b", [P, EXPERTS])
        rank, before, all_ones = sb("rank", [P, EXPERTS]), sb("before", [P, P]), sb("all_ones", [P, P])
        parts, N = spec["parts"], f["tiles"]
        PTILES, V = TILES // parts, parts * EXPERTS
        by_expert = [P, V, PTILES]
        tile_starts, tile_numbers = sb("tile_starts", [P, TILES]), sb("tile_numbers", [1, N])
        xn, xnT = [sb(f"xn_tile{k}", [P, D]) for k in range(4)], [sb(f"xnT{k}", [D, P]) for k in range(4)]
        zeros = sb("zeros", [P, 1024])
        logit, key, score, both = sb("logit", by_token), sb("key", by_token), sb("score", by_token), sb("both", by_token)
        first, second, place = sb("first", by_token), sb("second", by_token), sb("place", by_token)
        top, rec = sb("top", [P, TILES]), sb("rec", [P, TILES])
        ones_row, per_tile, running, over = (sb(k, by_expert) for k in ("ones_row", "per_tile", "running", "over"))
        earlier, count, tiles = sb("earlier", [P, V]), sb("count", [P, V]), sb("tiles", [P, V])
        tile_end, offset = sb("tile_end", [P, V]), sb("offset", [P, V])
        ended, owner = sb("ended", [1, N, EXPERTS]), sb("tile_owner", [1, N])
        bank_x = [own.enter_context(nc.psum_tensor(f"{name}_xT_psum{k}", [P, 512], F32)) for k in range(4)]
        bank_l = own.enter_context(nc.psum_tensor(f"{name}_logit_psum", [P, TILES, EXPERTS], F32))
        bank_p = own.enter_context(nc.psum_tensor(f"{name}_prefix_psum", [P, TILES, EXPERTS], F32))
        bank_c = own.enter_context(nc.psum_tensor(f"{name}_count_psum", [P, TILES, EXPERTS], F32))
        names = ("loaded", "xn_ready", "xnT_in_psum", "xnT_ready", "logits_in_psum", "step", "exp_in", "exp_out",
                 "kept", "both_ready", "counts_in_psum", "constants_set", "zeros_set", "slots_zeroed", "rstd_ready")
        S = {k: g.sem(f"{name}_r_{k}") for k in names}
        bc = lambda ap: ap[:].unsqueeze(2).to_broadcast(by_token)
        per_token = lambda ap: ap[:].unsqueeze(1).to_broadcast(by_token)
        loads = [(gate_w[:], dram[spec["gate_w"]]), (gate_b[:], dram[spec["gate_b"]].to_broadcast([P, EXPERTS])),
                 (rank[:], dram["rank"]), (before[:], dram["before"]), (tile_starts[:], dram["tile_starts"]),
                 (tile_numbers[:], dram["tile_numbers"][:, 0:N])]
        n_loads = len(loads)

        def load(sp):
            for dst, src in loads:
                sp.dma_start(dst, src).then_inc(S["loaded"], 16)

        row_statistics(g, name, load, split=True)
        with nc.Block() as block:

            @block.sync
            def _(sp):
                for dst, src in f["loads"]:
                    sp.dma_start(dst, src).then_inc(f["loaded"], 16)
                sp.wait_ge(S["zeros_set"], 1)
                width = zeros.shape[1]
                for slots in f["slots_x"]:
                    flat = slots.rearrange("(p a) d -> p (a d)", p=P)
                    for c in range(N * D // width):
                        sp.dma_start(flat[:, width * c:width * c + width], zeros[:]).then_inc(S["slots_zeroed"], 16)
                sp.wait_ge(S["slots_zeroed"], 16 * parts * (N * D // width))

            @block.vector
            def _(dve):
                done = [0]

                def seq(ins):
                    done[0] += 1
                    ins.then_inc(S["step"], 1)
                    dve.wait_ge(S["step"], done[0])

                def xn_step(i, k):
                    s = 4 * i + k
                    if live(s, TILES):
                        need(dve, S["xnT_in_psum"], s - 3)
                        dve.tensor_scalar(xn[k][:], g.X[:, s, :], g.mean[:, bass.ds(s, 1)],
                                          g.rstd[:, bass.ds(s, 1)], ALU.subtract, ALU.mult)\
                            .then_inc(S["xn_ready"], 1)
                skewed(dve, TILES, 0, xn_step, 4, between=lambda: dve.wait_ge(S["rstd_ready"], 1))
                dve.wait_ge(S["loaded"], 16 * n_loads)
                dve.wait_ge(S["logits_in_psum"], TILES)
                seq(dve.tensor_tensor(logit[:], bank_l[:], per_token(gate_b), ALU.add))

                def one_hot_of_max(out, values, peak):
                    seq(dve.tensor_reduce(peak[:], values[:], AXIS.X, ALU.max))
                    seq(dve.tensor_tensor(key[:], values[:], bc(peak), ALU.is_equal))
                    seq(dve.tensor_tensor(key[:], key[:], per_token(rank), ALU.mult))
                    seq(dve.tensor_reduce(rec[:], key[:], AXIS.X, ALU.max))
                    seq(dve.tensor_tensor(out[:], key[:], bc(rec), ALU.is_equal))

                one_hot_of_max(first, logit, top)
                seq(dve.scalar_tensor_tensor(out=score[:], in0=first[:], scalar=-BIG, in1=logit[:],
                                             op0=ALU.mult, op1=ALU.add))
                one_hot_of_max(second, score, rec)
                dve.tensor_tensor(both[:], first[:], second[:], ALU.add).then_inc(S["both_ready"], 1)

                def total(out, values, one_hot):
                    seq(dve.tensor_tensor(key[:], values[:], one_hot[:], ALU.mult))
                    seq(dve.tensor_reduce(out[:], key[:], AXIS.X, ALU.add))

                w = [f["weight0"], f["weight1"]]
                if spec["kind"] == "sigmoid":
                    dve.wait_ge(S["exp_out"], 1)
                    seq(dve.tensor_scalar(score[:], score[:], 1.0, None, ALU.add))
                    seq(dve.reciprocal(score[:], score[:]))
                    total(w[0], score, first)
                    total(w[1], score, second)
                    seq(dve.tensor_tensor(top[:], w[0], w[1], ALU.max))
                    dve.tensor_tensor(f["pair"][:], f["pair"][:], top[:].unsqueeze(1).to_broadcast([P, TOP_K, TILES]),
                                      ALU.subtract).then_inc(S["exp_in"], 1)
                    dve.wait_ge(S["exp_out"], 2)
                else:
                    dve.tensor_tensor(place[:], logit[:], bc(top), ALU.subtract).then_inc(S["exp_in"], 1)
                    dve.wait_ge(S["exp_out"], 1)
                    seq(dve.tensor_reduce(rec[:], score[:], AXIS.X, ALU.add))
                    seq(dve.reciprocal(rec[:], rec[:]))
                    seq(dve.tensor_tensor(score[:], score[:], bc(rec), ALU.mult))
                    total(w[0], score, first)
                    total(w[1], score, second)
                seq(dve.tensor_tensor(rec[:], w[0], w[1], ALU.add))
                if spec["kind"] == "softmax":
                    seq(dve.tensor_scalar(rec[:], rec[:], 1e-8, None, ALU.add))
                seq(dve.reciprocal(rec[:], rec[:]))
                dve.tensor_tensor(f["pair"][:], f["pair"][:], rec[:].unsqueeze(1).to_broadcast([P, TOP_K, TILES]),
                                  ALU.mult)

                dve.wait_ge(S["counts_in_psum"], 1)
                dve.wait_ge(S["constants_set"], 4)
                experts_of = lambda part: slice(part * EXPERTS, (part + 1) * EXPERTS)
                tiles_of = lambda part: slice(part * PTILES, (part + 1) * PTILES)
                for part in range(parts):
                    seq(dve.tensor_copy(per_tile[:, experts_of(part), :],
                                        bank_c[:, tiles_of(part), :].rearrange("p t e -> p e t")))
                flat = lambda ap: ap[:].rearrange("p e t -> p (e t)")
                seq(dve.tensor_tensor_scan(flat(running), flat(ones_row), flat(per_tile), 0.0, ALU.mult, ALU.add))
                seq(dve.tensor_copy(earlier[:, 1:V], running[:, 0:V - 1, PTILES - 1]))
                seq(dve.tensor_tensor(count[:], running[:, :, PTILES - 1], earlier[:], ALU.subtract))
                seq(dve.tensor_tensor(over[:], count[:].unsqueeze(2).to_broadcast(by_expert),
                                      tile_starts[:, 0:PTILES].unsqueeze(1).to_broadcast(by_expert), ALU.is_gt))
                seq(dve.tensor_reduce(tiles[:], over[:], AXIS.X, ALU.add))
                seq(dve.tensor_tensor_scan(tile_end[:], flat(ones_row)[:, 0:V], tiles[:], 0.0, ALU.mult, ALU.add))
                for part in range(parts - 1, 0, -1):
                    before_it = part * EXPERTS
                    seq(dve.tensor_scalar(tile_end[:, experts_of(part)], tile_end[:, experts_of(part)],
                                          tile_end[:, before_it - 1:before_it], None, ALU.subtract))
                seq(dve.tensor_tensor(offset[:], tile_end[:], tiles[:], ALU.subtract))
                seq(dve.scalar_tensor_tensor(out=offset[:], in0=offset[:], scalar=float(P), in1=earlier[:],
                                             op0=ALU.mult, op1=ALU.subtract))
                seq(dve.tensor_tensor(running[:], running[:], per_tile[:], ALU.subtract))
                for part in range(parts):
                    rows = place[:, tiles_of(part), :]
                    seq(dve.tensor_tensor(rows, bank_p[:, tiles_of(part), :],
                                          running[:, experts_of(part), :].rearrange("p e t -> p t e"), ALU.add))
                    seq(dve.tensor_tensor(rows, rows, offset[:, experts_of(part)].unsqueeze(1)
                                          .to_broadcast([P, PTILES, EXPERTS]), ALU.add))
                for n, one_hot in enumerate((first, second)):
                    total(rec, place, one_hot)
                    seq(dve.tensor_copy(f["slots"][:, n, :], rec[:]))
                shape = [1, N, EXPERTS]
                for part in range(parts):
                    seq(dve.tensor_tensor(ended[:], tile_end[0:1, experts_of(part)].unsqueeze(1).to_broadcast(shape),
                                          tile_numbers[:].unsqueeze(2).to_broadcast(shape), ALU.is_le))
                    seq(dve.tensor_reduce(owner[:], ended[:], AXIS.X, ALU.add))
                    seq(dve.tensor_scalar(owner[:], owner[:], float(EXPERTS - 1), None, ALU.min))
                    begin = part * f["owner_stride"] + LAG
                    seq(dve.tensor_copy(f["owner"][:, begin:begin + N], owner[:]))

            @block.gpsimd
            def _(pool):
                rest_of_rstd(g, pool, S["rstd_ready"])
                pool.memset(zeros[:], 0.0).then_inc(S["zeros_set"], 1)
                pool.memset(all_ones[:], 1.0).then_inc(S["constants_set"], 1)
                pool.memset(f["owner"][:], 0).then_inc(S["constants_set"], 1)
                pool.memset(ones_row[:], 1.0).then_inc(S["constants_set"], 1)
                pool.memset(earlier[:], 0.0).then_inc(S["constants_set"], 1)

            @block.scalar
            def _(act):
                def step(i, k):
                    s = 4 * i + k
                    act.wait_ge(S["xnT_in_psum"], s + 1)
                    need(act, S["logits_in_psum"], s - 3)
                    nc.scalar.activation(xnT[k][:], bank_x[k][:, 0:P], ACT.Copy).then_inc(S["xnT_ready"], 1)
                    if spec["shared"]:
                        nc.scalar.activation(f["xnT"][:, bass.ds(s * P, P)], bank_x[k][:, 0:P], ACT.Copy)\
                            .then_inc(S["kept"], 1)
                skewed(act, TILES, 0, step, 4)
                if spec["kind"] == "sigmoid":
                    act.wait_ge(S["both_ready"], 1)
                    nc.scalar.activation(score[:], bank_l[:], ACT.Exp, scale=-1.0).then_inc(S["exp_out"], 1)
                    act.wait_ge(S["exp_in"], 1)
                    nc.scalar.activation(f["pair"][:], f["pair"][:], ACT.Exp).then_inc(S["exp_out"], 1)
                else:
                    act.wait_ge(S["exp_in"], 1)
                    nc.scalar.activation(score[:], place[:], ACT.Exp).then_inc(S["exp_out"], 1)

            @block.tensor
            def _(pe):
                pe.wait_ge(S["loaded"], 16 * n_loads)

                def step(i, k):
                    s = 4 * i + k
                    if live(s, TILES):
                        pe.wait_ge(S["xn_ready"], s + 1)
                        need(pe, S["kept"] if spec["shared"] else S["xnT_ready"], s - 3)
                        pe.transpose(bank_x[k][:, 0:P], xn[k][:], g.ident[:]).then_inc(S["xnT_in_psum"], 1)
                    m, b = s - 2, (k - 2) % 4
                    if live(m, TILES):
                        pe.wait_ge(S["xnT_ready"], m + 1)
                        pe.matmul(bank_l[:, m, :], xnT[b][:], gate_w[:], start=True, stop=True)\
                            .then_inc(S["logits_in_psum"], 1)
                skewed(pe, TILES, 2, step, 4)
                pe.wait_ge(S["both_ready"], 1)
                pe.wait_ge(S["constants_set"], 4)
                pe.matmul(bank_p[:], before[:], both[:], start=True, stop=True)
                pe.matmul(bank_c[:], all_ones[:], both[:], start=True, stop=True).then_inc(S["counts_in_psum"], 1)


class SharedExpert:

    def __init__(self, g, name, ctx, spec, f, e):
        self.g, self.spec, self.f, self.e = g, spec, f, e
        self.hidden = [g.sbuf(f"{name}_hidden{k}", [P, FT, GT], ctx=ctx) for k in range(2)]
        self.bank_h = [ctx.enter_context(g.nc.psum_tensor(f"{name}_hidden_psum{k}", [P, GT], F32)) for k in range(4)]
        self.bank_y = [ctx.enter_context(g.nc.psum_tensor(f"{name}_y_psum{k}", [P, 4, D], F32)) for k in range(2)]
        self.up_done, self.hidden_ready = g.sem(f"{name}_up_done"), g.sem(f"{name}_hidden_ready")
        self.y_in_psum, self.y_added = g.sem(f"{name}_y_in_psum"), g.sem(f"{name}_y_added")

    def tensor(self, pe):
        f, e = self.f, self.e

        def step(i, k):
            s = 2 * i + k
            if live(s, GROUPS):
                for j in range(FT):
                    need(pe, self.hidden_ready, FT * (s - 1) + j + 1)
                    pe.matmul(self.bank_h[j][:], f["w_up"][:, e, j * P:(j + 1) * P], f["xnT"][:, bass.ds(s * GT, GT)],
                              start=True, stop=True).then_inc(self.up_done, 1)
            m, b = s - 1, (k - 1) % 2
            if live(m, GROUPS):
                pe.wait_ge(self.hidden_ready, FT * (m + 1))
                need(pe, self.y_added, m - 1)
                for t in range(GTILES):
                    for j in range(FT):
                        last = pe.matmul(self.bank_y[b][:, t, :], self.hidden[b][:, j, t * P:(t + 1) * P],
                                         f["w_down"][:, e, j, :], start=(j == 0), stop=(j == FT - 1))
                last.then_inc(self.y_in_psum, 1)
        skewed(pe, GROUPS, 1, step, peeled=2)

    def scalar(self, act):
        def step(i, k):
            s = 2 * i + k
            for j in range(FT):
                act.wait_ge(self.up_done, FT * s + j + 1)
                need(act, self.y_in_psum, s - 1)
                self.g.nc.scalar.activation(self.hidden[k][:, j, :], self.bank_h[j][:], self.spec["gelu"])\
                    .then_inc(self.hidden_ready, 1)
        skewed(act, GROUPS, 0, step, peeled=2)

    def vector(self, dve, s, k):
        dve.wait_ge(self.y_in_psum, s + 1)
        x = self.g.X[:, bass.ds(GTILES * s, GTILES), :]
        dve.tensor_tensor(x, self.bank_y[k][:], x, ALU.add).then_inc(self.y_added, 1)


class Turn:

    def __init__(self, g, name, ctx):
        self.cell = g.sbuf(f"{name}_turn_cell", [P, 1], ctx=ctx)
        self.done = g.sem(f"{name}_turn_done")
        self.source = g.ident

    def __call__(self, pool, number, *waits):
        need(pool, self.done, number)
        for sem, value in waits:
            need(pool, sem, value)
        pool.tensor_tensor(self.cell[:], self.source[:, 0:1], self.source[:, 0:1], ALU.add).then_inc(self.done, 1)


class Scatter:

    def __init__(self, g, name, ctx, f, part):
        self.g, self.f, self.slots = g, f, f["slots_x"][part]
        self.groups = GROUPS // len(f["slots_x"])
        self.first_tile = part * self.groups * GTILES
        self.turn = Turn(g, name, ctx)
        self.group_slots = [g.sbuf(f"{name}_group_slots{k}", [P, TOP_K, GTILES], I32, ctx=ctx) for k in range(2)]
        self.xn = [g.sbuf(f"{name}_xn{k}", [P, GTILES, D], ctx=ctx) for k in range(2)]
        self.slots_ready, self.xn_ready = g.sem(f"{name}_slots_ready"), g.sem(f"{name}_xn_ready")
        self.scattered, self.base = g.indirect_transfers(self.groups)

    def gpsimd(self, pool):
        def step(i, k):
            s = 2 * i + k
            self.turn(pool, s, (self.xn_ready, GTILES * (s + 1)), (self.slots_ready, s + 1))
            for t in range(GTILES):
                for n in range(TOP_K):
                    pool.indirect_dma_start(
                        out=self.slots[:, :],
                        out_offset=bass.IndirectOffsetOnAxis(ap=self.group_slots[k][:, n, t:t + 1], axis=0),
                        in_=self.xn[k][:, t, :], in_offset=None).then_inc(self.scattered[k], 16)
        skewed(pool, self.groups, 0, step)
        for k in range(2):
            pool.wait_ge(self.scattered[k], self.base + 16 * TOP_K * GTILES * self.groups // 2)

    def open_group(self, dve, i, k):
        s = 2 * i + k
        need(dve, self.scattered[k], self.base + 16 * TOP_K * GTILES * i)
        dve.tensor_copy(self.group_slots[k][:], self.f["slots"][:, :, bass.ds(self.first_tile + GTILES * s, GTILES)])\
            .then_inc(self.slots_ready, 1)

    def tile(self, dve, i, k, t):
        g, tile = self.g, self.first_tile + GTILES * (2 * i + k) + t
        dve.tensor_scalar(self.xn[k][:, t, :], g.X[:, tile, :], g.mean[:, bass.ds(tile, 1)],
                          g.rstd[:, bass.ds(tile, 1)], ALU.subtract, ALU.mult).then_inc(self.xn_ready, 1)

    ROUNDS = 2

    def beside(self, dve, s):
        group, t = s // GTILES, s % GTILES
        if group < self.groups:
            if t == 0:
                self.open_group(dve, group // 2, group % 2)
            self.tile(dve, group // 2, group % 2, t)


class Gather:

    def __init__(self, g, name, ctx, f, part):
        self.g, self.f, self.slots = g, f, f["slots_y"][part]
        self.groups = GROUPS // len(f["slots_y"])
        self.first_tile = part * self.groups * GTILES
        self.turn = Turn(g, name, ctx)
        self.group_slots = [g.sbuf(f"{name}_group_slots{k}", [P, TOP_K, GTILES], I32, ctx=ctx) for k in range(2)]
        self.rows = [g.sbuf(f"{name}_rows{k}", [P, GTILES, TOP_K, D], ctx=ctx) for k in range(2)]
        self.slots_ready = g.sem(f"{name}_slots_ready")
        self.gathered, self.base = g.indirect_transfers(self.groups)
        self.added = [g.sem(f"{name}_added{n}") for n in range(TOP_K)]

    def gpsimd(self, pool):
        def step(i, k):
            s = 2 * i + k
            self.turn(pool, s, (self.added[1], GTILES * (s - 1)), (self.slots_ready, s + 1))
            for t in range(GTILES):
                for n in range(TOP_K):
                    pool.indirect_dma_start(
                        out=self.rows[k][:, t, n, :], out_offset=None, in_=self.slots[:, :],
                        in_offset=bass.IndirectOffsetOnAxis(ap=self.group_slots[k][:, n, t:t + 1], axis=0))\
                        .then_inc(self.gathered[k], 16)
        skewed(pool, self.groups, 0, step)

    def open_group(self, dve, i, k):
        s = 2 * i + k
        need(dve, self.gathered[k], self.base + 16 * TOP_K * GTILES * i)
        dve.tensor_copy(self.group_slots[k][:], self.f["slots"][:, :, bass.ds(self.first_tile + GTILES * s, GTILES)])\
            .then_inc(self.slots_ready, 1)

    def wait_rows(self, dve, i, k):
        dve.wait_ge(self.gathered[k], self.base + 16 * TOP_K * GTILES * (i + 1))

    def add(self, dve, i, k, t, n):
        tile = self.first_tile + GTILES * (2 * i + k) + t
        x = self.g.X[:, tile, :]
        dve.scalar_tensor_tensor(out=x, in0=self.rows[k][:, t, n, :], scalar=self.f[f"weight{n}"][:, bass.ds(tile, 1)],
                                 in1=x, op0=ALU.mult, op1=ALU.add).then_inc(self.added[n], 1)

    def statistics(self, dve, i, k, t):
        tile = self.first_tile + GTILES * (2 * i + k) + t
        dve.bn_stats(self.g.stats[:, tile, :], self.g.X[:, tile, :])

    ROUNDS = 3

    def beside(self, dve, s):
        group, t = s // GTILES, s % GTILES
        if group < self.groups and t == 0:
            self.open_group(dve, group // 2, group % 2)
        group -= 2
        if 0 <= group < self.groups:
            at = (dve, group // 2, group % 2)
            if t == 0:
                self.wait_rows(*at)
            self.add(*at, t, 0)
            dve.wait_ge(self.added[0], s - 2 * GTILES + 1)
            self.add(*at, t, 1)


def dispatch(g, name, spec, f):
    with ExitStack() as ctx:
        shared = SharedExpert(g, f"{name}_s0", ctx, spec, f, 0) if spec["shared"] else None
        scatter = Scatter(g, name, ctx, f, 0)
        w_high_ready, xn_added = g.sem(f"{name}_w_high_ready"), g.sem(f"{name}_xn_added")
        with g.nc.Block() as block:

            @block.sync
            def _(sp):
                sp.wait_ge(f["loaded"], 16 * len(f["loads"]))

            @block.gpsimd
            def _(pool):
                scatter.gpsimd(pool)

            @block.vector
            def _(dve):
                def step(i, k):
                    s = 2 * i + k
                    if live(s, scatter.groups):
                        scatter.open_group(dve, i, k)
                        for t in range(GTILES):
                            scatter.tile(dve, i, k, t)
                        if spec["plus_xn"]:
                            dve.wait_ge(scatter.xn_ready, GTILES * (s + 1))
                            x = g.X[:, bass.ds(GTILES * s, GTILES), :]
                            dve.tensor_tensor(x, x, scatter.xn[k][:], ALU.add).then_inc(xn_added, 1)
                    m, b = s - 1, (k - 1) % 2
                    if shared and live(m, GROUPS):
                        dve.wait_ge(xn_added, m + 1)
                        shared.vector(dve, m, b)
                skewed(dve, scatter.groups, 1, step)
                dve.wait_ge(f["loaded"], 16 * len(f["loads"]))
                for e in range(EXPERTS):
                    dve.tensor_copy(f["w_high"][:, e, :], f["w_up"][:, spec["shared"] + e, :])\
                        .then_inc(w_high_ready, 1)
                for e in range(EXPERTS):
                    dve.wait_ge(w_high_ready, e + 1)
                    dve.tensor_tensor(f["w_low"][:, e, :], f["w_up"][:, spec["shared"] + e, :],
                                      f["w_high"][:, e, :], ALU.subtract)

            if shared:
                @block.tensor
                def _(pe):
                    pe.wait_ge(f["loaded"], 16 * len(f["loads"]))
                    shared.tensor(pe)

                @block.scalar
                def _(act):
                    shared.scalar(act)


class Owners:

    def __init__(self, g, kind, f, part):
        self.g, self.kind, self.f, self.held = g, kind, f, ()
        self.begin = part * f["owner_stride"]

    def new_round(self, i):
        _, self.held = self.g.nc.values_load_multi_w_load_instructions(
            self.f["owner"][0:1, bass.ds(self.begin + 2 * MOVED * i, LAG + 2 * MOVED)], engines=(self.kind,), min_val=0,
            max_val=EXPERTS - 1, skip_runtime_bounds_check_because="a minimum with EXPERTS - 1 bounds them")

    def of(self, place):
        return self.held[LAG + place]


def run_experts(g, name, spec, f, part, transfers=None):
    nc = g.nc
    biased, N, E0 = spec["b_up"] is not None, f["tiles"], spec["shared"]
    with ExitStack() as ctx:
        other = transfers[0](g, f"{name}_other", ctx, f, transfers[1]) if transfers else None
        def sb(n, shape):
            return g.sbuf(f"{name}_{n}", shape, ctx=ctx)

        x_in, y_out = [sb(f"x_in{k}", [P, MOVED, D]) for k in range(2)], [sb(f"y_out{k}", [P, MOVED, D]) for k in range(2)]
        x_high, x_low = ([g.sbuf(f"{name}_{part}{k}", [D, P], F32R, ctx=ctx) for k in range(2)]
                         for part in ("x_high", "x_low"))
        hidden = [sb(f"hid{k}", [P, FFN]) for k in range(2)]
        hT = [sb(f"hT{k}", [P, FT, P]) for k in range(2)]
        before_gelu = [sb(f"before_gelu{k}", [P, FFN]) for k in range(2)] if biased else None

        def ps(n, shape):
            return [ctx.enter_context(nc.psum_tensor(f"{name}_{n}_psum{k}", shape, F32)) for k in range(2)]

        bank_x, bank_h, bank_t, bank_y = ps("x", [P, 512]), ps("h", [P, FFN]), ps("hT", [P, FT, P]), ps("yt", [P, 512])
        names = ("xT_in_psum", "high_ready", "low_ready", "up_done", "biased", "hidden_ready", "hT_in_psum", "hT_ready",
                 "y_in_psum", "y_ready")
        S = {k: g.sem(f"{name}_{k}") for k in names}
        x_loaded = [g.sem(f"{name}_x_loaded{k}") for k in range(2)]
        stored = [g.sem(f"{name}_y_stored{k}") for k in range(2)]
        h_read = S["biased"] if biased else S["hidden_ready"]

        def tiles(slots):
            return slots.rearrange("(j p) d -> p j d", p=P)

        with nc.Block() as block:

            @block.sync
            def _(sp):
                def step(i, k):
                    s = 2 * i + k
                    if live(s, N // MOVED):
                        need(sp, S["xT_in_psum"], MOVED * (s - 1))
                        sp.dma_start(x_in[k][:], tiles(f["slots_x"][part])[:, bass.ds(MOVED * s, MOVED), :])\
                            .then_inc(x_loaded[k], 16)
                    m, b = s - 3, (k - 3) % 2
                    if live(m, N // MOVED):
                        sp.wait_ge(S["y_ready"], MOVED * (m + 1))
                        sp.dma_start(tiles(f["slots_y"][part])[:, bass.ds(MOVED * m, MOVED), :], y_out[b][:])\
                            .then_inc(stored[b], 16)
                skewed(sp, N // MOVED, 3, step, peeled=2)
                for k in range(2):
                    sp.wait_ge(stored[k], 16 * N // (2 * MOVED))

            if other:
                @block.gpsimd
                def _(pool):
                    other.gpsimd(pool)

            @block.tensor
            def _(pe):
                owners = Owners(g, mybir.EngineType.PE, f, part)

                def step(i, k):
                    s = 2 * MOVED * i + k
                    if k == 0:
                        owners.new_round(i)
                    m, b = s - 1, (k - 1) % 2
                    if live(m, N):
                        expert = owners.of(k - 1)
                        pe.wait_ge(S["low_ready"], m + 1)
                        need(pe, h_read, m - 1)
                        high, low = (f[part][:, bass.ds(expert, 1), :] for part in ("w_high", "w_low"))
                        pe.matmul(bank_h[b][:], x_high[b][:], high, start=True, stop=False)
                        pe.matmul(bank_h[b][:], x_high[b][:], low, start=False, stop=False)
                        pe.matmul(bank_h[b][:], x_low[b][:], high, start=False, stop=True)\
                            .then_inc(S["up_done"], 1)
                    if live(s, N):
                        if k % MOVED == 0:
                            pe.wait_ge(x_loaded[k // MOVED], 16 * (i + 1))
                        need(pe, S["low_ready"], s - 1)
                        pe.transpose(bank_x[k % 2][:, 0:P], x_in[k // MOVED][:, k % MOVED, :], g.ident[:])\
                            .then_inc(S["xT_in_psum"], 1)
                    m, b = s - 2, k % 2
                    if live(m, N):
                        pe.wait_ge(S["hidden_ready"], m + 1)
                        need(pe, S["hT_ready"], m - 1)
                        for j in range(FT):
                            last = pe.transpose(bank_t[b][:, j, :], hidden[b][:, j * P:(j + 1) * P], g.ident[:])
                        last.then_inc(S["hT_in_psum"], 1)
                    m, b = s - 3, (k - 3) % 2
                    if live(m, N):
                        expert = owners.of(k - 3)
                        pe.wait_ge(S["hT_ready"], m + 1)
                        need(pe, S["y_ready"], m - 1)
                        for j in range(FT):
                            last = pe.matmul(bank_y[b][:, 0:D], hT[b][:, j, :],
                                             f["w_down"][:, bass.ds(expert + E0, 1), j, :],
                                             start=(j == 0), stop=(j == FT - 1))
                        last.then_inc(S["y_in_psum"], 1)
                skewed(pe, N, 3, step, 2 * MOVED)

            @block.scalar
            def _(act):
                def step(i, k):
                    s = 2 * i + k
                    if live(s, N):
                        act.wait_ge(S["xT_in_psum"], s + 1)
                        need(act, S["up_done"], s - 1)
                        nc.scalar.activation(x_high[k][:], bank_x[k][:, 0:P], ACT.Copy).then_inc(S["high_ready"], 1)
                    m, b = s - 1, (k - 1) % 2
                    if live(m, N):
                        act.wait_ge(h_read if biased else S["up_done"], m + 1)
                        need(act, S["hT_in_psum"], m - 1)
                        nc.scalar.activation(hidden[b][:], before_gelu[b][:] if biased else bank_h[b][:],
                                             spec["gelu"]).then_inc(S["hidden_ready"], 1)
                    m, b = s - 2, k
                    if live(m, N):
                        act.wait_ge(S["hT_in_psum"], m + 1)
                        need(act, S["y_in_psum"], m - 1)
                        nc.scalar.activation(hT[b][:], bank_t[b][:], ACT.Copy).then_inc(S["hT_ready"], 1)
                skewed(act, N, 2, step, peeled=2)

            @block.vector
            def _(dve):
                owners = Owners(g, mybir.EngineType.DVE, f, part)

                def step(i, k):
                    s = 2 * MOVED * i + k
                    if biased and k == 0:
                        owners.new_round(i)
                    m, b = s - 1, (k - 1) % 2
                    if biased and live(m, N):
                        expert = owners.of(k - 1)
                        dve.wait_ge(S["up_done"], m + 1)
                        need(dve, S["hidden_ready"], m - 1)
                        dve.tensor_tensor(before_gelu[b][:].unsqueeze(1), bank_h[b][:].unsqueeze(1),
                                          f["b_up"][:, bass.ds(expert, 1), :], ALU.add).then_inc(S["biased"], 1)
                    if live(s, N):
                        dve.wait_ge(S["high_ready"], s + 1)
                        need(dve, S["up_done"], s - 1)
                        dve.tensor_tensor(x_low[k % 2][:], bank_x[k % 2][:, 0:P], x_high[k % 2][:], ALU.subtract)\
                            .then_inc(S["low_ready"], 1)
                    m, b = s - 3, (k - 3) % 2
                    if live(m, N):
                        if biased:
                            expert = owners.of(k - 3)
                        dve.wait_ge(S["y_in_psum"], m + 1)
                        turn, place = (k - 3) // MOVED, (k - 3) % MOVED
                        if place == 0:
                            need(dve, stored[turn % 2], 16 * (i + turn // 2))
                        y, out = bank_y[b][:, 0:D].unsqueeze(1), y_out[turn % 2][:, place:place + 1, :]
                        if biased:
                            ins = dve.tensor_tensor(out, y, f["b_down"][:, bass.ds(expert, 1), :], ALU.add)
                        else:
                            ins = dve.tensor_copy(out, y)
                        ins.then_inc(S["y_ready"], 1)
                    if other and isinstance(s, int):
                        other.beside(dve, s)
                skewed(dve, N, 3, step, 2 * MOVED, peeled=other.ROUNDS if other else 1)


def combine(g, name, spec, f, part):
    with ExitStack() as ctx:
        shared = SharedExpert(g, f"{name}_s1", ctx, spec, f, 1) if spec["shared"] else None
        gather = Gather(g, name, ctx, f, part)
        with g.nc.Block() as block:

            @block.gpsimd
            def _(pool):
                gather.gpsimd(pool)

            if spec["last"]:
                @block.sync
                def _(sp):
                    def store(first, tiles):
                        sp.dma_start(g.out.rearrange("(i p) d -> p i d", p=P)[:, bass.ds(first, tiles), :],
                                     g.X[:, bass.ds(first, tiles), :]).then_inc(g.stored, 16)
                    store(0, gather.first_tile)

                    def step(i, k):
                        s = 2 * i + k
                        sp.wait_ge(gather.added[1], GTILES * (s + 1))
                        store(gather.first_tile + GTILES * s, GTILES)
                    skewed(sp, gather.groups, 0, step)
                    sp.wait_ge(g.stored, 16 * (1 + gather.groups))

            if shared:
                @block.tensor
                def _(pe):
                    shared.tensor(pe)

                @block.scalar
                def _(act):
                    shared.scalar(act)

            @block.vector
            def _(dve):
                def step(i, k):
                    s = 2 * i + k
                    if live(s, gather.groups):
                        gather.open_group(dve, i, k)
                    m, b = s - 1, (k - 1) % 2
                    if not live(m, gather.groups):
                        return
                    if shared:
                        shared.vector(dve, m, b)
                    at = (dve, i + (k - 1) // 2, b)
                    gather.wait_rows(*at)
                    for n in range(TOP_K):
                        if n:
                            dve.wait_ge(gather.added[0], GTILES * (m + 1))
                        elif shared:
                            dve.wait_ge(shared.y_added, m + 1)
                        for t in range(GTILES):
                            gather.add(*at, t, n)
                    if not spec["last"]:
                        dve.wait_ge(gather.added[1], GTILES * (m + 1))
                        for t in range(GTILES):
                            gather.statistics(*at, t)
                skewed(dve, gather.groups, 1, step)


def ffn_phase(g, name, spec):
    with ExitStack() as ctx:
        E = spec["shared"] + EXPERTS
        f = {"pair": g.sbuf(f"{name}_weights", [P, TOP_K, TILES], ctx=ctx),
             "slots": g.sbuf(f"{name}_slots", [P, TOP_K, TILES], I32, ctx=ctx),
             "w_up": g.sbuf(f"{name}_w_up", [D, E, FFN], ctx=ctx),
             "w_down": g.sbuf(f"{name}_w_down", [P, E, FT, D], ctx=ctx)}
        parts, tiles = spec["parts"], slot_tiles(spec["parts"])
        f["tiles"], f["owner_stride"] = tiles, LAG + tiles + 2 * MOVED
        f["owner"] = g.sbuf(f"{name}_owner", [1, parts * f["owner_stride"]], I32, ctx=ctx)
        for n in ("slots_x", "slots_y"):
            f[n] = [g.nc.dram_tensor(f"{name}_{n}{part}", (tiles * P, D), F32, kind="Internal").ap()
                    for part in range(parts)]
        f["weight0"], f["weight1"] = f["pair"][:, 0, :], f["pair"][:, 1, :]
        if spec["b_up"]:
            f["b_up"] = g.sbuf(f"{name}_b_up", [P, EXPERTS, FFN], ctx=ctx)
            f["b_down"] = g.sbuf(f"{name}_b_down", [P, EXPERTS, D], ctx=ctx)
        f["loads"] = [(f[k][:], g.dram[spec[k]]) for k in ("w_up", "w_down")]
        if spec["b_up"]:
            f["loads"] += [(f[k][:], g.dram[spec[k]].partition_broadcast(P)) for k in ("b_up", "b_down")]
        f["loaded"] = g.sem(f"{name}_weights_loaded")
        for part in ("w_high", "w_low"):
            f[part] = g.sbuf(f"{name}_{part}", [D, EXPERTS, FFN], F32R, ctx=ctx)
        if spec["shared"]:
            f["xnT"] = g.sbuf(f"{name}_xnT", [D, TOKENS], ctx=ctx)
        route(g, name, spec, f)
        dispatch(g, f"{name}_d", spec, f)
        if parts == 1:
            run_experts(g, f"{name}_e", spec, f, 0)
        else:
            run_experts(g, f"{name}_e0", spec, f, 0, (Scatter, 1))
            run_experts(g, f"{name}_e1", spec, f, 1, (Gather, 0))
        combine(g, f"{name}_c", spec, f, parts - 1)


def ffn0(g):
    ffn_phase(g, "f0", dict(kind="sigmoid", plus_xn=True, parts=1, last=False, shared=2, gelu=ACT.Gelu, gate_w="f0_gate_w",
                            gate_b="L0_ffn_routing_bias", w_up="f0_up", w_down="f0_down", b_up=None))


def ffn1(g):
    ffn_phase(g, "f1", dict(kind="softmax", plus_xn=False, parts=2, last=True, shared=0, gelu=ACT.Gelu_apprx_tanh,
                            gate_w="L1_ffn_Wg", gate_b="L1_ffn_bg", w_up="f1_up", w_down="f1_down",
                            b_up="L1_ffn_b1", b_down="L1_ffn_b2"))


def xattn0(g):
    attention(g, "a0", False)


def xattn1(g):
    attention(g, "a1", True)


PHASES = (ssm_phase, xattn0, ffn0, retention_phase, xattn1, ffn1)


def launch_inputs(inputs):
    a = {k: np.ascontiguousarray(v) for k, v in inputs.items()}
    flip = lambda m: np.ascontiguousarray(m.T)
    out = {
        "x": a["x"].reshape(TOKENS, D),
        "ident": np.eye(P, dtype=np.float32),
        "time_row": np.tile(np.arange(SEQ, dtype=np.float32), (P, 1)),
        "ssm_b_re_im": flip(np.concatenate([a["L0_attn_B_real"], a["L0_attn_B_imag"]])),
        "ssm_b_im_re": flip(np.concatenate([a["L0_attn_B_imag"], a["L0_attn_B_real"]])),
        "ssm_c_re_im": np.concatenate([a["L0_attn_C_real"], a["L0_attn_C_imag"]], axis=1),
        "ssm_c_im_re": np.concatenate([a["L0_attn_C_imag"], a["L0_attn_C_real"]], axis=1),
        "ssm_w_out": flip(a["L0_attn_W_out"]),
        "L0_attn_log_Lam_real": a["L0_attn_log_Lam_real"].reshape(-1, 1),
        "L0_attn_Lam_imag": a["L0_attn_Lam_imag"].reshape(-1, 1),
        "L0_attn_log_dt": a["L0_attn_log_dt"].reshape(1, 1),
        "L0_attn_D": a["L0_attn_D"].reshape(-1, 1),
        "L0_attn_b_out": a["L0_attn_b_out"].reshape(1, -1),
        "ctxT": flip(a["ctx_1024"].reshape(TOKENS, D)).reshape(D, BATCH, SEQ),
        "ctx": a["ctx_1024"],
        "xa_wq": flip(a["L1_xattn_wq"]), "xa_wk": flip(a["L1_xattn_wk"]), "xa_wv": flip(a["L1_xattn_wv"]),
        "L1_xattn_bq": a["L1_xattn_bq"].reshape(-1, 1),
        "L1_xattn_bk": a["L1_xattn_bk"].reshape(-1, 1),
        "L1_xattn_bv": a["L1_xattn_bv"].reshape(1, -1),
        "rank": np.tile(np.arange(EXPERTS, 0, -1, dtype=np.float32), (P, 1)),
        "f0_gate_w": flip(a["L0_ffn_centroids"]),
        "L0_ffn_routing_bias": a["L0_ffn_routing_bias"].reshape(1, -1),
        "f0_up": np.concatenate([a["L0_ffn_Wfc_sh"], a["L0_ffn_Wfc_r"]]).transpose(2, 0, 1),
        "f0_down": np.concatenate([a["L0_ffn_Wproj_sh"], a["L0_ffn_Wproj_r"]])
        .reshape(-1, D, FT, P).transpose(3, 0, 2, 1),
        "L1_ffn_Wg": a["L1_ffn_Wg"], "L1_ffn_bg": a["L1_ffn_bg"].reshape(1, -1),
        "f1_up": a["L1_ffn_W1"].transpose(1, 0, 2),
        "f1_down": a["L1_ffn_W2"].reshape(EXPERTS, FT, P, D).transpose(2, 0, 1, 3),
        "L1_ffn_b1": a["L1_ffn_b1"], "L1_ffn_b2": a["L1_ffn_b2"],
        "before": np.triu(np.ones((P, P), np.float32), 1),
        "tile_starts": np.tile(P * np.arange(TILES, dtype=np.float32), (P, 1)),
        "tile_numbers": np.arange(slot_tiles(1), dtype=np.float32).reshape(1, -1),
        "ret_wqk": flip(np.concatenate([a["L1_attn_Wq"], a["L1_attn_Wk"]])),
        "ret_wv": flip(a["L1_attn_Wv"]).reshape(D, R_HEADS, R_VAL),
        "ret_wg": flip(a["L1_attn_Wg"]),
        "ret_wo": np.ascontiguousarray(a["L1_attn_Wo"].reshape(D, R_HEADS, R_VAL).transpose(2, 1, 0)),
        "ret_gn_w": flip(a["L1_attn_gn_weight"].reshape(R_HEADS, R_VAL)),
        "ret_gn_b": flip(a["L1_attn_gn_bias"].reshape(R_HEADS, R_VAL)),
    }
    out["ret_cos"], out["ret_sin"], out["ret_decay"] = retention_tables()
    return {k: np.ascontiguousarray(v) for k, v in out.items()}


def build(nc, dram, out):
    with ExitStack() as ctx:
        g = Program(nc, ctx, dram, out)
        for phase in PHASES:
            g.run(phase)


def kernel(**inputs):
    import concourse.bacc as bacc
    from concourse.bass_utils import run_bass_kernel_spmd

    nc = bacc.Bacc("TRN2", target_bir_lowering=False, num_devices=1)
    arrays = launch_inputs(inputs)
    dram = {k: nc.dram_tensor(f"in_{k}", a.shape, mybir.dt.from_np(a.dtype), kind="ExternalInput").ap()
            for k, a in arrays.items()}
    out = nc.dram_tensor("out", (TOKENS, D), F32, kind="ExternalOutput").ap()
    build(nc, dram, out)
    result = run_bass_kernel_spmd(nc, [{f"in_{k}": a for k, a in arrays.items()}], core_ids=[0])
    return result.results[0]["out"].reshape(BATCH, SEQ, D)
```
